# Optimizing a Trainium2 kernel written in Bass

```python
import numpy as np
import jax
import jax.numpy as jnp

def _softmax(x, axis=-1):
    return jax.nn.softmax(x, axis=axis)

def _gelu(x):
    return jax.nn.gelu(x, approximate=True)

def _silu(x):
    return jax.nn.silu(x)

def _sigmoid(x):
    return jax.nn.sigmoid(x)

def _layernorm(x, axis=-1, eps=1e-05):
    m = jnp.mean(x, axis=axis, keepdims=True)
    v = jnp.var(x, axis=axis, keepdims=True)
    return (x - m) / jnp.sqrt(v + eps)

def _scatter_add(tgt, idx, src, axis=0):
    return tgt.at[idx].add(src)

def _segment_sum(src, seg, n):
    return jax.ops.segment_sum(src, seg, n)
kernel_name = 'mk_gnn_resnorm_d4_gnn_r16_100e24'

def setup_inputs(seed: int=0):
    np.random.seed(seed)
    _w = jnp.asarray

    def _rec_inputs():
        import jax
        import jax.numpy as jnp
        _gk = jax.random.key(seed)
        x = -0.0009044 + 1 * jax.random.normal(jax.random.fold_in(_gk, 1), (6250, 160), jnp.float32)
        src = jax.random.randint(jax.random.fold_in(_gk, 2), (100000,), 0, 6250, jnp.int32)
        dst = jnp.minimum((6250 * jax.random.uniform(jax.random.fold_in(_gk, 3), (100000,)) ** 2.0).astype(jnp.int32), 99999)
        _o = jnp.argsort(dst, stable=True)
        src = src[_o]
        dst = dst[_o]
        edge_attr_16 = jax.random.uniform(jax.random.fold_in(_gk, 12), (100000, 16), jnp.float32, 0.0, 1)
        edge_attr_3 = 0.00262751 + 0.999568 * jax.random.normal(jax.random.fold_in(_gk, 13), (100000, 3), jnp.float32)
        edge_attr_4 = 0.000898722 + 1.00012 * jax.random.normal(jax.random.fold_in(_gk, 14), (100000, 4), jnp.float32)
        edge_attr_64 = jax.random.uniform(jax.random.fold_in(_gk, 15), (100000, 64), jnp.float32, 0.0, 1)
        edge_attr_8 = jax.random.uniform(jax.random.fold_in(_gk, 16), (100000, 8), jnp.float32, 0.0, 1)
        node_vec1 = jax.random.uniform(jax.random.fold_in(_gk, 18), (6250, 1), jnp.float32, 0.0, 1)
        return (x, src, dst, edge_attr_16, edge_attr_3, edge_attr_4, edge_attr_64, edge_attr_8, node_vec1)
    x, src, dst, edge_attr_16, edge_attr_3, edge_attr_4, edge_attr_64, edge_attr_8, node_vec1 = _rec_inputs()

    def _L0_gnn_setup():
        import jax, jax.numpy as jnp
        import numpy as np
        N, E = (625, 10000)
        C0, C1 = (64, 32)
        H, A = (8, 8)
        H0, H1 = (8, 4)
        M0, M1 = (128, 64)
        NG, RH = (64, 64)
        WN = C0 + C0 + C1 + C1 + C1
        DS, DV = (C0 + C1, C0 + 2 * C1)
        EPS = 1e-05
        SQ3 = np.float32(np.sqrt(3.0))
        SQ2 = np.float32(np.sqrt(2.0))

        def _split(x):
            return (x[:, :C0], x[:, C0:].reshape(x.shape[0], C1, 3))

        def _merge(s, v):
            return jnp.concatenate([s, v.reshape(v.shape[0], -1)], axis=1)

        def _eq_ln(x, w0, b0, w1):
            s, v = _split(x)
            s = s - s.mean(axis=1, keepdims=True)
            s = s * jax.lax.rsqrt(jnp.square(s).mean(axis=1, keepdims=True) + EPS) * w0 + b0
            v = v * jax.lax.rsqrt(jnp.square(v).mean(axis=(1, 2), keepdims=True) + EPS) * w1[None, :, None]
            return (s, v)

        def _eq_lin(s, v, ws, bs, wv):
            return (s @ ws + bs, jnp.einsum('nud,uk->nkd', v, wv))

        def _ln(x, g, b):
            xc = x - x.mean(-1, keepdims=True)
            return xc * jax.lax.rsqrt(jnp.square(xc).mean(-1, keepdims=True) + EPS) * g + b

        def _smooth_leaky(x, alpha=0.2):
            return 0.5 * (1 + alpha) * x + 0.5 * (1 - alpha) * x * (2.0 * jax.nn.sigmoid(x) - 1.0)

        def _forward(node_input, node_attr, edge_vec, edge_scalars, edge_src, edge_dst, ln1_w0, ln1_b0, ln1_w1, ln2_w0, ln2_b0, ln2_w1, msrc_ws, msrc_wv, mdst_ws, mdst_bs, mdst_wv, rw1, rb1, rg1, rbe1, rw2, rb2, rg2, rbe2, rw3, roff, lin_ws, lin_bs, lin_wv, alpha_dot, proj_ws, proj_bs, proj_wv, f1_ws, f1_bs, f1_wv, f2_ws, f2_bs, f2_wv):
            n = node_input.shape[0]
            s, v = _eq_ln(node_input, ln1_w0, ln1_b0, ln1_w1)
            src_s = s @ msrc_ws
            src_v = jnp.einsum('nud,uk->nkd', v, msrc_wv)
            dst_s = s @ mdst_ws + mdst_bs
            dst_v = jnp.einsum('nud,uk->nkd', v, mdst_wv)
            ms = src_s[edge_src] + dst_s[edge_dst]
            mv = src_v[edge_src] + dst_v[edge_dst]
            h = jax.nn.silu(_ln(edge_scalars @ rw1 + rb1, rg1, rbe1))
            h = jax.nn.silu(_ln(h @ rw2 + rb2, rg2, rbe2))
            w = h @ rw3 + roff
            rhat = edge_vec * jax.lax.rsqrt(jnp.sum(jnp.square(edge_vec), -1, keepdims=True) + 1e-12)
            Y1 = SQ3 * rhat
            w1, w2, w3, w4, w5 = jnp.split(w, [C0, 2 * C0, 2 * C0 + C1, 2 * C0 + 2 * C1], axis=1)
            o0a = w1 * ms
            o0b = w4 * (jnp.einsum('eud,ed->eu', mv, Y1) / SQ3)
            o1a = (w2 * ms)[:, :, None] * Y1[:, None, :]
            o1b = w3[:, :, None] * mv
            o1c = w5[:, :, None] * (jnp.cross(mv, Y1[:, None, :]) / SQ2)
            ds = jnp.concatenate([o0a, o0b], axis=1)
            dv = jnp.concatenate([o1a, o1b, o1c], axis=1)
            ls, lv = _eq_lin(ds, dv, lin_ws, lin_bs, lin_wv)
            e = ls.shape[0]
            alpha = ls[:, :H * A].reshape(e, H, A)
            vs = ls[:, H * A:].reshape(e, H, H0)
            vv = lv.reshape(e, H, H1, 3)
            a = jnp.einsum('ehk,hk->eh', _smooth_leaky(alpha), alpha_dot)
            amax = jax.lax.stop_gradient(jax.ops.segment_max(a, edge_dst, num_segments=n))
            a = jnp.exp(a - amax[edge_dst])
            a = a / (jax.ops.segment_sum(a, edge_dst, num_segments=n)[edge_dst] + 1e-12)
            ns = jax.ops.segment_sum(vs * a[..., None], edge_dst, num_segments=n).reshape(n, H * H0)
            nv = jax.ops.segment_sum(vv * a[..., None, None], edge_dst, num_segments=n).reshape(n, H * H1, 3)
            ps, pv = _eq_lin(ns, nv, proj_ws, proj_bs, proj_wv)
            x = node_input + _merge(ps, pv)
            s2, v2 = _eq_ln(x, ln2_w0, ln2_b0, ln2_w1)
            a0 = node_attr[:, :1]
            fs, fv = _eq_lin(s2, v2, f1_ws, f1_bs, f1_wv)
            fs = fs * a0
            fv = fv * a0[:, :, None]
            sc = jax.nn.silu(fs[:, :M0])
            fv = fv * jax.nn.sigmoid(fs[:, M0:])[:, :, None]
            os_, ov = _eq_lin(sc, fv, f2_ws, f2_bs, f2_wv)
            os_ = os_ * a0
            ov = ov * a0[:, :, None]
            return x + _merge(os_, ov)
        key = jax.random.key(seed)
        ks = iter(jax.random.split(key, 24))

        def nrm(shape, fan):
            return jax.random.normal(next(ks), shape, jnp.float32) / np.float32(np.sqrt(fan))
        inp = {}
        inp['node_input'] = jax.random.normal(next(ks), (N, C0 + 3 * C1), jnp.float32)
        inp['node_attr'] = jnp.ones((N, 1), jnp.float32)
        inp['edge_vec'] = jax.random.normal(next(ks), (E, 3), jnp.float32)
        inp['edge_scalars'] = jax.random.uniform(next(ks), (E, NG), dtype=jnp.float32)
        inp['edge_src'] = jax.random.randint(next(ks), (E,), 0, N)
        inp['edge_dst'] = jax.random.randint(next(ks), (E,), 0, N)
        inp['ln1_w0'] = jnp.ones((C0,), jnp.float32)
        inp['ln1_b0'] = jnp.zeros((C0,), jnp.float32)
        inp['ln1_w1'] = jnp.ones((C1,), jnp.float32)
        inp['ln2_w0'] = jnp.ones((C0,), jnp.float32)
        inp['ln2_b0'] = jnp.zeros((C0,), jnp.float32)
        inp['ln2_w1'] = jnp.ones((C1,), jnp.float32)
        inp['msrc_ws'] = nrm((C0, C0), C0)
        inp['msrc_wv'] = nrm((C1, C1), C1)
        inp['mdst_ws'] = nrm((C0, C0), C0)
        inp['mdst_bs'] = jnp.zeros((C0,), jnp.float32)
        inp['mdst_wv'] = nrm((C1, C1), C1)
        inp['rw1'] = nrm((NG, RH), NG)
        inp['rb1'] = jnp.zeros((RH,), jnp.float32)
        inp['rg1'] = jnp.ones((RH,), jnp.float32)
        inp['rbe1'] = jnp.zeros((RH,), jnp.float32)
        inp['rw2'] = nrm((RH, RH), RH)
        inp['rb2'] = jnp.zeros((RH,), jnp.float32)
        inp['rg2'] = jnp.ones((RH,), jnp.float32)
        inp['rbe2'] = jnp.zeros((RH,), jnp.float32)
        inp['rw3'] = nrm((RH, WN), RH)
        inp['roff'] = 0.1 * jax.random.normal(next(ks), (WN,), jnp.float32)
        inp['lin_ws'] = nrm((DS, H * A + H * H0), DS)
        inp['lin_bs'] = jnp.zeros((H * A + H * H0,), jnp.float32)
        inp['lin_wv'] = nrm((DV, H * H1), DV)
        inp['alpha_dot'] = nrm((H, A), A)
        inp['proj_ws'] = nrm((H * H0, C0), H * H0)
        inp['proj_bs'] = jnp.zeros((C0,), jnp.float32)
        inp['proj_wv'] = nrm((H * H1, C1), H * H1)
        inp['f1_ws'] = nrm((C0, M0 + M1), C0)
        inp['f1_bs'] = jnp.zeros((M0 + M1,), jnp.float32)
        inp['f1_wv'] = nrm((C1, M1), C1)
        inp['f2_ws'] = nrm((M0, C0), M0)
        inp['f2_bs'] = jnp.zeros((C0,), jnp.float32)
        inp['f2_wv'] = nrm((M1, C1), M1)
        return inp
    _L0_gnn_all = _L0_gnn_setup()
    _L0_gnn_in = {k: v for k, v in _L0_gnn_all.items() if k in ('ln1_w0', 'ln1_b0', 'ln1_w1', 'ln2_w0', 'ln2_b0', 'ln2_w1', 'msrc_ws', 'msrc_wv', 'mdst_ws', 'mdst_bs', 'mdst_wv', 'rw1', 'rb1', 'rg1', 'rbe1', 'rw2', 'rb2', 'rg2', 'rbe2', 'rw3', 'roff', 'lin_ws', 'lin_bs', 'lin_wv', 'alpha_dot', 'proj_ws', 'proj_bs', 'proj_wv', 'f1_ws', 'f1_bs', 'f1_wv', 'f2_ws', 'f2_bs', 'f2_wv')}
    del _L0_gnn_all

    def _L1_gnn_setup():
        import jax, jax.numpy as jnp
        import numpy as np
        N_NODES = 625
        N_EDGES = 20000
        MUL0, MUL1 = (64, 32)
        EDGE_DIM = 64
        W_NUMEL = 224
        DENOM = 32.0
        SQRT3 = 3.0 ** 0.5
        INV_SQRT3 = 1.0 / SQRT3
        INV_SQRT2 = 2.0 ** (-0.5)

        def _forward(node_feature, edge_attr, edge_feature, W_skip0, W_skip1, W_nl0, W_nl1, W_fc1, W_fc2, W_out_s, W_out_v, edge_index):
            N = node_feature.shape[0]
            E = edge_attr.shape[0]
            s = node_feature[:, :MUL0]
            v = node_feature[:, MUL0:].reshape(N, MUL1, 3)
            skip_s = s @ W_skip0
            skip_v = jnp.einsum('nmi,mk->nki', v, W_skip1)
            s = s @ W_nl0
            v = jnp.einsum('nmi,mk->nki', v, W_nl1)
            rhat = edge_attr / jnp.linalg.norm(edge_attr, axis=-1, keepdims=True)
            sh1 = SQRT3 * rhat
            w = jax.nn.relu(edge_feature @ W_fc1) @ W_fc2
            w0, w1, w2, w3, w4 = jnp.split(w, [64, 128, 160, 192], axis=-1)
            src, dst = (edge_index[0], edge_index[1])
            xs = s[dst]
            xv = v[dst]
            out0a = w0 * xs
            out0b = w3 * (jnp.einsum('emi,ei->em', xv, sh1) * INV_SQRT3)
            out1a = (w1 * xs)[:, :, None] * sh1[:, None, :]
            out1b = w2[:, :, None] * xv
            out1c = w4[:, :, None] * (jnp.cross(xv, sh1[:, None, :]) * INV_SQRT2)
            tp = jnp.concatenate([out0a, out0b, out1a.reshape(E, -1), out1b.reshape(E, -1), out1c.reshape(E, -1)], axis=-1)
            agg = jax.ops.segment_sum(tp, src, num_segments=N) / DENOM
            agg_s = agg[:, :96]
            agg_v = agg[:, 96:].reshape(N, 128, 3)
            out_s = agg_s @ W_out_s + skip_s
            out_v = jnp.einsum('nmi,mk->nki', agg_v, W_out_v) + skip_v
            fs = jax.nn.silu(out_s[:, :MUL0])
            gate = jax.nn.sigmoid(out_s[:, MUL0:MUL0 + 32])
            gv = gate[:, :, None] * out_v
            return jnp.concatenate([fs, gv.reshape(N, -1)], axis=-1)
        key = jax.random.key(seed)
        ks = jax.random.split(key, 12)

        def lin(k, fi, fo):
            return jax.random.normal(k, (fi, fo), jnp.float32) / np.float32(np.sqrt(fi))
        return {'node_feature': jax.random.normal(ks[0], (N_NODES, MUL0 + 3 * MUL1), jnp.float32), 'edge_attr': jax.random.normal(ks[1], (N_EDGES, 3), jnp.float32), 'edge_feature': jax.random.normal(ks[2], (N_EDGES, EDGE_DIM), jnp.float32), 'W_skip0': lin(ks[3], MUL0, 96), 'W_skip1': lin(ks[4], MUL1, 32), 'W_nl0': lin(ks[5], MUL0, MUL0), 'W_nl1': lin(ks[6], MUL1, MUL1), 'W_fc1': lin(ks[7], EDGE_DIM, 64), 'W_fc2': lin(ks[8], 64, W_NUMEL), 'W_out_s': lin(ks[9], 96, 96), 'W_out_v': lin(ks[10], 128, 32), 'edge_index': jax.random.randint(ks[11], (2, N_EDGES), 0, N_NODES)}
    _L1_gnn_all = _L1_gnn_setup()
    _L1_gnn_in = {k: v for k, v in _L1_gnn_all.items() if k in ('W_skip0', 'W_skip1', 'W_nl0', 'W_nl1', 'W_fc1', 'W_fc2', 'W_out_s', 'W_out_v')}
    del _L1_gnn_all

    def _L2_gnn_setup():
        import jax, jax.numpy as jnp
        import numpy as np
        N, E = (1250, 20000)
        CS, CV = (64, 32)
        AS_, AV, H = (16, 8, 4)
        NB = 16
        SQRT3 = 1.7320508075688772
        SQRT2 = 1.4142135623730951
        EPS = 1e-05

        def _cg_tp(s, v, y0, y1, w_ss, w_sv, w_vs, w_vv0, w_vv1):
            out_s = jnp.concatenate([w_ss * s * y0[:, None], w_vv0 * (jnp.einsum('eci,ei->ec', v, y1) / SQRT3)], axis=-1)
            out_v = jnp.concatenate([(w_sv * s)[:, :, None] * y1[:, None, :], (w_vs * jnp.ones_like(v[..., 0]))[..., None] * v * y0[:, None, None], (w_vv1 * jnp.ones_like(v[..., 0]))[..., None] * (jnp.cross(v, y1[:, None, :]) / SQRT2)], axis=1)
            return (out_s, out_v)

        def _equiv_layernorm(s, v, gamma_s, beta_s, gamma_v):
            mu = jnp.mean(s, axis=-1, keepdims=True)
            var = jnp.var(s, axis=-1, keepdims=True)
            s_n = (s - mu) * jax.lax.rsqrt(var + EPS) * gamma_s + beta_s
            rms = jnp.sqrt(jnp.mean(jnp.sum(v * v, axis=-1), axis=-1, keepdims=True) + EPS)
            v_n = v / rms[..., None] * gamma_v[None, :, None]
            return (s_n, v_n)
        key = jax.random.key(seed)
        ks = jax.random.split(key, 26)

        def rn(k, shape, fan):
            return jax.random.normal(k, shape, jnp.float32) / np.sqrt(fan)
        D1S, D1V = (CS + CV, CS + 2 * CV)
        WN = 2 * CS + 3 * CV
        inp = {'node': jax.random.normal(ks[0], (N, CS + 3 * CV), jnp.float32), 'edge_index': jax.random.randint(ks[1], (2, E), 0, N, jnp.int64 if jax.config.jax_enable_x64 else jnp.int32), 'rbf': jax.random.uniform(ks[2], (E, NB), jnp.float32), 'rsh': jax.random.normal(ks[3], (E, 4), jnp.float32), 'gamma_s': jnp.ones((CS,), jnp.float32), 'beta_s': jnp.zeros((CS,), jnp.float32), 'gamma_v': jnp.ones((CV,), jnp.float32), 'Ws_src': rn(ks[4], (CS, CS), CS), 'Wv_src': rn(ks[5], (CV, CV), CV), 'Ws_dst': rn(ks[6], (CS, CS), CS), 'Wv_dst': rn(ks[7], (CV, CV), CV), 'W_rbf': rn(ks[8], (NB, WN), NB), 'W_alpha': rn(ks[9], (D1S, H * AS_), D1S), 'alpha_dot': rn(ks[10], (1, H, AS_), AS_), 'Ws_val': rn(ks[11], (D1S, CS), D1S), 'Wv_val': rn(ks[12], (D1V, CV), D1V), 'Wg': rn(ks[13], (CS, CV), CS), 'w2_ss': rn(ks[14], (CS,), 1), 'w2_sv': rn(ks[15], (CS,), 1), 'w2_vs': rn(ks[16], (CV,), 1), 'w2_vv0': rn(ks[17], (CV,), 1), 'w2_vv1': rn(ks[18], (CV,), 1), 'Ws_vlin': rn(ks[19], (D1S, H * AS_), D1S), 'Wv_vlin': rn(ks[20], (D1V, H * AV), D1V), 'Wps': rn(ks[21], (H * AS_, CS), H * AS_), 'Wpv': rn(ks[22], (H * AV, CV), H * AV)}
        return inp
    _L2_gnn_all = _L2_gnn_setup()
    _L2_gnn_in = {k: v for k, v in _L2_gnn_all.items() if k in ('gamma_s', 'beta_s', 'gamma_v', 'Ws_src', 'Wv_src', 'Ws_dst', 'Wv_dst', 'W_rbf', 'W_alpha', 'alpha_dot', 'Ws_val', 'Wv_val', 'Wg', 'w2_ss', 'w2_sv', 'w2_vs', 'w2_vv0', 'w2_vv1', 'Ws_vlin', 'Wv_vlin', 'Wps', 'Wpv')}
    del _L2_gnn_all

    def _L3_gnn_setup():
        import jax, jax.numpy as jnp
        import numpy as np
        N = 2500
        E = 25000
        MUL0, MUL1 = (64, 32)
        RAD, HID = (8, 64)
        WNUM = 192
        NUM_NEIGHBORS = 10.0
        INV3 = 1.0 / np.sqrt(3.0)

        def _lin(s, v, Ws, Wv, attr):
            out_s = s @ Ws * attr * (1.0 / np.sqrt(Ws.shape[0]))
            out_v = jnp.einsum('nud,uv->nvd', v, Wv) * attr[..., None] * (1.0 / np.sqrt(Wv.shape[0]))
            return (out_s, out_v)
        key = jax.random.key(seed)
        ks = jax.random.split(key, 16)
        return {'node_input': jax.random.normal(ks[0], (N, MUL0 + 3 * MUL1), jnp.float32), 'node_attr': jnp.ones((N, 1), jnp.float32), 'edge_attr': jax.random.normal(ks[1], (E, 4), jnp.float32), 'edge_scalars': jax.random.uniform(ks[2], (E, RAD), jnp.float32), 'W_sc_s': jax.random.normal(ks[3], (MUL0, MUL0), jnp.float32), 'W_sc_v': jax.random.normal(ks[4], (MUL1, MUL1), jnp.float32), 'W1_s': jax.random.normal(ks[5], (MUL0, MUL0), jnp.float32), 'W1_v': jax.random.normal(ks[6], (MUL1, MUL1), jnp.float32), 'W2_s': jax.random.normal(ks[7], (MUL0 + MUL1, MUL0), jnp.float32), 'W2_v': jax.random.normal(ks[8], (MUL0 + MUL1, MUL1), jnp.float32), 'W3': jax.random.normal(ks[9], (MUL0 + MUL1, 1), jnp.float32), 'fcW1': jax.random.normal(ks[10], (RAD, HID), jnp.float32), 'fcW2': jax.random.normal(ks[11], (HID, WNUM), jnp.float32), 'edge_src': jax.random.randint(ks[12], (E,), 0, N, jnp.int32), 'edge_dst': jax.random.randint(ks[13], (E,), 0, N, jnp.int32)}
    _L3_gnn_all = _L3_gnn_setup()
    _L3_gnn_in = {k: v for k, v in _L3_gnn_all.items() if k in ('W_sc_s', 'W_sc_v', 'W1_s', 'W1_v', 'W2_s', 'W2_v', 'W3', 'fcW1', 'fcW2')}
    del _L3_gnn_all
    return {'x': x, 'src': src, 'dst': dst, 'edge_attr_16': edge_attr_16, 'edge_attr_3': edge_attr_3, 'edge_attr_4': edge_attr_4, 'edge_attr_64': edge_attr_64, 'edge_attr_8': edge_attr_8, 'node_vec1': node_vec1, 'L0_gnn_ln1_w0': _L0_gnn_in['ln1_w0'], 'L0_gnn_ln1_b0': _L0_gnn_in['ln1_b0'], 'L0_gnn_ln1_w1': _L0_gnn_in['ln1_w1'], 'L0_gnn_ln2_w0': _L0_gnn_in['ln2_w0'], 'L0_gnn_ln2_b0': _L0_gnn_in['ln2_b0'], 'L0_gnn_ln2_w1': _L0_gnn_in['ln2_w1'], 'L0_gnn_msrc_ws': _L0_gnn_in['msrc_ws'], 'L0_gnn_msrc_wv': _L0_gnn_in['msrc_wv'], 'L0_gnn_mdst_ws': _L0_gnn_in['mdst_ws'], 'L0_gnn_mdst_bs': _L0_gnn_in['mdst_bs'], 'L0_gnn_mdst_wv': _L0_gnn_in['mdst_wv'], 'L0_gnn_rw1': _L0_gnn_in['rw1'], 'L0_gnn_rb1': _L0_gnn_in['rb1'], 'L0_gnn_rg1': _L0_gnn_in['rg1'], 'L0_gnn_rbe1': _L0_gnn_in['rbe1'], 'L0_gnn_rw2': _L0_gnn_in['rw2'], 'L0_gnn_rb2': _L0_gnn_in['rb2'], 'L0_gnn_rg2': _L0_gnn_in['rg2'], 'L0_gnn_rbe2': _L0_gnn_in['rbe2'], 'L0_gnn_rw3': _L0_gnn_in['rw3'], 'L0_gnn_roff': _L0_gnn_in['roff'], 'L0_gnn_lin_ws': _L0_gnn_in['lin_ws'], 'L0_gnn_lin_bs': _L0_gnn_in['lin_bs'], 'L0_gnn_lin_wv': _L0_gnn_in['lin_wv'], 'L0_gnn_alpha_dot': _L0_gnn_in['alpha_dot'], 'L0_gnn_proj_ws': _L0_gnn_in['proj_ws'], 'L0_gnn_proj_bs': _L0_gnn_in['proj_bs'], 'L0_gnn_proj_wv': _L0_gnn_in['proj_wv'], 'L0_gnn_f1_ws': _L0_gnn_in['f1_ws'], 'L0_gnn_f1_bs': _L0_gnn_in['f1_bs'], 'L0_gnn_f1_wv': _L0_gnn_in['f1_wv'], 'L0_gnn_f2_ws': _L0_gnn_in['f2_ws'], 'L0_gnn_f2_bs': _L0_gnn_in['f2_bs'], 'L0_gnn_f2_wv': _L0_gnn_in['f2_wv'], 'L1_gnn_W_skip0': _L1_gnn_in['W_skip0'], 'L1_gnn_W_skip1': _L1_gnn_in['W_skip1'], 'L1_gnn_W_nl0': _L1_gnn_in['W_nl0'], 'L1_gnn_W_nl1': _L1_gnn_in['W_nl1'], 'L1_gnn_W_fc1': _L1_gnn_in['W_fc1'], 'L1_gnn_W_fc2': _L1_gnn_in['W_fc2'], 'L1_gnn_W_out_s': _L1_gnn_in['W_out_s'], 'L1_gnn_W_out_v': _L1_gnn_in['W_out_v'], 'L2_gnn_gamma_s': _L2_gnn_in['gamma_s'], 'L2_gnn_beta_s': _L2_gnn_in['beta_s'], 'L2_gnn_gamma_v': _L2_gnn_in['gamma_v'], 'L2_gnn_Ws_src': _L2_gnn_in['Ws_src'], 'L2_gnn_Wv_src': _L2_gnn_in['Wv_src'], 'L2_gnn_Ws_dst': _L2_gnn_in['Ws_dst'], 'L2_gnn_Wv_dst': _L2_gnn_in['Wv_dst'], 'L2_gnn_W_rbf': _L2_gnn_in['W_rbf'], 'L2_gnn_W_alpha': _L2_gnn_in['W_alpha'], 'L2_gnn_alpha_dot': _L2_gnn_in['alpha_dot'], 'L2_gnn_Ws_val': _L2_gnn_in['Ws_val'], 'L2_gnn_Wv_val': _L2_gnn_in['Wv_val'], 'L2_gnn_Wg': _L2_gnn_in['Wg'], 'L2_gnn_w2_ss': _L2_gnn_in['w2_ss'], 'L2_gnn_w2_sv': _L2_gnn_in['w2_sv'], 'L2_gnn_w2_vs': _L2_gnn_in['w2_vs'], 'L2_gnn_w2_vv0': _L2_gnn_in['w2_vv0'], 'L2_gnn_w2_vv1': _L2_gnn_in['w2_vv1'], 'L2_gnn_Ws_vlin': _L2_gnn_in['Ws_vlin'], 'L2_gnn_Wv_vlin': _L2_gnn_in['Wv_vlin'], 'L2_gnn_Wps': _L2_gnn_in['Wps'], 'L2_gnn_Wpv': _L2_gnn_in['Wpv'], 'L3_gnn_W_sc_s': _L3_gnn_in['W_sc_s'], 'L3_gnn_W_sc_v': _L3_gnn_in['W_sc_v'], 'L3_gnn_W1_s': _L3_gnn_in['W1_s'], 'L3_gnn_W1_v': _L3_gnn_in['W1_v'], 'L3_gnn_W2_s': _L3_gnn_in['W2_s'], 'L3_gnn_W2_v': _L3_gnn_in['W2_v'], 'L3_gnn_W3': _L3_gnn_in['W3'], 'L3_gnn_fcW1': _L3_gnn_in['fcW1'], 'L3_gnn_fcW2': _L3_gnn_in['fcW2']}

def reference(x, src, dst, edge_attr_16, edge_attr_3, edge_attr_4, edge_attr_64, edge_attr_8, node_vec1, L0_gnn_ln1_w0, L0_gnn_ln1_b0, L0_gnn_ln1_w1, L0_gnn_ln2_w0, L0_gnn_ln2_b0, L0_gnn_ln2_w1, L0_gnn_msrc_ws, L0_gnn_msrc_wv, L0_gnn_mdst_ws, L0_gnn_mdst_bs, L0_gnn_mdst_wv, L0_gnn_rw1, L0_gnn_rb1, L0_gnn_rg1, L0_gnn_rbe1, L0_gnn_rw2, L0_gnn_rb2, L0_gnn_rg2, L0_gnn_rbe2, L0_gnn_rw3, L0_gnn_roff, L0_gnn_lin_ws, L0_gnn_lin_bs, L0_gnn_lin_wv, L0_gnn_alpha_dot, L0_gnn_proj_ws, L0_gnn_proj_bs, L0_gnn_proj_wv, L0_gnn_f1_ws, L0_gnn_f1_bs, L0_gnn_f1_wv, L0_gnn_f2_ws, L0_gnn_f2_bs, L0_gnn_f2_wv, L1_gnn_W_skip0, L1_gnn_W_skip1, L1_gnn_W_nl0, L1_gnn_W_nl1, L1_gnn_W_fc1, L1_gnn_W_fc2, L1_gnn_W_out_s, L1_gnn_W_out_v, L2_gnn_gamma_s, L2_gnn_beta_s, L2_gnn_gamma_v, L2_gnn_Ws_src, L2_gnn_Wv_src, L2_gnn_Ws_dst, L2_gnn_Wv_dst, L2_gnn_W_rbf, L2_gnn_W_alpha, L2_gnn_alpha_dot, L2_gnn_Ws_val, L2_gnn_Wv_val, L2_gnn_Wg, L2_gnn_w2_ss, L2_gnn_w2_sv, L2_gnn_w2_vs, L2_gnn_w2_vv0, L2_gnn_w2_vv1, L2_gnn_Ws_vlin, L2_gnn_Wv_vlin, L2_gnn_Wps, L2_gnn_Wpv, L3_gnn_W_sc_s, L3_gnn_W_sc_v, L3_gnn_W1_s, L3_gnn_W1_v, L3_gnn_W2_s, L3_gnn_W2_v, L3_gnn_W3, L3_gnn_fcW1, L3_gnn_fcW2):
    import jax
    import jax.numpy as jnp

    def _L0_gnn_ref(node_input, node_attr, edge_vec, edge_scalars, edge_src, edge_dst, ln1_w0, ln1_b0, ln1_w1, ln2_w0, ln2_b0, ln2_w1, msrc_ws, msrc_wv, mdst_ws, mdst_bs, mdst_wv, rw1, rb1, rg1, rbe1, rw2, rb2, rg2, rbe2, rw3, roff, lin_ws, lin_bs, lin_wv, alpha_dot, proj_ws, proj_bs, proj_wv, f1_ws, f1_bs, f1_wv, f2_ws, f2_bs, f2_wv):
        import jax, jax.numpy as jnp
        import numpy as np
        N, E = (625, 10000)
        C0, C1 = (64, 32)
        H, A = (8, 8)
        H0, H1 = (8, 4)
        M0, M1 = (128, 64)
        NG, RH = (64, 64)
        WN = C0 + C0 + C1 + C1 + C1
        DS, DV = (C0 + C1, C0 + 2 * C1)
        EPS = 1e-05
        SQ3 = np.float32(np.sqrt(3.0))
        SQ2 = np.float32(np.sqrt(2.0))

        def _split(x):
            return (x[:, :C0], x[:, C0:].reshape(x.shape[0], C1, 3))

        def _merge(s, v):
            return jnp.concatenate([s, v.reshape(v.shape[0], -1)], axis=1)

        def _eq_ln(x, w0, b0, w1):
            s, v = _split(x)
            s = s - s.mean(axis=1, keepdims=True)
            s = s * jax.lax.rsqrt(jnp.square(s).mean(axis=1, keepdims=True) + EPS) * w0 + b0
            v = v * jax.lax.rsqrt(jnp.square(v).mean(axis=(1, 2), keepdims=True) + EPS) * w1[None, :, None]
            return (s, v)

        def _eq_lin(s, v, ws, bs, wv):
            return (s @ ws + bs, jnp.einsum('nud,uk->nkd', v, wv))

        def _ln(x, g, b):
            xc = x - x.mean(-1, keepdims=True)
            return xc * jax.lax.rsqrt(jnp.square(xc).mean(-1, keepdims=True) + EPS) * g + b

        def _smooth_leaky(x, alpha=0.2):
            return 0.5 * (1 + alpha) * x + 0.5 * (1 - alpha) * x * (2.0 * jax.nn.sigmoid(x) - 1.0)

        def _forward(node_input, node_attr, edge_vec, edge_scalars, edge_src, edge_dst, ln1_w0, ln1_b0, ln1_w1, ln2_w0, ln2_b0, ln2_w1, msrc_ws, msrc_wv, mdst_ws, mdst_bs, mdst_wv, rw1, rb1, rg1, rbe1, rw2, rb2, rg2, rbe2, rw3, roff, lin_ws, lin_bs, lin_wv, alpha_dot, proj_ws, proj_bs, proj_wv, f1_ws, f1_bs, f1_wv, f2_ws, f2_bs, f2_wv):
            n = node_input.shape[0]
            s, v = _eq_ln(node_input, ln1_w0, ln1_b0, ln1_w1)
            src_s = s @ msrc_ws
            src_v = jnp.einsum('nud,uk->nkd', v, msrc_wv)
            dst_s = s @ mdst_ws + mdst_bs
            dst_v = jnp.einsum('nud,uk->nkd', v, mdst_wv)
            ms = src_s[edge_src] + dst_s[edge_dst]
            mv = src_v[edge_src] + dst_v[edge_dst]
            h = jax.nn.silu(_ln(edge_scalars @ rw1 + rb1, rg1, rbe1))
            h = jax.nn.silu(_ln(h @ rw2 + rb2, rg2, rbe2))
            w = h @ rw3 + roff
            rhat = edge_vec * jax.lax.rsqrt(jnp.sum(jnp.square(edge_vec), -1, keepdims=True) + 1e-12)
            Y1 = SQ3 * rhat
            w1, w2, w3, w4, w5 = jnp.split(w, [C0, 2 * C0, 2 * C0 + C1, 2 * C0 + 2 * C1], axis=1)
            o0a = w1 * ms
            o0b = w4 * (jnp.einsum('eud,ed->eu', mv, Y1) / SQ3)
            o1a = (w2 * ms)[:, :, None] * Y1[:, None, :]
            o1b = w3[:, :, None] * mv
            o1c = w5[:, :, None] * (jnp.cross(mv, Y1[:, None, :]) / SQ2)
            ds = jnp.concatenate([o0a, o0b], axis=1)
            dv = jnp.concatenate([o1a, o1b, o1c], axis=1)
            ls, lv = _eq_lin(ds, dv, lin_ws, lin_bs, lin_wv)
            e = ls.shape[0]
            alpha = ls[:, :H * A].reshape(e, H, A)
            vs = ls[:, H * A:].reshape(e, H, H0)
            vv = lv.reshape(e, H, H1, 3)
            a = jnp.einsum('ehk,hk->eh', _smooth_leaky(alpha), alpha_dot)
            amax = jax.lax.stop_gradient(jax.ops.segment_max(a, edge_dst, num_segments=n))
            a = jnp.exp(a - amax[edge_dst])
            a = a / (jax.ops.segment_sum(a, edge_dst, num_segments=n)[edge_dst] + 1e-12)
            ns = jax.ops.segment_sum(vs * a[..., None], edge_dst, num_segments=n).reshape(n, H * H0)
            nv = jax.ops.segment_sum(vv * a[..., None, None], edge_dst, num_segments=n).reshape(n, H * H1, 3)
            ps, pv = _eq_lin(ns, nv, proj_ws, proj_bs, proj_wv)
            x = node_input + _merge(ps, pv)
            s2, v2 = _eq_ln(x, ln2_w0, ln2_b0, ln2_w1)
            a0 = node_attr[:, :1]
            fs, fv = _eq_lin(s2, v2, f1_ws, f1_bs, f1_wv)
            fs = fs * a0
            fv = fv * a0[:, :, None]
            sc = jax.nn.silu(fs[:, :M0])
            fv = fv * jax.nn.sigmoid(fs[:, M0:])[:, :, None]
            os_, ov = _eq_lin(sc, fv, f2_ws, f2_bs, f2_wv)
            os_ = os_ * a0
            ov = ov * a0[:, :, None]
            return x + _merge(os_, ov)
        return _forward(node_input, node_attr, edge_vec, edge_scalars, edge_src, edge_dst, ln1_w0, ln1_b0, ln1_w1, ln2_w0, ln2_b0, ln2_w1, msrc_ws, msrc_wv, mdst_ws, mdst_bs, mdst_wv, rw1, rb1, rg1, rbe1, rw2, rb2, rg2, rbe2, rw3, roff, lin_ws, lin_bs, lin_wv, alpha_dot, proj_ws, proj_bs, proj_wv, f1_ws, f1_bs, f1_wv, f2_ws, f2_bs, f2_wv)

    def _L1_gnn_ref(node_feature, edge_attr, edge_feature, W_skip0, W_skip1, W_nl0, W_nl1, W_fc1, W_fc2, W_out_s, W_out_v, edge_index):
        import jax, jax.numpy as jnp
        import numpy as np
        N_NODES = 625
        N_EDGES = 20000
        MUL0, MUL1 = (64, 32)
        EDGE_DIM = 64
        W_NUMEL = 224
        DENOM = 32.0
        SQRT3 = 3.0 ** 0.5
        INV_SQRT3 = 1.0 / SQRT3
        INV_SQRT2 = 2.0 ** (-0.5)

        def _forward(node_feature, edge_attr, edge_feature, W_skip0, W_skip1, W_nl0, W_nl1, W_fc1, W_fc2, W_out_s, W_out_v, edge_index):
            N = node_feature.shape[0]
            E = edge_attr.shape[0]
            s = node_feature[:, :MUL0]
            v = node_feature[:, MUL0:].reshape(N, MUL1, 3)
            skip_s = s @ W_skip0
            skip_v = jnp.einsum('nmi,mk->nki', v, W_skip1)
            s = s @ W_nl0
            v = jnp.einsum('nmi,mk->nki', v, W_nl1)
            rhat = edge_attr / jnp.linalg.norm(edge_attr, axis=-1, keepdims=True)
            sh1 = SQRT3 * rhat
            w = jax.nn.relu(edge_feature @ W_fc1) @ W_fc2
            w0, w1, w2, w3, w4 = jnp.split(w, [64, 128, 160, 192], axis=-1)
            src, dst = (edge_index[0], edge_index[1])
            xs = s[dst]
            xv = v[dst]
            out0a = w0 * xs
            out0b = w3 * (jnp.einsum('emi,ei->em', xv, sh1) * INV_SQRT3)
            out1a = (w1 * xs)[:, :, None] * sh1[:, None, :]
            out1b = w2[:, :, None] * xv
            out1c = w4[:, :, None] * (jnp.cross(xv, sh1[:, None, :]) * INV_SQRT2)
            tp = jnp.concatenate([out0a, out0b, out1a.reshape(E, -1), out1b.reshape(E, -1), out1c.reshape(E, -1)], axis=-1)
            agg = jax.ops.segment_sum(tp, src, num_segments=N) / DENOM
            agg_s = agg[:, :96]
            agg_v = agg[:, 96:].reshape(N, 128, 3)
            out_s = agg_s @ W_out_s + skip_s
            out_v = jnp.einsum('nmi,mk->nki', agg_v, W_out_v) + skip_v
            fs = jax.nn.silu(out_s[:, :MUL0])
            gate = jax.nn.sigmoid(out_s[:, MUL0:MUL0 + 32])
            gv = gate[:, :, None] * out_v
            return jnp.concatenate([fs, gv.reshape(N, -1)], axis=-1)
        return _forward(node_feature, edge_attr, edge_feature, W_skip0, W_skip1, W_nl0, W_nl1, W_fc1, W_fc2, W_out_s, W_out_v, edge_index)

    def _L2_gnn_ref(node, rbf, rsh, gamma_s, beta_s, gamma_v, Ws_src, Wv_src, Ws_dst, Wv_dst, W_rbf, W_alpha, alpha_dot, Ws_val, Wv_val, Wg, w2_ss, w2_sv, w2_vs, w2_vv0, w2_vv1, Ws_vlin, Wv_vlin, Wps, Wpv, edge_index):
        import jax, jax.numpy as jnp
        import numpy as np
        N, E = (1250, 20000)
        CS, CV = (64, 32)
        AS_, AV, H = (16, 8, 4)
        NB = 16
        SQRT3 = 1.7320508075688772
        SQRT2 = 1.4142135623730951
        EPS = 1e-05

        def _cg_tp(s, v, y0, y1, w_ss, w_sv, w_vs, w_vv0, w_vv1):
            out_s = jnp.concatenate([w_ss * s * y0[:, None], w_vv0 * (jnp.einsum('eci,ei->ec', v, y1) / SQRT3)], axis=-1)
            out_v = jnp.concatenate([(w_sv * s)[:, :, None] * y1[:, None, :], (w_vs * jnp.ones_like(v[..., 0]))[..., None] * v * y0[:, None, None], (w_vv1 * jnp.ones_like(v[..., 0]))[..., None] * (jnp.cross(v, y1[:, None, :]) / SQRT2)], axis=1)
            return (out_s, out_v)

        def _equiv_layernorm(s, v, gamma_s, beta_s, gamma_v):
            mu = jnp.mean(s, axis=-1, keepdims=True)
            var = jnp.var(s, axis=-1, keepdims=True)
            s_n = (s - mu) * jax.lax.rsqrt(var + EPS) * gamma_s + beta_s
            rms = jnp.sqrt(jnp.mean(jnp.sum(v * v, axis=-1), axis=-1, keepdims=True) + EPS)
            v_n = v / rms[..., None] * gamma_v[None, :, None]
            return (s_n, v_n)
        n = node.shape[0]
        e = rsh.shape[0]
        s = node[:, :CS]
        v = node[:, CS:].reshape(n, CV, 3)
        s_n, v_n = _equiv_layernorm(s, v, gamma_s, beta_s, gamma_v)
        src, dst = (edge_index[0], edge_index[1])
        msg_s = (s_n @ Ws_src)[src] + (s_n @ Ws_dst)[dst]
        msg_v = jnp.einsum('ncx,cd->ndx', v_n, Wv_src)[src] + jnp.einsum('ncx,cd->ndx', v_n, Wv_dst)[dst]
        y0, y1 = (rsh[:, 0], rsh[:, 1:4])
        w1 = rbf @ W_rbf
        m1_s, m1_v = _cg_tp(msg_s, msg_v, y0, y1, w1[:, :CS], w1[:, CS:2 * CS], w1[:, 2 * CS:2 * CS + CV], w1[:, 2 * CS + CV:2 * CS + 2 * CV], w1[:, 2 * CS + 2 * CV:])
        a = (m1_s @ W_alpha).reshape(e, H, AS_)
        a = jnp.where(a > 0, a, 0.2 * a)
        a = jnp.sum(a * alpha_dot, axis=-1, keepdims=True)
        amax = jax.ops.segment_max(a, dst, num_segments=n)
        amax = jnp.where(jnp.isfinite(amax), amax, 0.0)
        ex = jnp.exp(a - amax[dst])
        den = jax.ops.segment_sum(ex, dst, num_segments=n)
        alpha = ex / (den[dst] + 1e-16)
        val_s = m1_s @ Ws_val
        val_v = jnp.einsum('ecx,cd->edx', m1_v, Wv_val)
        val_v = val_v * jax.nn.sigmoid(val_s @ Wg)[..., None]
        val_s = jax.nn.sigmoid(val_s)
        m2_s, m2_v = _cg_tp(val_s, val_v, y0, y1, w2_ss, w2_sv, w2_vs, w2_vv0, w2_vv1)
        hs = (m2_s @ Ws_vlin).reshape(e, H, AS_)
        hv = jnp.einsum('ecx,cd->edx', m2_v, Wv_vlin).reshape(e, H, AV, 3)
        h = jnp.concatenate([hs, hv.reshape(e, H, AV * 3)], axis=-1)
        agg = jax.ops.segment_sum(alpha * h, dst, num_segments=n)
        agg_s = agg[:, :, :AS_].reshape(n, H * AS_)
        agg_v = agg[:, :, AS_:].reshape(n, H * AV, 3)
        out = node + jnp.concatenate([agg_s @ Wps, jnp.einsum('ncx,cd->ndx', agg_v, Wpv).reshape(n, CV * 3)], axis=-1)
        return out

    def _L3_gnn_ref(node_input, node_attr, edge_attr, edge_scalars, W_sc_s, W_sc_v, W1_s, W1_v, W2_s, W2_v, W3, fcW1, fcW2, edge_src, edge_dst):
        import jax, jax.numpy as jnp
        import numpy as np
        N = 2500
        E = 25000
        MUL0, MUL1 = (64, 32)
        RAD, HID = (8, 64)
        WNUM = 192
        NUM_NEIGHBORS = 10.0
        INV3 = 1.0 / np.sqrt(3.0)

        def _lin(s, v, Ws, Wv, attr):
            out_s = s @ Ws * attr * (1.0 / np.sqrt(Ws.shape[0]))
            out_v = jnp.einsum('nud,uv->nvd', v, Wv) * attr[..., None] * (1.0 / np.sqrt(Wv.shape[0]))
            return (out_s, out_v)
        n = node_input.shape[0]
        s_in = node_input[:, :MUL0]
        v_in = node_input[:, MUL0:].reshape(n, MUL1, 3)
        sc_s, sc_v = _lin(s_in, v_in, W_sc_s, W_sc_v, node_attr)
        f_s, f_v = _lin(s_in, v_in, W1_s, W1_v, node_attr)
        h = jax.nn.silu(edge_scalars @ fcW1 * (1.0 / np.sqrt(RAD)))
        w = h @ fcW2 * (1.0 / np.sqrt(HID))
        wA, wB, wC, wD = (w[:, :64], w[:, 64:128], w[:, 128:160], w[:, 160:192])
        xs = f_s[edge_src]
        xv = f_v[edge_src]
        y0 = edge_attr[:, :1]
        y1 = edge_attr[:, 1:4]
        outA = wA * xs * y0
        outD = wD * jnp.einsum('eud,ed->eu', xv, y1) * INV3
        outB = wB[:, :, None] * xs[:, :, None] * y1[:, None, :]
        outC = wC[:, :, None] * xv * y0[:, :, None]
        edge_feat = jnp.concatenate([outA, outD, outB.reshape(-1, MUL0 * 3), outC.reshape(-1, MUL1 * 3)], axis=1)
        agg = jax.ops.segment_sum(edge_feat, edge_dst, num_segments=n)
        agg = agg * (1.0 / np.sqrt(NUM_NEIGHBORS))
        ms = agg[:, :MUL0 + MUL1]
        mv = agg[:, MUL0 + MUL1:].reshape(n, MUL0 + MUL1, 3)
        c_s, c_v = _lin(ms, mv, W2_s, W2_v, node_attr)
        conv = jnp.concatenate([c_s, c_v.reshape(n, -1)], axis=1)
        sc = jnp.concatenate([sc_s, sc_v.reshape(n, -1)], axis=1)
        angle = 0.1 * (ms @ W3) * node_attr * (1.0 / np.sqrt(MUL0 + MUL1))
        cos, sin = (jnp.cos(angle), jnp.sin(angle))
        return cos * sc + sin * conv
    edge_index = jnp.stack([src, dst])
    x = _layernorm(x + _L0_gnn_ref(x, node_vec1, edge_attr_3, edge_attr_64, src, dst, L0_gnn_ln1_w0, L0_gnn_ln1_b0, L0_gnn_ln1_w1, L0_gnn_ln2_w0, L0_gnn_ln2_b0, L0_gnn_ln2_w1, L0_gnn_msrc_ws, L0_gnn_msrc_wv, L0_gnn_mdst_ws, L0_gnn_mdst_bs, L0_gnn_mdst_wv, L0_gnn_rw1, L0_gnn_rb1, L0_gnn_rg1, L0_gnn_rbe1, L0_gnn_rw2, L0_gnn_rb2, L0_gnn_rg2, L0_gnn_rbe2, L0_gnn_rw3, L0_gnn_roff, L0_gnn_lin_ws, L0_gnn_lin_bs, L0_gnn_lin_wv, L0_gnn_alpha_dot, L0_gnn_proj_ws, L0_gnn_proj_bs, L0_gnn_proj_wv, L0_gnn_f1_ws, L0_gnn_f1_bs, L0_gnn_f1_wv, L0_gnn_f2_ws, L0_gnn_f2_bs, L0_gnn_f2_wv), axis=-1)
    x = _layernorm(x + _L1_gnn_ref(x, edge_attr_3, edge_attr_64, L1_gnn_W_skip0, L1_gnn_W_skip1, L1_gnn_W_nl0, L1_gnn_W_nl1, L1_gnn_W_fc1, L1_gnn_W_fc2, L1_gnn_W_out_s, L1_gnn_W_out_v, edge_index), axis=-1)
    x = _layernorm(x + _L2_gnn_ref(x, edge_attr_16, edge_attr_4, L2_gnn_gamma_s, L2_gnn_beta_s, L2_gnn_gamma_v, L2_gnn_Ws_src, L2_gnn_Wv_src, L2_gnn_Ws_dst, L2_gnn_Wv_dst, L2_gnn_W_rbf, L2_gnn_W_alpha, L2_gnn_alpha_dot, L2_gnn_Ws_val, L2_gnn_Wv_val, L2_gnn_Wg, L2_gnn_w2_ss, L2_gnn_w2_sv, L2_gnn_w2_vs, L2_gnn_w2_vv0, L2_gnn_w2_vv1, L2_gnn_Ws_vlin, L2_gnn_Wv_vlin, L2_gnn_Wps, L2_gnn_Wpv, edge_index), axis=-1)
    x = _layernorm(x + _L3_gnn_ref(x, node_vec1, edge_attr_4, edge_attr_8, L3_gnn_W_sc_s, L3_gnn_W_sc_v, L3_gnn_W1_s, L3_gnn_W1_v, L3_gnn_W2_s, L3_gnn_W2_v, L3_gnn_W3, L3_gnn_fcW1, L3_gnn_fcW2, src, dst), axis=-1)
    return x

_drawn_inputs = setup_inputs


def setup_inputs(seed=0):
    import zlib

    import numpy as np

    out = dict(_drawn_inputs(seed))
    spreads = {'L0_gnn_ln1_w0': (1.0, 0.2),
     'L0_gnn_ln1_b0': (0.0, 0.386),
     'L0_gnn_ln1_w1': (1.0, 0.6),
     'L0_gnn_ln2_w0': (1.0, 0.6),
     'L0_gnn_ln2_b0': (0.0, 0.8),
     'L0_gnn_ln2_w1': (1.0, 0.6),
     'L0_gnn_mdst_bs': (0.0, 0.54),
     'L0_gnn_rb1': (0.0, 0.1),
     'L0_gnn_rg1': (1.0, 0.2),
     'L0_gnn_rbe1': (0.0, 0.291),
     'L0_gnn_rb2': (0.0, 0.1),
     'L0_gnn_rg2': (1.0, 0.2),
     'L0_gnn_rbe2': (0.0, 0.305),
     'L0_gnn_lin_bs': (0.0, 0.275),
     'L0_gnn_proj_bs': (0.0, 0.1),
     'L0_gnn_f1_bs': (0.0, 0.8),
     'L0_gnn_f2_bs': (0.0, 0.531),
     'L2_gnn_gamma_s': (1.0, 0.6),
     'L2_gnn_beta_s': (0.0, 0.8),
     'L2_gnn_gamma_v': (1.0, 0.6)}
    factors = {'edge_attr_8': 8.0,
     'L1_gnn_W_nl1': 2.79,
     'L1_gnn_W_fc1': 2.741,
     'L1_gnn_W_out_s': 2.7,
     'L1_gnn_W_out_v': 2.965,
     'L2_gnn_w2_vv1': 3.158,
     'L3_gnn_W1_s': 8.0,
     'L3_gnn_W1_v': 8.0,
     'L3_gnn_W2_s': 8.0,
     'L3_gnn_W2_v': 8.0,
     'L3_gnn_W3': 8.0,
     'L3_gnn_fcW1': 8.0,
     'L3_gnn_fcW2': 8.0,
     'L3_gnn_W_sc_s': 7.791,
     'L3_gnn_W_sc_v': 7.095}
    for name, (base, spread) in spreads.items():
        noise = np.random.default_rng([zlib.crc32(name.encode()), seed]).standard_normal(out[name].shape)
        drawn = base * np.exp(spread * noise) if base else spread * noise
        out[name] = jnp.asarray(drawn.astype(out[name].dtype))
    for name, factor in factors.items():
        out[name] = (out[name] * factor).astype(out[name].dtype)
    return out
```

```python
from contextlib import ExitStack

import numpy as np

import concourse.bass as bass
from concourse import mybir

F32 = mybir.dt.float32
I32 = mybir.dt.int32
ALU = mybir.AluOpType
ACT = mybir.ActivationFunctionType
AX = mybir.AxisListType

P = 128
N_NODES, N_EDGES = 6250, 100000
C0, C1 = 64, 32
C1V = 3 * C1
CX = C0 + C1V
NT = -(-N_NODES // P)
ET = 784
NPAD, EPAD = P * NT, P * ET
G = 7
NG = NT // G
TM = 4
NM = ET // TM
ME = TM * P
ROWS = NPAD + P
ACC_W = (168, 480, 164, 384)
NBIG = -1.0e30
SQ3 = float(np.sqrt(np.float32(3.0)))


class Names:

    def __init__(self, nc, ctx, tag):
        self.nc, self.ctx, self.tag, self.sems = nc, ctx, tag, {}
        ctx.callback(self.release)

    def release(self):
        self.nc.clear_and_free_semaphores(list(self.sems.values()))
        self.nc.all_engine_barrier()

    def sb(self, name, shape, dt=F32):
        return self.ctx.enter_context(self.nc.sbuf_tensor(f"{self.tag}_{name}", shape, dt))

    def ps(self, name, shape):
        return self.ctx.enter_context(self.nc.psum_tensor(f"{self.tag}_{name}", shape, F32))

    def sem(self, name):
        if name not in self.sems:
            self.sems[name] = self.nc.alloc_semaphore(f"{self.tag}_{name}")
        return self.sems[name]


def wait(eng, sem, value):
    if not isinstance(value, int) or value > 0:
        eng.wait_ge(sem, value)


def wait_apart(eng, sem, value, passed):
    if not isinstance(value, int):
        eng.wait_ge(sem, value)
        eng.sem_inc(passed, 1)
    elif value > 0:
        eng.wait_ge(sem, value)


def steps(eng, n_macros, last_skew, body):
    total = n_macros + last_skew
    lead = last_skew + last_skew % 2
    turns = (n_macros - lead) // 2

    def fixed(n):
        def i_of(skew):
            i = n - skew
            return (i, i % 2, i // 2) if 0 <= i < n_macros else None
        return i_of

    def looped(j, s):
        def i_of(skew):
            u = (s - skew) % 2
            half = (s - skew - u) // 2
            return (j + half) * 2 + u, u, j + half
        return i_of

    for n in range(lead):
        body(fixed(n))
    with eng.Fori(lead // 2, lead // 2 + turns) as j:
        for s in range(2):
            body(looped(j, s))
    for n in range(lead + 2 * turns, total):
        body(fixed(n))


def bcast(ap, axis, n):
    ap = ap.unsqueeze(axis)
    shape = list(ap.shape)
    shape[axis] = n
    return ap.to_broadcast(shape)


def col(ap):
    return ap.rearrange("(a b) -> a b", b=1)


def row(ap):
    return ap.rearrange("(a b) -> a b", a=1)



def setup(nc, ctx, D):
    N = Names(nc, ctx, "w")
    W = {}
    loads = []

    def tile(name, shape, *parts, dt=F32):
        W[name] = N.sb(name, shape, dt)
        loads.extend((W[name], region, src) for region, src in parts)

    def whole(name, shape, src):
        tile(name, shape, ((slice(0, shape[0]), slice(0, shape[1])), src))

    def blocks(name, shape, src, at):
        r, c = src.shape
        tile(name, shape, *[((slice(a, a + r), slice(b, b + c)), src) for a, b in at])

    W["x"] = N.sb("x", [P, NT, CX])
    W["na"] = N.sb("na", [P, NT])
    W["ident"] = N.sb("ident", [P, P])
    W["tri"] = N.sb("tri", [P, P])
    W["spare"] = N.sb("spare", [P, 1], I32)
    W["zeros"] = N.sb("zeros", [P, 2400])
    W["half"] = N.sb("half", [P, 16])
    diag3 = [(C1 * d, C1 * d) for d in range(3)]

    tile("l0_rw1", [65, 64], ((slice(0, 64), slice(0, 64)), D["L0_gnn_rw1"]), ((slice(64, 65), slice(0, 64)), row(D["L0_gnn_rb1"])))
    tile("l0_rw2", [65, 64], ((slice(0, 64), slice(0, 64)), D["L0_gnn_rw2"]), ((slice(64, 65), slice(0, 64)), row(D["L0_gnn_rb2"])))
    tile("l0_rw3", [65, 224], ((slice(0, 64), slice(0, 224)), D["L0_gnn_rw3"]), ((slice(64, 65), slice(0, 224)), row(D["L0_gnn_roff"])))
    for k in ("rg1", "rbe1", "rg2", "rbe2", "ln1_w0", "ln1_b0", "ln2_w0", "ln2_b0"):
        whole("l0_" + k, [64, 1], col(D["L0_gnn_" + k]))
    for k in ("ln1_w1", "ln2_w1"):
        tile("l0_" + k, [96, 1], *[((slice(C1 * d, C1 * d + C1), slice(0, 1)), col(D["L0_gnn_" + k])) for d in range(3)])
    tile("l0_tab_s", [65, 128], ((slice(0, 64), slice(0, 64)), D["L0_gnn_msrc_ws"]), ((slice(0, 64), slice(64, 128)), D["L0_gnn_mdst_ws"]),
         ((slice(64, 65), slice(64, 128)), row(D["L0_gnn_mdst_bs"])))
    tile("l0_tab_v", [96, 192], *[((slice(32 * d, 32 * d + 32), slice(o + 32 * d, o + 32 * d + 32)), D["L0_gnn_" + k])
                                  for d in range(3) for o, k in ((0, "msrc_wv"), (96, "mdst_wv"))])
    message_weights(tile, "l0", [(D["L0_gnn_lin_ws"], 0)], D["L0_gnn_lin_wv"])
    tile("l0_bias", [P, 128], ((slice(0, P), slice(0, 128)), D["L0_gnn_lin_bs"].partition_broadcast(P)))
    tile("l0_adot", [P, 64], ((slice(0, P), slice(0, 64)), D["L0_gnn_alpha_dot"].rearrange("h a -> (h a)").partition_broadcast(P)))
    tile("l0_proj_s", [65, 64], ((slice(0, 64), slice(0, 64)), D["L0_gnn_proj_ws"]), ((slice(64, 65), slice(0, 64)), row(D["L0_gnn_proj_bs"])))
    blocks("l0_proj_v", [96, 96], D["L0_gnn_proj_wv"], diag3)
    tile("l0_f1_s", [65, 192], ((slice(0, 64), slice(0, 192)), D["L0_gnn_f1_ws"]), ((slice(64, 65), slice(0, 192)), row(D["L0_gnn_f1_bs"])))
    blocks("l0_f1_v", [96, 192], D["L0_gnn_f1_wv"], [(C1 * d, 64 * d) for d in range(3)])
    whole("l0_f2_s", [128, 64], D["L0_gnn_f2_ws"])
    blocks("l0_f2_va", [128, 96], D["L0_gnn_f2_wv"], [(0, 0), (64, 32)])
    blocks("l0_f2_vb", [64, 96], D["L0_gnn_f2_wv"], [(0, 64)])
    tile("l0_f2_b", [P, 64], ((slice(0, P), slice(0, 64)), D["L0_gnn_f2_bs"].partition_broadcast(P)))
    whole("l1_fc1", [64, 64], D["L1_gnn_W_fc1"])
    whole("l1_fc2", [64, 224], D["L1_gnn_W_fc2"])
    whole("l1_tab_s", [64, 64], D["L1_gnn_W_nl0"])
    blocks("l1_tab_v", [96, 96], D["L1_gnn_W_nl1"], diag3)
    whole("l1_skip_s", [64, 96], D["L1_gnn_W_skip0"])
    blocks("l1_skip_v", [96, 96], D["L1_gnn_W_skip1"], diag3)
    whole("l1_out_s", [96, 96], D["L1_gnn_W_out_s"])
    whole("l1_out_v", [128, 32], D["L1_gnn_W_out_v"])
    whole("l2_rbf", [16, 224], D["L2_gnn_W_rbf"])
    for k in ("gamma_s", "beta_s"):
        whole("l2_" + k, [64, 1], col(D["L2_gnn_" + k]))
    tile("l2_gamma_v", [96, 1], *[((slice(C1 * d, C1 * d + C1), slice(0, 1)), col(D["L2_gnn_gamma_v"])) for d in range(3)])
    tile("l2_tab_s", [64, 128], ((slice(0, 64), slice(0, 64)), D["L2_gnn_Ws_src"]), ((slice(0, 64), slice(64, 128)), D["L2_gnn_Ws_dst"]))
    tile("l2_tab_v", [96, 192], *[((slice(32 * d, 32 * d + 32), slice(o + 32 * d, o + 32 * d + 32)), D["L2_gnn_" + k])
                                  for d in range(3) for o, k in ((0, "Wv_src"), (96, "Wv_dst"))])
    message_weights(tile, "l2", [(D["L2_gnn_W_alpha"], 0), (D["L2_gnn_Ws_val"], 64)], D["L2_gnn_Wv_val"])
    message_weights(tile, "l2b", [(D["L2_gnn_Ws_vlin"], 0)], D["L2_gnn_Wv_vlin"])
    whole("l2_wg", [64, 32], D["L2_gnn_Wg"])
    tile("l2_adot", [P, 64], ((slice(0, P), slice(0, 64)), D["L2_gnn_alpha_dot"].rearrange("o h a -> (o h a)").partition_broadcast(P)))
    tile("l2_w2", [P, 3], *[((slice(a, a + n), slice(c, c + 1)), col(D["L2_gnn_" + k])) for k, a, n, c in (
        ("w2_ss", 0, 64, 0), ("w2_vv0", 64, 32, 0), ("w2_vv1", 96, 32, 0),
        ("w2_vv1", 0, 32, 1), ("w2_vv1", 32, 32, 1), ("w2_sv", 64, 64, 1),
        ("w2_vs", 0, 32, 2), ("w2_vs", 32, 32, 2), ("w2_vs", 64, 32, 2))])
    whole("l2_proj_s", [64, 64], D["L2_gnn_Wps"])
    blocks("l2_proj_v", [96, 96], D["L2_gnn_Wpv"], diag3)
    whole("l3_fc1", [8, 64], D["L3_gnn_fcW1"])
    whole("l3_fc2", [64, 192], D["L3_gnn_fcW2"])
    whole("l3_tab_s", [64, 64], D["L3_gnn_W1_s"])
    blocks("l3_tab_v", [96, 96], D["L3_gnn_W1_v"], diag3)
    whole("l3_sc_s", [64, 64], D["L3_gnn_W_sc_s"])
    blocks("l3_sc_v", [96, 96], D["L3_gnn_W_sc_v"], diag3)
    tile("l3_w2_s", [96, 65], ((slice(0, 96), slice(0, 64)), D["L3_gnn_W2_s"]), ((slice(0, 96), slice(64, 65)), D["L3_gnn_W3"]))
    whole("l3_w2_v", [96, 32], D["L3_gnn_W2_v"])

    cleared = [k for k in W if k not in ("x", "na", "ident", "tri", "spare", "half")]
    with ExitStack() as inner:
        L = Names(nc, inner, "setup")
        filled, loaded, shaped, wiped = L.sem("filled"), L.sem("loaded"), L.sem("shaped"), L.sem("wiped")
        mean = L.sb("mean", [65, 2])
        block = inner.enter_context(nc.Block())
        n_acc = sum(-(-(ROWS // P * w) // 2400) for w in ACC_W[:1]) * TM

        @block.gpsimd
        def _(pool):
            nc.gpsimd.memset(W["ident"][:, :], 0.0).then_inc(filled, 1)
            nc.gpsimd.memset(W["tri"][:, :], 1.0).then_inc(filled, 1)
            nc.gpsimd.memset(W["half"][:, :], -0.5).then_inc(filled, 1)
            nc.gpsimd.iota(W["spare"][:, :], [[0, 1]], base=NPAD, channel_multiplier=1).then_inc(filled, 1)
            pool.wait_ge(filled, 4)
            nc.gpsimd.affine_select(out=W["ident"][:, :], in_=W["ident"][:, :], compare_op=ALU.not_equal, fill=1.0,
                                    base=0, pattern=[[-1, P]], channel_multiplier=1).then_inc(shaped, 1)
            nc.gpsimd.affine_select(out=W["tri"][:, :], in_=W["tri"][:, :], compare_op=ALU.is_gt, fill=0.0,
                                    base=0, pattern=[[-1, P]], channel_multiplier=1).then_inc(shaped, 1)

        @block.vector
        def _(dve):
            for k in cleared:
                t = W[k]
                last = nc.vector.memset(t[:, :], 0.0)
            last.then_inc(wiped, 1)
            dve.wait_ge(loaded, 16 * (len(loads) + 2))
            n = 0

            def link(ins):
                nonlocal n
                n += 1
                ins.then_inc(shaped_dve, 1)
                dve.wait_ge(shaped_dve, n)

            shaped_dve = L.sem("shaped_dve")
            for c, k in enumerate(("l0_rw1", "l0_rw2")):
                link(nc.vector.tensor_reduce(mean[:, c:c + 1], W[k][:, :], AX.X, ALU.add))
                link(nc.vector.tensor_scalar(mean[:, c:c + 1], mean[:, c:c + 1], 1.0 / 64, None, ALU.mult))
                link(nc.vector.tensor_scalar(W[k][:, :], W[k][:, :], mean[:, c:c + 1], None, ALU.subtract))
            link(nc.vector.tensor_scalar(W["l0_adot"][:, :], W["l0_adot"][:, :], 0.4, None, ALU.mult))

            def scale(k, rows, cols, by):
                t = W[k][rows, cols]
                link(nc.vector.tensor_scalar(t, t, by, None, ALU.mult))

            A = slice(None)
            scale("l0_t1", slice(64, 128), A, SQ3)
            scale("l0_x0", slice(96, 128), A, float(np.sqrt(1.5)))
            scale("l0_t1", slice(0, 64), A, float(np.sqrt(1.5)))
            for k, w2 in (("l2", False), ("l2b", True)):
                scale(k + "_t0", slice(64, 96), A, 1.0 / SQ3)
                scale(k + "_x0", slice(96, 128), A, float(np.sqrt(0.5)))
                scale(k + "_t1", slice(0, 64), A, float(np.sqrt(0.5)))
                if w2:
                    scale(k + "_t0", slice(0, 96), A, W["l2_w2"][0:96, 0:1])
                    scale(k + "_x0", slice(96, 128), A, W["l2_w2"][96:128, 0:1])
                    scale(k + "_t1", A, A, W["l2_w2"][:, 1:2])
                    scale(k + "_t2", A, A, W["l2_w2"][0:96, 2:3])
            scale("l1_out_s", A, A, 1.0 / 32)
            scale("l1_out_v", slice(0, 64), A, SQ3 / 32)
            scale("l1_out_v", slice(64, 96), A, 1.0 / 32)
            scale("l1_out_v", slice(96, 128), A, SQ3 / 32 / float(np.sqrt(2.0)))
            f = 1.0 / 8 / float(np.sqrt(10.0)) / float(np.sqrt(96.0))
            scale("l3_tab_s", A, A, 1.0 / 8)
            scale("l3_tab_v", A, A, 1.0 / float(np.sqrt(32.0)))
            scale("l3_sc_s", A, A, 1.0 / 8)
            scale("l3_sc_v", A, A, 1.0 / float(np.sqrt(32.0)))
            scale("l3_w2_s", A, slice(0, 64), f)
            scale("l3_w2_s", A, slice(64, 65), 0.1 * f)
            scale("l3_w2_s", slice(64, 96), A, 1.0 / SQ3)
            scale("l3_w2_v", A, A, f)

        @block.sync
        def _(sp):
            sp.dma_start(W["x"][:, :, :], D["x"].rearrange("(p t) c -> p t c", p=P)).then_inc(loaded, 16)
            sp.dma_start(W["na"][:, :], D["node_vec1"]).then_inc(loaded, 16)
            sp.wait_ge(wiped, 1)
            for t, region, src in loads[0::2]:
                sp.dma_start(t[region], src).then_inc(loaded, 16)
            n = 0
            for k in range(TM):
                n += clear(sp, W["zeros"], D["acc"][0][k], ACC_W[0], L.sem("clear"))
            sp.wait_ge(L.sem("clear"), 16 * n)

        @block.scalar
        def _(act):
            act.wait_ge(wiped, 1)
            for t, region, src in loads[1::2]:
                act.dma_start(t[region], src).then_inc(loaded, 16)
    return W


def message_weights(tile, tag, scalar, vector):
    width = max(o + s.shape[1] for s, o in scalar)
    wb, wc, wx = vector[0:64, :], vector[64:96, :], vector[96:128, :]
    tile(tag + "_t0", [96, width], *[((slice(0, 96), slice(o, o + s.shape[1])), s) for s, o in scalar])
    tile(tag + "_x0", [128, 96], ((slice(96, 128), slice(0, 32)), wx))
    tile(tag + "_t1", [128, 128], ((slice(0, 32), slice(32, 64)), wx), ((slice(32, 64), slice(64, 96)), wx),
         ((slice(64, 128), slice(96, 128)), wb))
    tile(tag + "_t2", [96, 96], *[((slice(32 * d, 32 * d + 32), slice(32 * d, 32 * d + 32)), wc) for d in range(3)])


def clear(sp, zeros, acc, width, done):
    per = ROWS // P * width
    flat = acc.rearrange("(p t) c -> p (t c)", p=P)
    n = 0
    for a in range(0, per, zeros.shape[1]):
        b = min(per, a + zeros.shape[1])
        sp.dma_start(flat[:, a:b], zeros[:, 0:b - a]).then_inc(done, 16)
        n += 1
    return n



F_A, F_D, F_X, F_B, F_C, F_W = 0, 64, 96, 192, 256, 384


def load_directions(nc, S, D, eps):
    vec, dirs, norm = S.sb("vec", [P, ET, 3]), S.sb("dirs", [P, ET, 5]), S.sb("norm", [P, ET])
    expo = S.sb("expo", [P, ET])
    loaded, steps_done, root = S.sem("vec_loaded"), S.sem("norm_steps"), S.sem("norm_root")

    def sp_part(sp):
        sp.dma_start(vec[:, :, :], D["edge_attr_3"].rearrange("p (t c) -> p t c", c=3)).then_inc(loaded, 16)

    def pool_part(pool):
        pool.wait_ge(steps_done, 4)
        nc.gpsimd.tensor_tensor(norm[:, :], norm[:, :], expo[:, :], ALU.pow).then_inc(root, 1)

    def dve_part(dve):
        nc.vector.memset(expo[:, :], -0.5).then_inc(steps_done, 1)
        dve.wait_ge(loaded, 16)
        sq = dirs[:, :, 0:3]
        nc.vector.tensor_tensor(sq, vec[:, :, :], vec[:, :, :], ALU.mult).then_inc(steps_done, 1)
        dve.wait_ge(steps_done, 2)
        nc.vector.tensor_reduce(norm[:, :], sq, AX.X, ALU.add).then_inc(steps_done, 1)
        dve.wait_ge(steps_done, 3)
        nc.vector.tensor_scalar(norm[:, :], norm[:, :], eps, None, ALU.add).then_inc(steps_done, 1)
        dve.wait_ge(root, 1)
        nc.vector.tensor_tensor(dirs[:, :, 0:3], vec[:, :, :], bcast(norm[:, :], 2, 3), ALU.mult).then_inc(steps_done, 1)
        nc.vector.tensor_tensor(dirs[:, :, 3:5], vec[:, :, 0:2], bcast(norm[:, :], 2, 2), ALU.mult).then_inc(steps_done, 1)
        dve.wait_ge(steps_done, 6)

    return dirs, sp_part, pool_part, dve_part


def comp(ap, n=3):
    return ap.rearrange("p t (d c) -> p t d c", d=n)


def dirs_of(dirs, i, a, b):
    return bcast(dirs[:, bass.ds(i * TM, TM), a:b], 3, C1)


def dve_cross(nc, dve, i, O, tmp, dirs, c0, x0, u0, S, tag):
    first, second, done = S.sem(tag + "_first"), S.sem(tag + "_second"), S.sem(tag + "_done")
    wait(dve, done, i)
    X = lambda a, b: O[:, :, x0 + C1 * a:x0 + C1 * b]
    T = lambda n, a, b: comp(tmp[:, n, :, C1 * a:C1 * b], b - a)
    tt = nc.vector.tensor_tensor
    tt(T(0, 0, 3), bcast(O[:, :, u0:u0 + C1], 2, 3), dirs_of(dirs, i, 0, 3), ALU.mult)
    tt(T(1, 0, 2), comp(X(1, 3), 2), dirs_of(dirs, i, 2, 4), ALU.mult)
    tt(T(1, 2, 3), comp(X(0, 1), 1), dirs_of(dirs, i, 4, 5), ALU.mult)
    tt(T(2, 0, 1), comp(X(2, 3), 1), dirs_of(dirs, i, 1, 2), ALU.mult)
    tt(T(2, 1, 3), comp(X(0, 2), 2), dirs_of(dirs, i, 2, 4), ALU.mult).then_inc(first, 1)
    C = O[:, :, c0:c0 + C1V]
    dve.wait_ge(first, i + 1)
    tt(C, C, tmp[:, 0, :, :], ALU.add)
    tt(tmp[:, 1, :, :], tmp[:, 1, :, :], tmp[:, 2, :, :], ALU.subtract).then_inc(second, 1)
    dve.wait_ge(second, i + 1)
    tt(C, C, tmp[:, 1, :, :], ALU.add).then_inc(done, 1)


def pe_linear(nc, pe, i, F, FT, psF, psO, W, w, scalars, ident, S, tag, free_f, free_o):
    turned, linear, moved = S.sem(tag + "_turned"), S.sem(tag + "_linear"), S.sem(tag + "_FT")
    passed = S.sem("pe_passed")
    c0, x0, u0 = scalars, scalars + C1V, scalars + 2 * C1V

    def turn(k):
        wait_apart(pe, *free_f(k), passed)
        for g in range(3):
            last = nc.tensor.transpose(psF[:, k % 2, P * g:P * g + P], F[:, k, P * g:P * g + P], ident[:, :])
        last.then_inc(turned, 1)

    def maps(k):
        wait_apart(pe, moved, i * TM + k + 1, passed)
        wait_apart(pe, *free_o(k), passed)
        o, f = psO[:, k % psO.shape[1], :], FT[:, k % 2, :]
        nc.tensor.matmul(o[:, 0:scalars], f[0:96, 0:P], W[w + "_t0"][:, :], start=True, stop=True, skip_group_check=True)
        nc.tensor.matmul(o[:, x0:x0 + C1V], f[:, 0:P], W[w + "_x0"][:, :], start=True, stop=False, skip_group_check=True)
        nc.tensor.matmul(o[:, x0:x0 + P], f[:, P:2 * P], W[w + "_t1"][:, :], start=False, stop=True, skip_group_check=True)
        nc.tensor.matmul(o[:, c0:c0 + C1V], f[0:96, 2 * P:3 * P], W[w + "_t2"][:, :], start=True, stop=True,
                         skip_group_check=True).then_inc(linear, 1)

    turn(0)
    turn(1)
    maps(0)
    turn(2)
    maps(1)
    turn(3)
    maps(2)
    maps(3)


def act_linear(nc, act, i, FT, psF, O, psO, width, S, tag):
    turned, linear, moved, out = S.sem(tag + "_turned"), S.sem(tag + "_linear"), S.sem(tag + "_FT"), S.sem(tag + "_O")

    def move(k):
        act.wait_ge(turned, i * TM + k + 1)
        wait(act, linear, i * TM + k - 1)
        nc.scalar.activation(FT[:, k % 2, :], psF[:, k % 2, 0:F_W], ACT.Copy).then_inc(moved, 1)

    def result(k):
        act.wait_ge(linear, i * TM + k + 1)
        nc.scalar.activation(O[:, k, :], psO[:, k % psO.shape[1], 0:width], ACT.Copy).then_inc(out, 1)

    move(0)
    move(1)
    result(0)
    move(2)
    result(1)
    move(3)
    result(2)
    result(3)


def sp_indices(sp, i, u, j, ix, D, keys, S, used):
    wait_apart(sp, used[u], j * 16 * TM * len(keys), S.sem("sp_passed"))
    for n, k in enumerate(keys):
        sp.dma_start(ix[u][:, n, :], D[k][:, bass.ds(i * TM, TM)]).then_inc(S.sem(f"ix{u}"), 16)


def pool_gather(nc, pool, i, u, j, ix, tables, into, S, free):
    n = len(tables)
    wait_apart(pool, S.sem(f"ix{u}"), (j + 1) * 16 * n, S.sem("pool_passed"))
    wait_apart(pool, *free, S.sem("pool_passed"))
    for t in range(n):
        for k in range(TM):
            pool.indirect_dma_start(into[t][u][:, k, :], None, tables[t], bass.IndirectOffsetOnAxis(ix[u][:, t, k:k + 1], 0))\
                .then_inc(S.sem(f"gathered{u}"), 16)


def scatter_tensors(S, width):
    return dict(krow=[S.sb(f"krow{u}", [P, TM, P], I32) for u in range(2)],
                kcol=[S.sb(f"kcol{u}", [P, TM], I32) for u in range(2)],
                same=[S.sb(f"same{u}", [P, TM, P]) for u in range(2)], early=S.sb("early", [P, TM, P]), count=S.sb("count", [P, TM]),
                away=S.sb("away", [P, TM]), row=[S.sb(f"row{u}", [P, TM], I32) for u in range(2)],
                sums=[S.sb(f"sums{u}", [P, TM, width]) for u in range(2)])


def sp_keys(sp, i, u, j, T, D, key, S):
    wait_apart(sp, S.sem("rows"), i - 1, S.sem("sp_passed"))
    sp.dma_start(T["kcol"][u][:, :], D[key][:, bass.ds(i * TM, TM)]).then_inc(S.sem(f"keys{u}"), 16)
    sp.dma_start(T["krow"][u][:, :, :], D[key + "_t"][bass.ds(i * TM, TM), :].partition_broadcast(P))\
        .then_inc(S.sem(f"keys{u}"), 16)


def dve_rows(nc, dve, i, u, j, T, W, S):
    dve.wait_ge(S.sem(f"keys{u}"), (j + 1) * 32)
    wait(dve, S.sem("summed"), (i - 1) * TM)
    nc.vector.tensor_tensor(T["same"][u][:, :, :], T["krow"][u][:, :, :], bcast(T["kcol"][u][:, :], 2, P),
                            ALU.is_equal).then_inc(S.sem("same"), 1)
    dve.wait_ge(S.sem("same"), i + 1)
    wait(dve, S.sem("rows"), i)
    for k in range(TM):
        nc.vector.tensor_tensor_reduce(T["early"][:, k, :], T["same"][u][:, k, :], W["tri"][:, :], 1.0, 0.0, ALU.mult, ALU.add,
                                       T["count"][:, k:k + 1]).then_inc(S.sem("counted"), 1)
    nc.vector.tensor_tensor(T["away"][:, :], W["spare"][:, 0:1].to_broadcast([P, TM]), T["kcol"][u][:, :], ALU.subtract)\
        .then_inc(S.sem("away"), 1)
    dve.wait_ge(S.sem("counted"), (i + 1) * TM)
    dve.wait_ge(S.sem("away"), 2 * i + 1)
    nc.vector.scalar_tensor_tensor(out=T["away"][:, :], in0=T["count"][:, :], scalar=1.0, in1=T["away"][:, :], op0=ALU.min,
                                   op1=ALU.mult).then_inc(S.sem("away"), 1)
    dve.wait_ge(S.sem("away"), 2 * i + 2)
    for k in range(TM):
        wait(dve, S.sem(f"added{k}"), (i - 1) * 16)
    nc.vector.tensor_tensor(T["row"][u][:, :], T["away"][:, :], T["kcol"][u][:, :], ALU.add).then_inc(S.sem("rows"), 1)


def pe_sums(nc, pe, i, u, T, values, psS, S, ready):
    passed = S.sem("pe_passed")
    wait_apart(pe, S.sem("same"), i + 1, passed)
    wait_apart(pe, *ready, passed)
    for k in range(TM):
        wait_apart(pe, S.sem("sums"), i * TM + k - len(psS) + 1, passed)
        nc.tensor.matmul(psS[(k) % len(psS)], T["same"][u][:, k, :], values[:, k, :], start=True, stop=True)\
            .then_inc(S.sem("summed"), 1)


def act_sums(nc, act, i, u, j, T, psS, S):
    for k in range(TM):
        wait(act, S.sem(f"added{k}"), (i - 1) * 16)
        act.wait_ge(S.sem("summed"), i * TM + k + 1)
        nc.scalar.activation(T["sums"][u][:, k, :], psS[k % len(psS)], ACT.Copy).then_inc(S.sem("sums"), 1)


def pool_scatter(nc, pool, i, u, j, T, acc, S):
    passed = S.sem("pool_passed")
    wait_apart(pool, S.sem("rows"), i + 1, passed)
    for k in range(TM):
        wait_apart(pool, S.sem("sums"), i * TM + k + 1, passed)
        wait_apart(pool, S.sem(f"added{k}"), i * 16, passed)
        pool.indirect_dma_start(acc[k], bass.IndirectOffsetOnAxis(T["row"][u][:, k:k + 1], 0), T["sums"][u][:, k, :], None,
                                compute_op=ALU.add).then_inc(S.sem(f"added{k}"), 16)



def layer0_edges(nc, W, D, logits):
    with ExitStack() as ctx:
        S = Names(nc, ctx, "e0")
        dirs, sp_dirs, pool_dirs, dve_dirs = load_directions(nc, S, D, 1e-12)
        es = [S.sb(f"es{u}", [65, ME]) for u in range(2)]
        ix = [S.sb(f"ix{u}", [P, 2, TM], I32) for u in range(2)]
        gs, gd = ([S.sb(f"{n}{u}", [P, TM, CX]) for u in range(2)] for n in ("gs", "gd"))
        sq = [S.sb(f"sq{n}", [P, TM, 64]) for n in range(2)]
        hn = [S.sb(f"hn{n}", [P, TM, 64]) for n in range(2)]
        var = [S.sb(f"var{n}", [P, TM]) for n in range(2)]
        rstd = [S.sb(f"rstd{n}", [P, TM]) for n in range(2)]
        h = [S.sb(f"h{n}", [65, ME]) for n in range(2)]
        msg, prod, dot = S.sb("msg", [P, TM, CX]), S.sb("prod", [P, TM, C1V]), S.sb("dot", [P, TM, C1])
        F = [S.sb(f"F{u}", [P, TM, F_W]) for u in range(2)]
        FT, tmp = S.sb("FT", [P, 2, F_W]), S.sb("tmp", [P, 3, TM, C1V])
        O_W = 352
        O = [S.sb(f"O{u}", [P, TM, O_W]) for u in range(2)]
        xb, th = S.sb("xb", [P, TM, 64]), S.sb("th", [P, TM, 64])
        psH, psT = S.ps("psH", [P, 2, 512]), S.ps("psT", [P, 512])
        psW, psF, psO = S.ps("psW", [P, TM, 256]), S.ps("psF", [P, 2, 512]), S.ps("psO", [P, 1, 512])
        pre = [psH[:, n, 0:256].rearrange("p (t c) -> p t c", t=TM) for n in range(2)]
        sem = S.sem
        LAST = 5
        block = ctx.enter_context(nc.Block())

        @block.sync
        def _(sp):
            sp_dirs(sp)

            def body(i_of):
                if m := i_of(0):
                    i, u, j = m
                    wait_apart(sp, sem("pre0"), i - 1, S.sem("sp_passed"))
                    sp.dma_start(es[u][:, :], D["es64"][:, bass.ds(i * ME, ME)]).then_inc(sem(f"es{u}"), 16)
                    sp_indices(sp, i, u, j, ix, D, ("src", "dst"), S, [sem("gathered0"), sem("gathered1")])
                if m := i_of(LAST):
                    i, u, j = m
                    wait_apart(sp, sem("cross_done"), i + 1, sem("sp_passed"))
                    sp.dma_start(D["val"][:, bass.ds(i * TM, TM), :], O[u][:, :, 64:224]).then_inc(sem(f"stored{u}"), 16)

            steps(sp, NM, LAST, body)
            for u in range(2):
                sp.wait_ge(sem(f"stored{u}"), 16 * (NM // 2))

        @block.gpsimd
        def _(pool):
            pool_dirs(pool)

            def root(m, n):
                i = m[0]
                pool.wait_ge(sem(f"var{n}"), 2 * i + 2)
                wait(pool, sem(f"hn{n}"), i)
                nc.gpsimd.tensor_tensor(rstd[n][:, :], var[n][:, :], W["half"][:, 0:TM], ALU.pow).then_inc(sem(f"rstd{n}"), 1)

            def body(i_of):
                if m := i_of(1):
                    pool_gather(nc, pool, *m, ix, (D["tab_src"], D["tab_dst"]), (gs, gd), S, (sem("msg"), m[0] - 1))
                if m := i_of(0):
                    root(m, 0)
                if m := i_of(1):
                    root(m, 1)

            steps(pool, NM, LAST, body)

        @block.scalar
        def _(act):
            def square(m, n):
                i = m[0]
                act.wait_ge(sem(f"pre{n}"), i + 1)
                wait(act, sem(f"var{n}"), 2 * i - 1)
                nc.scalar.activation(sq[n][:, :, :], pre[n], ACT.Square).then_inc(sem(f"sq{n}"), 1)

            def silu(m, n):
                i = m[0]
                act.wait_ge(sem(f"turned_h{n}"), i + 1)
                wait(act, sem("pre1") if n == 0 else sem("weights"), i)
                nc.scalar.activation(h[n][0:64, :], psT[0:64, :], ACT.Silu, scale=W[f"l0_rg{n + 1}"][:, 0:1],
                                     bias=W[f"l0_rbe{n + 1}"][:, 0:1]).then_inc(sem(f"h{n}"), 1)

            def body(i_of):
                if m := i_of(2):
                    silu(m, 1)
                if m := i_of(1):
                    silu(m, 0)
                if m := i_of(0):
                    square(m, 0)
                if m := i_of(4):
                    act.wait_ge(sem("xb"), m[0] + 1)
                    wait(act, sem("leaky"), m[0])
                    nc.scalar.activation(th[:, :, :], xb[:, :, :], ACT.Tanh, scale=0.5).then_inc(sem("th"), 1)
                if m := i_of(1):
                    square(m, 1)
                if m := i_of(3):
                    i, u, j = m
                    wait(act, sem(f"stored{u}"), j * 16)
                    act_linear(nc, act, i, FT, psF, O[u], psO, O_W, S, "lin")

            steps(act, NM, LAST, body)

        @block.tensor
        def _(pe):
            passed = sem("pe_passed")

            def turn(m, n):
                i = m[0]
                wait_apart(pe, sem(f"hn{n}"), i + 1, passed)
                wait_apart(pe, sem("h0"), i + 1 if n == 1 else i, passed)
                wait_apart(pe, sem("h1"), i, passed)
                for k in range(TM):
                    last = nc.tensor.transpose(psT[0:64, P * k:P * k + P], hn[n][:, k, :], W["ident"][:, :])
                last.then_inc(sem(f"turned_h{n}"), 1)

            def body(i_of):
                if m := i_of(2):
                    turn(m, 1)
                if m := i_of(1):
                    turn(m, 0)
                if m := i_of(0):
                    i, u, j = m
                    wait_apart(pe, sem(f"es{u}"), (j + 1) * 16, passed)
                    wait_apart(pe, sem("hn0"), i, passed)
                    for k in range(TM):
                        last = nc.tensor.matmul(pre[0][:, k, :], es[u][:, P * k:P * k + P], W["l0_rw1"][:, :], start=True, stop=True)
                    last.then_inc(sem("pre0"), 1)
                if m := i_of(2):
                    i = m[0]
                    wait_apart(pe, sem("h1"), i + 1, passed)
                    wait_apart(pe, sem("products"), i, passed)
                    for k in range(TM):
                        last = nc.tensor.matmul(psW[:, k, 0:224], h[1][:, P * k:P * k + P], W["l0_rw3"][:, :], start=True, stop=True)
                    last.then_inc(sem("weights"), 1)
                if m := i_of(1):
                    i = m[0]
                    wait_apart(pe, sem("h0"), i + 1, passed)
                    wait_apart(pe, sem("hn1"), i, passed)
                    for k in range(TM):
                        last = nc.tensor.matmul(pre[1][:, k, :], h[0][:, P * k:P * k + P], W["l0_rw2"][:, :], start=True, stop=True)
                    last.then_inc(sem("pre1"), 1)
                if m := i_of(3):
                    i, u, j = m
                    wait_apart(pe, sem("products"), i + 1, passed)
                    pe_linear(nc, pe, i, F[u], FT, psF, psO, W, "l0", 128, W["ident"], S, "lin",
                              lambda k: (sem("lin_FT"), i * TM + k - 1), lambda k: (sem("lin_O"), i * TM + k))

            pe.wait_ge(sem("ones"), 4)
            steps(pe, NM, LAST, body)

        @block.vector
        def _(dve):
            for n in range(2):
                nc.vector.memset(h[n][64:65, :], 1.0).then_inc(sem("ones"), 1)
                nc.vector.memset(F[n][:, :, 352:F_W], 0.0).then_inc(sem("ones"), 1)
            dve_dirs(dve)
            tt = nc.vector.tensor_tensor

            def variance(m, n):
                i = m[0]
                dve.wait_ge(sem(f"sq{n}"), i + 1)
                wait(dve, sem(f"rstd{n}"), i)
                nc.vector.tensor_reduce(var[n][:, :], sq[n][:, :, :], AX.X, ALU.add).then_inc(sem(f"var{n}"), 1)
                dve.wait_ge(sem(f"var{n}"), 2 * i + 1)
                nc.vector.tensor_scalar(var[n][:, :], var[n][:, :], 1.0 / 64, 1e-5, ALU.mult, ALU.add).then_inc(sem(f"var{n}"), 1)

            def normalise(m, n):
                i = m[0]
                dve.wait_ge(sem(f"rstd{n}"), i + 1)
                wait(dve, sem(f"turned_h{n}"), i)
                tt(hn[n][:, :, :], pre[n], bcast(rstd[n][:, :], 2, 64), ALU.mult).then_inc(sem(f"hn{n}"), 1)

            def body(i_of):
                if m := i_of(2):
                    normalise(m, 1)
                if m := i_of(1):
                    normalise(m, 0)
                if m := i_of(0):
                    variance(m, 0)
                if m := i_of(4):
                    i, u, j = m
                    dve.wait_ge(sem("lin_O"), (i + 1) * TM)
                    wait(dve, sem("leaky"), i)
                    tt(xb[:, :, :], O[u][:, :, 0:64], bcast(W["l0_bias"][:, 0:64], 1, TM), ALU.add).then_inc(sem("xb"), 1)
                if m := i_of(2):
                    i, u, j = m
                    dve.wait_ge(sem(f"gathered{u}"), (j + 1) * 16 * 2 * TM)
                    wait(dve, sem("products"), i)
                    tt(msg[:, :, :], gs[u][:, :, :], gd[u][:, :, :], ALU.add).then_inc(sem("msg"), 1)
                if m := i_of(4):
                    i, u, j = m
                    dve_cross(nc, dve, i, O[u], tmp, dirs, 128, 224, 320, S, "cross")
                if m := i_of(2):
                    i, u, j = m
                    dve_products(nc, dve, i, psW, msg, msg, prod, dot, F[u], dirs_of(dirs, i, 0, 3), S,
                                 (sem("msg"), i + 1), (sem("lin_turned"), (i - 1) * TM))
                if m := i_of(4):
                    i, u, j = m
                    dve.wait_ge(sem("th"), i + 1)
                    nc.vector.scalar_tensor_tensor(out=xb[:, :, :], in0=th[:, :, :], scalar=1.5, in1=xb[:, :, :], op0=ALU.add,
                                                   op1=ALU.mult).then_inc(sem("leaky_a"), 1)
                    dve.wait_ge(sem("leaky_a"), 2 * i + 1)
                    tt(xb[:, :, :], xb[:, :, :], bcast(W["l0_adot"][:, :], 1, TM), ALU.mult).then_inc(sem("leaky_a"), 1)
                    dve.wait_ge(sem("leaky_a"), 2 * i + 2)
                    dve.sem_inc(sem("dve_passed"), 1)
                    nc.vector.tensor_reduce(logits[:, bass.ds(i * TM, TM), :], xb[:, :, :].rearrange("p t (h a) -> p t h a", a=8),
                                            AX.X, ALU.add).then_inc(sem("leaky"), 1)
                if m := i_of(1):
                    variance(m, 1)

            steps(dve, NM, LAST, body)


def dve_products(nc, dve, i, psW, msg, msg0, prod, dot, F, r, S, ready, free):
    tt = nc.vector.tensor_tensor
    v, v0 = comp(msg[:, :, C0:CX]), comp(msg0[:, :, C0:CX])
    dve.wait_ge(*ready)
    tt(comp(prod[:, :, :]), v, r, ALU.mult).then_inc(S.sem("prod"), 1)
    dve.wait_ge(S.sem("prod"), i + 1)
    nc.vector.tensor_reduce(dot[:, :, :], prod[:, :, :].rearrange("p t (d c) -> p t c d", d=3), AX.X, ALU.add)\
        .then_inc(S.sem("dot"), 1)
    dve.wait_ge(S.sem("weights"), i + 1)
    wait(dve, *free)
    tt(F[:, :, F_A:F_A + C0], psW[:, :, 0:64], msg0[:, :, 0:C0], ALU.mult)
    tt(F[:, :, F_B:F_B + C0], psW[:, :, 64:128], msg[:, :, 0:C0], ALU.mult)
    tt(comp(F[:, :, F_C:F_C + C1V]), bcast(psW[:, :, 128:160], 2, 3), v0, ALU.mult)
    tt(comp(F[:, :, F_X:F_X + C1V]), bcast(psW[:, :, 192:224], 2, 3), v, ALU.mult)
    dve.wait_ge(S.sem("dot"), i + 1)
    tt(F[:, :, F_D:F_D + C1], psW[:, :, 160:192], dot[:, :, :], ALU.mult).then_inc(S.sem("products"), 1)



def softmax_weights(nc, W, D, logits, probs, H, tag):
    with ExitStack() as ctx:
        S = Names(nc, ctx, tag)
        dst, gap = S.sb("dst", [P, ET], I32), S.sb("gap", [P, ET + 1])
        ends = S.sb("ends", [H, 2, P], I32)
        link = S.sb("link", [H, P + 1])
        thru = S.sb("thru", [H, P + 1])
        one = S.sb("one", [H, P])
        edge, edgeT = S.sb("edge", [P, H]), S.sb("edgeT", [H, P])
        run, carryT = S.sb("run", [H, P]), S.sb("carryT", [H, P])
        carry = S.sb("carry", [P, H])
        best = S.sb("best", [P, ET, H])
        psC, psR = S.ps("psC", [P, 512]), S.ps("psR", [P, 512])
        sem = S.sem
        block = ctx.enter_context(nc.Block())

        @block.sync
        def _(sp):
            sp.dma_start(dst[:, :], D["dst"]).then_inc(sem("dst"), 16)
            sp.dma_start(ends[:, 0, :], D["dst_t"][0, :].partition_broadcast(H)).then_inc(sem("ends"), 16)
            sp.dma_start(ends[:, 1, :], D["dst_t"][ET - 1, :].partition_broadcast(H)).then_inc(sem("ends"), 16)

        @block.tensor
        def _(pe):
            for n in range(2):
                pe.wait_ge(sem("edge"), n + 1)
                nc.tensor.transpose(psR[0:H, 0:P], edge[:, :], W["ident"][:, :]).then_inc(sem("edge_T"), 1)
                pe.wait_ge(sem("carry_T"), n + 1)
                nc.tensor.transpose(psC[:, 0:H], carryT[:, :], W["ident"][0:H, 0:H]).then_inc(sem("carry_ps"), 1)

        @block.scalar
        def _(act):
            act.wait_ge(sem("shifted"), 1)
            nc.scalar.activation(probs[:, :, :], probs[:, :, :], ACT.Exp).then_inc(sem("probs"), 1)

        @block.vector
        def _(dve):
            n = 0

            def then(ins):
                nonlocal n
                n += 1
                ins.then_inc(sem("order"), 1)
                dve.wait_ge(sem("order"), n)

            tt, ts = nc.vector.tensor_tensor, nc.vector.tensor_scalar
            scan = nc.vector.tensor_tensor_scan
            dve.wait_ge(sem("dst"), 16)
            dve.wait_ge(sem("ends"), 32)
            nc.vector.memset(link[:, :], NBIG)
            nc.vector.memset(thru[:, :], NBIG)
            then(nc.vector.memset(gap[:, :], NBIG))
            then(tt(gap[:, 1:ET], dst[:, 1:ET], dst[:, 0:ET - 1], ALU.not_equal))
            ts(gap[:, 1:ET], gap[:, 1:ET], NBIG, None, ALU.mult)
            then(tt(link[:, 1:P], ends[:, 0, 1:P], ends[:, 1, 0:P - 1], ALU.not_equal))
            then(tt(one[:, :], ends[:, 0, :], ends[:, 1, :], ALU.not_equal))

            def across(backward):
                a = slice(0, P) if not backward else slice(1, P + 1)
                then(tt(thru[:, 0:P], one[:, :], link[:, a], ALU.add))
                then(ts(thru[:, 0:P], thru[:, 0:P], 1.0, NBIG, ALU.min, ALU.mult))
                r = slice(None, None, -1) if backward else slice(None)
                then(scan(run[:, r], thru[:, 0:P][:, r], edgeT[:, r], NBIG, ALU.add, ALU.max))
                then(nc.vector.memset(carryT[:, :], NBIG))
                if backward:
                    then(ts(carryT[:, 0:P - 1], link[:, 1:P], NBIG, None, ALU.mult))
                    tt(carryT[:, 0:P - 1], carryT[:, 0:P - 1], run[:, 1:P], ALU.add).then_inc(sem("carry_T"), 1)
                else:
                    then(ts(carryT[:, 1:P], link[:, 1:P], NBIG, None, ALU.mult))
                    tt(carryT[:, 1:P], carryT[:, 1:P], run[:, 0:P - 1], ALU.add).then_inc(sem("carry_T"), 1)

            nc.vector.memset(link[:, 0:1], 1.0)
            then(nc.vector.memset(link[:, P:P + 1], 1.0))
            for backward in (False, True):
                src = best if backward else logits
                r = slice(None, None, -1) if backward else slice(None)
                g = gap[:, 1:ET + 1][:, r] if backward else gap[:, 0:ET]
                for h in range(H):
                    last = scan(probs[:, r, h], g, src[:, r, h], NBIG, ALU.add, ALU.max)
                then(last)
                end = 0 if backward else ET - 1
                then(nc.vector.tensor_copy(edge[:, :], probs[:, end, :]))
                dve.sem_inc(sem("edge"), 1)
                dve.wait_ge(sem("edge_T"), 1 + backward)
                then(nc.vector.tensor_copy(edgeT[:, :], psR[0:H, 0:P]))
                across(backward)
                dve.wait_ge(sem("carry_ps"), 1 + backward)
                then(nc.vector.tensor_copy(carry[:, :], psC[:, 0:H]))
                then(nc.vector.memset(gap[:, ET:ET + 1] if backward else gap[:, 0:1], 0.0))
                out = probs if backward else best
                for h in range(H):
                    last = scan(out[:, r, h], g, src[:, r, h], carry[:, h:h + 1], ALU.add, ALU.max)
                then(last)
            tt(probs[:, :, :], logits[:, :, :], probs[:, :, :], ALU.subtract).then_inc(sem("shifted"), 1)



def attention_sums(nc, W, D, probs, layer, H, tag, clear_layers=()):
    HS, HV = C0 // H, C1 // H
    width = CX + H
    acc = D["acc"][layer]
    with ExitStack() as ctx:
        S = Names(nc, ctx, tag)
        T = scatter_tensors(S, width)
        val = [S.sb(f"val{u}", [P, TM, CX]) for u in range(2)]
        wv = [S.sb(f"wv{u}", [P, TM, width]) for u in range(2)]
        pb = [S.sb(f"pb{u}", [P, TM, H]) for u in range(2)]
        psS = S.ps("psS", [P, 4, 512])
        banks = [psS[:, k, 0:width] for k in range(4)]
        sem = S.sem
        LAST = 2
        block = ctx.enter_context(nc.Block())

        @block.sync
        def _(sp):
            def body(i_of):
                if m := i_of(0):
                    i, u, j = m
                    wait_apart(sp, sem("weighted"), i - 1, S.sem("sp_passed"))
                    sp.dma_start(val[u][:, :, :], D["val"][:, bass.ds(i * TM, TM), :]).then_inc(sem(f"val{u}"), 16)
                    sp_keys(sp, i, u, j, T, D, "dst", S)

            steps(sp, NM, LAST, body)

        @block.vector
        def _(dve):
            tt = nc.vector.tensor_tensor

            def body(i_of):
                if m := i_of(1):
                    i, u, j = m
                    wait(dve, sem("weighted"), i - 1)
                    nc.vector.tensor_copy(pb[u][:, :, :], probs[:, bass.ds(i * TM, TM), :]).then_inc(sem("pb"), 1)
                    dve_rows(nc, dve, i, u, j, T, W, S)
                    dve.wait_ge(sem(f"val{u}"), (j + 1) * 16)
                    dve.wait_ge(sem("pb"), i + 1)
                    wait(dve, sem("summed"), (i - 1) * TM)
                    tt(wv[u][:, :, 0:C0].rearrange("p t (h c) -> p t h c", h=H), val[u][:, :, 0:C0].rearrange("p t (h c) -> p t h c", h=H),
                       bcast(pb[u][:, :, :], 3, HS), ALU.mult)
                    for d in range(3):
                        a = C0 + C1 * d
                        tt(wv[u][:, :, a:a + C1].rearrange("p t (h c) -> p t h c", h=H),
                           val[u][:, :, a:a + C1].rearrange("p t (h c) -> p t h c", h=H), bcast(pb[u][:, :, :], 3, HV), ALU.mult)
                    nc.vector.tensor_copy(wv[u][:, :, CX:width], pb[u][:, :, :]).then_inc(sem("weighted"), 1)

            steps(dve, NM, LAST, body)

        @block.tensor
        def _(pe):
            def body(i_of):
                if m := i_of(1):
                    i, u, j = m
                    pe_sums(nc, pe, i, u, T, wv[u], banks, S, (sem("weighted"), i + 1))

            steps(pe, NM, LAST, body)

        @block.scalar
        def _(act):
            n = 0
            for later in clear_layers:
                for k in range(TM):
                    n += clear(act, W["zeros"], D["acc"][later][k], ACC_W[later], sem("clear"))

            def body(i_of):
                if m := i_of(1):
                    act_sums(nc, act, *m, T, banks, S)

            steps(act, NM, LAST, body)
            if n:
                act.wait_ge(sem("clear"), 16 * n)

        @block.gpsimd
        def _(pool):
            def body(i_of):
                if m := i_of(2):
                    pool_scatter(nc, pool, *m, T, acc, S)

            steps(pool, NM, LAST, body)
            for k in range(TM):
                pool.wait_ge(sem(f"added{k}"), 16 * NM)



def convolution_edges(nc, W, D, layer, gather_by, sum_by, tag):
    cross = layer == 1
    kin, wn = (64, 224) if cross else (8, 192)
    per = 128 if cross else 96
    width = 96 + 3 * per
    acc = D["acc"][layer]
    with ExitStack() as ctx:
        S = Names(nc, ctx, tag)
        if cross:
            dirs, sp_dirs, pool_dirs, dve_dirs = load_directions(nc, S, D, 0.0)
            Y = lambda i, a, b: dirs_of(dirs, i, a, b)
        else:
            y = S.sb("y", [P, ET, 4])
            Y = lambda i, a, b: bcast(y[:, bass.ds(i * TM, TM), 1 + a:1 + b], 3, C1)
        T = scatter_tensors(S, width)
        es = [S.sb(f"es{u}", [kin, ME]) for u in range(2)]
        ix = [S.sb(f"ix{u}", [P, 1, TM], I32) for u in range(2)]
        g = [S.sb(f"g{u}", [P, TM, CX]) for u in range(2)]
        g0 = S.sb("feat_y0", [P, TM, CX])
        h = [S.sb(f"h{u}", [64, ME]) for u in range(2)]
        prod, dot, bs = S.sb("prod", [P, TM, C1V]), S.sb("dot", [P, TM, C1]), S.sb("bs", [P, TM, C0])
        xw, tmp = S.sb("xw", [P, TM, C1V]), S.sb("tmp", [P, TM, C1V])
        rows = [S.sb(f"rows{u}", [P, TM, width]) for u in range(2)]
        psH, psS = S.ps("psH", [64, 512]), S.ps("psS", [P, 2, 512])
        psWs = [S.ps(f"psW{u}", [P, TM, 256]) for u in range(2)]
        banks = [psS[:, k, 0:width] for k in range(2)]
        sem = S.sem
        LAST = 3
        source = D["es64"] if cross else D["es8"]
        block = ctx.enter_context(nc.Block())

        @block.sync
        def _(sp):
            if cross:
                sp_dirs(sp)
            else:
                sp.dma_start(y[:, :, :], D["edge_attr_4"].rearrange("p (t c) -> p t c", c=4)).then_inc(sem("y"), 16)

            def body(i_of):
                if m := i_of(0):
                    i, u, j = m
                    wait_apart(sp, sem("pre"), i - 1, S.sem("sp_passed"))
                    sp.dma_start(es[u][:, :], source[0:kin, bass.ds(i * ME, ME)]).then_inc(sem(f"es{u}"), 16)
                    sp_indices(sp, i, u, j, ix, D, (gather_by,), S, [sem("gathered0"), sem("gathered1")])
                    sp_keys(sp, *m, T, D, sum_by, S)

            steps(sp, NM, LAST, body)

        @block.gpsimd
        def _(pool):
            if cross:
                pool_dirs(pool)

            def body(i_of):
                if m := i_of(LAST):
                    pool_scatter(nc, pool, *m, T, acc, S)
                if m := i_of(0):
                    pool_gather(nc, pool, *m, ix, (D["tab_src"],), (g,), S, (sem("products"), m[0] - 1))

            steps(pool, NM, LAST, body)
            for k in range(TM):
                pool.wait_ge(sem(f"added{k}"), 16 * NM)

        @block.tensor
        def _(pe):
            passed = sem("pe_passed")

            def body(i_of):
                if m := i_of(0):
                    i, u, j = m
                    wait_apart(pe, sem(f"es{u}"), (j + 1) * 16, passed)
                    wait_apart(pe, sem("h"), i, passed)
                    nc.tensor.matmul(psH[:, :], W[f"l{layer}_fc1"][:, :], es[u][:, :], start=True, stop=True).then_inc(sem("pre"), 1)
                if m := i_of(2):
                    i, u, j = m
                    pe_sums(nc, pe, i, u, T, rows[u], banks, S, (sem("products"), i + 1))
                if m := i_of(0):
                    i, u, j = m
                    wait_apart(pe, sem("h"), i + 1, passed)
                    wait_apart(pe, sem("products"), i - 1, passed)
                    for k in range(TM):
                        last = nc.tensor.matmul(psWs[u][:, k, 0:wn], h[u][:, P * k:P * k + P], W[f"l{layer}_fc2"][:, :], start=True, stop=True)
                    last.then_inc(sem("weights"), 1)

            steps(pe, NM, LAST, body)

        @block.scalar
        def _(act):
            if not cross:
                act.wait_ge(sem("y"), 16)

            def body(i_of):
                if m := i_of(0):
                    i, u, j = m
                    act.wait_ge(sem("pre"), i + 1)
                    wait(act, sem("weights"), i - 1)
                    nc.scalar.activation(h[u][:, :], psH[:, :], ACT.Relu if cross else ACT.Silu,
                                         scale=1.0 if cross else 1.0 / float(np.sqrt(8.0))).then_inc(sem("h"), 1)
                if m := i_of(2):
                    act_sums(nc, act, *m, T, banks, S)

            steps(act, NM, LAST, body)

        @block.vector
        def _(dve):
            if cross:
                dve_dirs(dve)
            else:
                dve.wait_ge(sem("y"), 16)
            tt = nc.vector.tensor_tensor

            def body(i_of):
                if m := i_of(1):
                    i, u, j = m
                    psW = psWs[u]
                    dve.wait_ge(sem(f"gathered{u}"), (j + 1) * 16 * TM)
                    wait(dve, sem("products"), i)
                    R = rows[u]
                    s, v = g[u][:, :, 0:C0], comp(g[u][:, :, C0:CX])
                    D3 = R[:, :, 96:width].rearrange("p t (d c) -> p t d c", d=3)
                    if cross:
                        s0, v0 = s, v
                    else:
                        y0 = y[:, bass.ds(i * TM, TM), 0:1].rearrange("p t c -> p (t c)")
                        tt(g0[:, :, :], g[u][:, :, :], bcast(y0, 2, CX), ALU.mult).then_inc(sem("g0"), 1)
                        s0, v0 = g0[:, :, 0:C0], comp(g0[:, :, C0:CX])
                    tt(comp(prod[:, :, :]), v, Y(i, 0, 3), ALU.mult).then_inc(sem("prod"), 1)
                    dve.wait_ge(sem("weights"), i + 1)
                    tt(bs[:, :, :], psW[:, :, 64:128], s, ALU.mult)
                    if cross:
                        tt(comp(xw[:, :, :]), bcast(psW[:, :, 192:224], 2, 3), v, ALU.mult)
                    dve.wait_ge(sem("prod"), i + 1)
                    nc.vector.tensor_reduce(dot[:, :, :], prod[:, :, :].rearrange("p t (d c) -> p t c d", d=3), AX.X, ALU.add)\
                        .then_inc(sem("dot"), 1)
                    wait(dve, sem("summed"), (i - 1) * TM)
                    if not cross:
                        dve.wait_ge(sem("g0"), i + 1)
                    tt(R[:, :, 0:C0], psW[:, :, 0:64], s0, ALU.mult)
                    tt(D3[:, :, :, 64:96], bcast(psW[:, :, 128:160], 2, 3), v0, ALU.mult)
                    dve.wait_ge(sem("dot"), i + 1)
                    tt(R[:, :, C0:96], psW[:, :, 160:192], dot[:, :, :], ALU.mult)
                    for half in range(2):
                        c = slice(C1 * half, C1 * half + C1)
                        last = tt(D3[:, :, :, c], bcast(bs[:, :, c], 2, 3), Y(i, 0, 3), ALU.mult)
                    if cross:
                        X = lambda a, b: comp(xw[:, :, C1 * a:C1 * b], b - a)
                        Z = lambda a, b: comp(tmp[:, :, C1 * a:C1 * b], b - a)
                        tt(D3[:, :, 0:2, 96:128], X(1, 3), Y(i, 2, 4), ALU.mult)
                        tt(D3[:, :, 2:3, 96:128], X(0, 1), Y(i, 4, 5), ALU.mult)
                        tt(Z(0, 1), X(2, 3), Y(i, 1, 2), ALU.mult)
                        tt(Z(1, 3), X(0, 2), Y(i, 2, 4), ALU.mult).then_inc(sem("crossed"), 1)
                        dve.wait_ge(sem("crossed"), i + 1)
                        last = tt(D3[:, :, :, 96:128], D3[:, :, :, 96:128], comp(tmp[:, :, :]), ALU.subtract)
                    last.then_inc(sem("products"), 1)
                    dve_rows(nc, dve, i, u, j, T, W, S)

            steps(dve, NM, LAST, body)



def layer2_edges(nc, W, D, logits):
    with ExitStack() as ctx:
        S = Names(nc, ctx, "e2")
        y, dirs = S.sb("y", [P, ET, 4]), S.sb("dirs", [P, ET, 5])
        es = [S.sb(f"es{u}", [16, ME]) for u in range(2)]
        ix = [S.sb(f"ix{u}", [P, 2, TM], I32) for u in range(2)]
        gs, gd = ([S.sb(f"{n}{u}", [P, TM, CX]) for u in range(2)] for n in ("gs", "gd"))
        msg, msg0 = S.sb("msg", [P, TM, CX]), S.sb("msg0", [P, TM, CX])
        prod, dot = S.sb("prod", [P, TM, C1V]), S.sb("dot", [P, TM, C1])
        F, F2 = S.sb("F", [P, TM, F_W]), S.sb("F2", [P, TM, F_W])
        FT, FT2, tmp = S.sb("FT", [P, 2, F_W]), S.sb("FT2", [P, 2, F_W]), S.sb("tmp", [P, 3, TM, C1V])
        O_W, O2_W = 352, 288
        O = [S.sb(f"O{u}", [P, TM, O_W]) for u in range(2)]
        O2 = [S.sb(f"O2{u}", [P, TM, O2_W]) for u in range(2)]
        lk, valT, gate = S.sb("lk", [P, TM, 64]), S.sb("valT", [64, ME]), S.sb("gate", [P, TM, C1])
        psW, psF, psO = S.ps("psW", [P, TM, 256]), S.ps("psF", [P, 2, 512]), S.ps("psO", [P, 2, 512])
        psV, psG = S.ps("psV", [64, 512]), S.ps("psG", [P, 512])
        sem = S.sem
        SECOND, LAST = 3, 5
        block = ctx.enter_context(nc.Block())

        @block.sync
        def _(sp):
            sp.dma_start(y[:, :, :], D["edge_attr_4"].rearrange("p (t c) -> p t c", c=4)).then_inc(sem("y"), 16)

            def body(i_of):
                if m := i_of(0):
                    i, u, j = m
                    wait_apart(sp, sem("weights"), i - 1, S.sem("sp_passed"))
                    sp.dma_start(es[u][:, :], D["es16"][:, bass.ds(i * ME, ME)]).then_inc(sem(f"es{u}"), 16)
                    sp_indices(sp, i, u, j, ix, D, ("src", "dst"), S, [sem("gathered0"), sem("gathered1")])
                if m := i_of(LAST):
                    i, u, j = m
                    wait_apart(sp, sem("cross2_done"), i + 1, sem("sp_passed"))
                    sp.dma_start(D["val"][:, bass.ds(i * TM, TM), :], O2[u][:, :, 0:CX]).then_inc(sem(f"stored{u}"), 16)

            steps(sp, NM, LAST, body)
            for u in range(2):
                sp.wait_ge(sem(f"stored{u}"), 16 * (NM // 2))

        @block.gpsimd
        def _(pool):
            def body(i_of):
                if m := i_of(0):
                    pool_gather(nc, pool, *m, ix, (D["tab_src"], D["tab_dst"]), (gs, gd), S, (sem("msg"), m[0] - 1))

            steps(pool, NM, LAST, body)

        @block.scalar
        def _(act):
            def body(i_of):
                if m := i_of(2):
                    i, u, j = m
                    wait(act, sem("gated"), i - 1)
                    wait(act, sem("sig"), i - 1)
                    act_linear(nc, act, i, FT, psF, O[u], psO, O_W, S, "lin")
                    act.wait_ge(sem("val_T"), i + 1)
                    wait(act, sem("gate_in"), i)
                    nc.scalar.activation(valT[:, :], psV[:, :], ACT.Copy).then_inc(sem("valT"), 1)
                    act.wait_ge(sem("gate_in"), i + 1)
                    wait(act, sem("gated"), i)
                    nc.scalar.activation(gate[:, :, :], psG[:, 0:P].rearrange("p (t c) -> p t c", t=TM), ACT.Sigmoid).then_inc(sem("gate"), 1)
                if m := i_of(SECOND):
                    i, u, j = m
                    wait(act, sem(f"stored{u}"), j * 16)
                    act_linear(nc, act, i, FT2, psF, O2[u], psO, O2_W, S, "lin2")
                if m := i_of(2):
                    i, u, j = m
                    wait(act, sem("lin2_turned"), i * TM)
                    nc.scalar.activation(F2[:, :, F_B:F_B + C0], O[u][:, :, 64:128], ACT.Sigmoid).then_inc(sem("sig"), 1)

            steps(act, NM, LAST, body)

        @block.tensor
        def _(pe):
            passed = sem("pe_passed")

            def body(i_of):
                if m := i_of(2):
                    i, u, j = m
                    wait_apart(pe, sem("products"), i + 1, passed)
                    first = lambda own, other: (lambda k: (sem(own), i * TM + k - 1) if k > 1 else (sem(other), (i - 1) * TM))
                    pe_linear(nc, pe, i, F, FT, psF, psO, W, "l2", 128, W["ident"], S, "lin",
                              first("lin_FT", "lin2_FT"), first("lin_O", "lin2_O"))
                    wait_apart(pe, sem("lin_O"), (i + 1) * TM, passed)
                    wait_apart(pe, sem("valT"), i, passed)
                    for k in range(TM):
                        last = nc.tensor.transpose(psV[:, P * k:P * k + P], O[u][:, k, 64:128], W["ident"][:, :])
                    last.then_inc(sem("val_T"), 1)
                    wait_apart(pe, sem("valT"), i + 1, passed)
                    wait_apart(pe, sem("gate"), i, passed)
                    for k in range(TM):
                        last = nc.tensor.matmul(psG[:, C1 * k:C1 * k + C1], valT[:, P * k:P * k + P], W["l2_wg"][:, :], start=True, stop=True)
                    last.then_inc(sem("gate_in"), 1)
                if m := i_of(1):
                    i, u, j = m
                    wait_apart(pe, sem(f"es{u}"), (j + 1) * 16, passed)
                    wait_apart(pe, sem("products"), i, passed)
                    for k in range(TM):
                        last = nc.tensor.matmul(psW[:, k, 0:224], es[u][:, P * k:P * k + P], W["l2_rbf"][:, :], start=True, stop=True)
                    last.then_inc(sem("weights"), 1)
                if m := i_of(SECOND):
                    i, u, j = m
                    wait_apart(pe, sem("products2"), i + 1, passed)
                    second = lambda own, other: (lambda k: (sem(own), i * TM + k - 1) if k > 1 else (sem(other), last_first(i)))
                    last_first = lambda i: min(i + 2, NM) * TM if isinstance(i, int) else (i + 2) * TM
                    pe_linear(nc, pe, i, F2, FT2, psF, psO, W, "l2b", 64, W["ident"], S, "lin2",
                              second("lin2_FT", "lin_FT"), second("lin2_O", "lin_O"))

            pe.wait_ge(sem("padded"), 2)
            steps(pe, NM, LAST, body)

        @block.vector
        def _(dve):
            tt = nc.vector.tensor_tensor
            nc.vector.memset(F[:, :, 352:F_W], 0.0).then_inc(sem("padded"), 1)
            nc.vector.memset(F2[:, :, 352:F_W], 0.0).then_inc(sem("padded"), 1)
            dve.wait_ge(sem("y"), 16)
            nc.vector.tensor_copy(dirs[:, :, 0:3], y[:, :, 1:4]).then_inc(sem("dirs"), 1)
            nc.vector.tensor_copy(dirs[:, :, 3:5], y[:, :, 1:3]).then_inc(sem("dirs"), 1)
            dve.wait_ge(sem("dirs"), 2)

            def y0_of(i, n):
                return bcast(y[:, bass.ds(i * TM, TM), 0:1].rearrange("p t c -> p (t c)"), 2, n)

            def body(i_of):
                if m := i_of(1):
                    i, u, j = m
                    dve.wait_ge(sem(f"gathered{u}"), (j + 1) * 16 * 2 * TM)
                    wait(dve, sem("products"), i)
                    tt(msg[:, :, :], gs[u][:, :, :], gd[u][:, :, :], ALU.add).then_inc(sem("msg"), 1)
                    dve.wait_ge(sem("msg"), i + 1)
                    tt(msg0[:, :, :], msg[:, :, :], y0_of(i, CX), ALU.mult).then_inc(sem("msg0"), 1)
                if m := i_of(3):
                    i, u, j = m
                    dve.wait_ge(sem("lin_O"), (i + 1) * TM)
                    wait(dve, sem("logit"), i)
                    a = O[u][:, :, 0:64]
                    nc.vector.scalar_tensor_tensor(out=lk[:, :, :], in0=a, scalar=0.2, in1=a, op0=ALU.mult, op1=ALU.max)\
                        .then_inc(sem("leaky"), 1)
                    wait(dve, sem("cross2_done"), i - 1)
                    dve_cross(nc, dve, i, O[u], tmp, dirs, 128, 224, 320, S, "cross")
                    dve.wait_ge(sem("leaky"), 2 * i + 1)
                    tt(lk[:, :, :], lk[:, :, :], bcast(W["l2_adot"][:, :], 1, TM), ALU.mult).then_inc(sem("leaky"), 1)
                    dve.wait_ge(sem("cross_done"), i + 1)
                    dve.wait_ge(sem("gate"), i + 1)
                    wait(dve, sem("lin2_turned"), i * TM)
                    V2 = comp(F2[:, :, F_X:F_X + C1V])
                    tt(V2, comp(O[u][:, :, 128:224]), bcast(gate[:, :, :], 2, 3), ALU.mult).then_inc(sem("gated"), 1)
                    dve.wait_ge(sem("leaky"), 2 * i + 2)
                    dve.sem_inc(sem("dve_passed"), 1)
                    nc.vector.tensor_reduce(logits[:, bass.ds(i * TM, TM), :], lk[:, :, :].rearrange("p t (h a) -> p t h a", a=16),
                                            AX.X, ALU.add).then_inc(sem("logit"), 1)
                    dve.wait_ge(sem("gated"), i + 1)
                    dve.wait_ge(sem("sig"), i + 1)
                    wait(dve, sem("dot"), i + 2 if not isinstance(i, int) else min(i + 2, NM))
                    tt(comp(prod[:, :, :]), V2, dirs_of(dirs, i, 0, 3), ALU.mult).then_inc(sem("prod2"), 1)
                    tt(F2[:, :, F_A:F_A + C0], F2[:, :, F_B:F_B + C0], y0_of(i, C0), ALU.mult)
                    tt(F2[:, :, F_C:F_C + C1V], F2[:, :, F_X:F_X + C1V], y0_of(i, C1V), ALU.mult)
                    dve.wait_ge(sem("prod2"), i + 1)
                    nc.vector.tensor_reduce(F2[:, :, F_D:F_D + C1], prod[:, :, :].rearrange("p t (d c) -> p t c d", d=3), AX.X,
                                            ALU.add).then_inc(sem("products2"), 1)
                if m := i_of(1):
                    i, u, j = m
                    dve.wait_ge(sem("msg0"), i + 1)
                    wait(dve, sem("products2"), i - 1)
                    dve_products(nc, dve, i, psW, msg, msg0, prod, dot, F, dirs_of(dirs, i, 0, 3), S,
                                 (sem("msg"), i + 1), (sem("lin_turned"), i * TM))
                if m := i_of(4):
                    i, u, j = m
                    dve.wait_ge(sem("lin2_O"), (i + 1) * TM)
                    wait(dve, sem("cross_done"), i + 2 if not isinstance(i, int) else min(i + 2, NM))
                    dve_cross(nc, dve, i, O2[u], tmp, dirs, 64, 160, 256, S, "cross2")

            steps(dve, NM, LAST, body)



def node_phase(nc, W, D, post, pre):
    PI = float(np.pi)
    stages = []

    def stats(tag):
        stages.extend(tag + n for n in ("mean", "scale_mean", "centre", "square", "sum", "var", "root", "norm"))

    if post is not None:
        stages += ["pair", "sum"]
        if post in (0, 2):
            stages += ["denom", "recip", "ratio", "share"] if post == 0 else ["denom", "recip", "share"]
        if post == 0:
            stages += ["bias", "merged"]
        if post in (1, 3):
            stages += ["turn_s", "move_s", "turn_v", "move_v", "turn_x", "move_x", "product", "product_v"]
        else:
            stages += ["turn_a", "move_a", "product"]
        if post == 0:
            stages += ["residual"]
            stats("ln2_")
            stages += ["turn_n", "move_n", "f1", "attr", "scalars", "gate_t", "gate_v", "gated", "turn_f", "move_f", "f2", "f2_bias",
                       "f2_attr", "both", "whole"]
        if post == 1:
            stages += ["silu", "gate_t", "gate_half", "gated", "whole"]
        if post == 2:
            stages += ["twice", "whole"]
        if post == 3:
            stages += ["angle", "attr", "turns", "turns_i", "turns_f", "reduce", "shift", "shift_gt", "shift_in", "sine", "skip_attr",
                       "conv_attr", "mix_a", "mix_b", "mix_c", "whole"]
        stats("end_")
    if pre is not None:
        if pre in (0, 2):
            stats("pre_")
        stages += ["turn_p", "move_p", "tables", "move_t"]
        if pre == 3:
            stages += ["tab_attr"]
    L = len(stages)
    index = {n: k for k, n in enumerate(stages)}

    with ExitStack() as ctx:
        S = Names(nc, ctx, f"n{post}{pre}".replace("None", "x"))
        sem = S.sem
        done = sem("done")
        aw = ACC_W[post] if post is not None else 1
        ag = [S.sb(f"ag{k}", [P, G, aw]) for k in range(TM)]
        cen, sqr, nrm = S.sb("cen", [P, G, CX]), S.sb("sqr", [P, G, CX]), S.sb("nrm", [P, G, CX])
        res, out = S.sb("res", [P, G, CX]), S.sb("out", [P, G, CX])
        st, attr = S.sb("st", [P, 2, G]), S.sb("attr", [P, 2, G])
        sT, vT = S.sb("sT", [65, G * P]), S.sb("vT", [96, G * P])
        psA, psB = S.ps("psA", [P, 2048]), S.ps("psB", [P, 2048])
        wideA, wideB = (t[:, 0:G * 256].rearrange("p (t c) -> p t c", t=G) for t in (psA, psB))
        X = lambda g: W["x"][:, bass.ds(g * G, G), :]
        NA = lambda g: W["na"][:, bass.ds(g * G, G)]
        if post in (0, 2):
            H = ACC_W[post] - CX
            HS, HV = C0 // H, C1 // H
            den, ratio = S.sb("den", [P, G, H]), S.sb("ratio", [P, G, H])
        if post == 0:
            th, fv = S.sb("th", [P, G, 64]), S.sb("fv", [P, G, 192])
            sc, scT = S.sb("sc", [P, G, P]), S.sb("scT", [P, G * P])
            fvTa, fvTb = S.sb("fvTa", [P, G * P]), S.sb("fvTb", [64, G * P])
        if post == 1:
            th = S.sb("th", [P, G, C1])
            gT = [S.sb(f"gT{d}", [P, G * P]) for d in range(3)]
            aT = S.sb("aT", [96, G * P])
        if post == 3:
            gT = [S.sb(f"gT{d}", [96, G * P]) for d in range(3)]
            aT = S.sb("aT", [96, G * P])
            ang, whole_t = S.sb("ang", [P, 2, G]), S.sb("whole_t", [P, 2, G])
            turns_i = S.sb("turns_i", [P, 2, G], I32)
            skip = S.sb("skip", [P, G, CX])
        if pre is not None:
            n_tab = 2 if pre in (0, 2) else 1
            tab = S.sb("tab", [P, n_tab, G, CX])
        else:
            final = S.sb("final", [P, G, CX])
        block = ctx.enter_context(nc.Block())

        def at(eng, name, g):
            eng.wait_ge(done, g * L + index[name])

        @block.sync
        def _(sp):
            if post is not None:
                def load(g):
                    for k in range(TM):
                        sp.dma_start(ag[k][:, :, :], D["acc"][post][k][0:NPAD, :].rearrange("(p t) c -> p t c", p=P)[:, bass.ds(g * G, G), :])\
                            .then_inc(sem("loaded"), 16)

                load(0)

            def store(g):
                if pre is not None:
                    for n, name in enumerate(("tab_src", "tab_dst")[0:n_tab]):
                        sp.dma_start(D[name].rearrange("(p t) c -> p t c", p=P)[:, bass.ds(g * G, G), :], tab[:, n, :, :]).then_inc(sem("stored"), 16)
                else:
                    sp.dma_start(D["out"].rearrange("(p t) c -> p t c", p=P)[:, bass.ds(g * G, G), :], final[:, :, :]).then_inc(sem("stored"), 16)

            with sp.Fori(1, NG) as g:
                wait_apart(sp, done, g * L, sem("sp_passed"))
                if post is not None:
                    load(g)
                store(g - 1)
            sp.wait_ge(done, NG * L)
            store(NG - 1)
            sp.wait_ge(sem("stored"), 16 * NG * (n_tab if pre is not None else 1))

        @block.gpsimd
        def _(pool):
            with pool.Fori(0, NG) as g:
                for tag in ("ln2_", "end_", "pre_"):
                    if tag + "root" in index:
                        at(pool, tag + "root", g)
                        nc.gpsimd.tensor_tensor(st[:, :, :], st[:, :, :], W["half"][:, 0:2 * G].rearrange("p (a t) -> p a t", a=2), ALU.pow)\
                            .then_inc(done, 1)

        @block.tensor
        def _(pe):
            ident = W["ident"]

            def turn(src, a, b, to, base=0):
                for t in range(G):
                    last = nc.tensor.transpose(to[0:b - a, base + P * t:base + P * t + P], src[:, t, a:b], ident[:, :])
                return last

            def times(to, a, *pairs):
                for t in range(G):
                    for n, (f, w) in enumerate(pairs):
                        last = nc.tensor.matmul(to[:, t, a:a + w.shape[1]], f[:, P * t:P * t + P], w, start=(n == 0), stop=(n == len(pairs) - 1),
                                                skip_group_check=True)
                return last

            def at(eng, name, g):
                wait_apart(eng, done, g * L + index[name], sem("pe_passed"))

            pe.wait_ge(sem("ones"), 1)
            with pe.Fori(0, NG) as g:
                if post in (0, 2):
                    at(pe, "turn_a", g)
                    turn(nrm, 0, C0, psA)
                    turn(nrm, C0, CX, psA, 1024).then_inc(done, 1)
                    at(pe, "product", g)
                    if post == 0:
                        times(wideB, 0, (sT[:, :], W["l0_proj_s"][:, :]))
                    else:
                        times(wideB, 0, (sT[0:64, :], W["l2_proj_s"][:, :]))
                    times(wideB, C0, (vT[:, :], W[f"l{post}_proj_v"][:, :])).then_inc(done, 1)
                if post == 0:
                    at(pe, "turn_n", g)
                    turn(nrm, 0, C0, psA)
                    turn(nrm, C0, CX, psA, 1024).then_inc(done, 1)
                    at(pe, "f1", g)
                    times(wideB, 0, (sT[:, :], W["l0_f1_s"][:, :]))
                    times(wideA, 0, (vT[:, :], W["l0_f1_v"][:, :])).then_inc(done, 1)
                    at(pe, "turn_f", g)
                    turn(sc, 0, P, psA)
                    turn(fv, 0, P, psA, 1024)
                    turn(fv, P, 192, psB).then_inc(done, 1)
                    at(pe, "f2", g)
                    times(wideB, 0, (scT[:, :], W["l0_f2_s"][:, :]))
                    times(wideB, C0, (fvTa[:, :], W["l0_f2_va"][:, :]), (fvTb[:, :], W["l0_f2_vb"][:, :])).then_inc(done, 1)
                if post in (1, 3):
                    per = 128 if post == 1 else 96
                    at(pe, "turn_s", g)
                    turn(ag[0], 0, 96, psA)
                    turn(ag[0], 96, 96 + per, psA, 1024).then_inc(done, 1)
                    at(pe, "turn_v", g)
                    turn(ag[0], 96 + per, 96 + 2 * per, psA)
                    turn(ag[0], 96 + 2 * per, 96 + 3 * per, psA, 1024).then_inc(done, 1)
                    at(pe, "turn_x", g)
                    for t in range(G):
                        nc.tensor.transpose(psA[0:64, P * t:P * t + P], res[:, t, 0:C0], ident[:, :])
                        last = nc.tensor.transpose(psA[0:96, 1024 + P * t:1024 + P * t + P], res[:, t, C0:CX], ident[:, :])
                    last.then_inc(done, 1)
                    if post == 1:
                        at(pe, "product", g)
                        times(wideB, 0, (aT[:, :], W["l1_out_s"][:, :]), (sT[0:64, :], W["l1_skip_s"][:, :])).then_inc(done, 1)
                        at(pe, "product_v", g)
                        for t in range(G):
                            c = slice(P * t, P * t + P)
                            nc.tensor.matmul(wideA[:, t, 0:C1V], vT[:, c], W["l1_skip_v"][:, :], start=True, stop=False, skip_group_check=True)
                            for d in range(3):
                                last = nc.tensor.matmul(wideA[:, t, C1 * d:C1 * d + C1], gT[d][:, c], W["l1_out_v"][:, :], start=False,
                                                        stop=True, skip_group_check=True)
                        last.then_inc(done, 1)
                    else:
                        at(pe, "product", g)
                        times(wideB, 0, (aT[:, :], W["l3_w2_s"][:, :]))
                        for d in range(3):
                            last = times(wideB, 65 + C1 * d, (gT[d][:, :], W["l3_w2_v"][:, :]))
                        last.then_inc(done, 1)
                        at(pe, "product_v", g)
                        times(wideA, 0, (sT[0:64, :], W["l3_sc_s"][:, :]))
                        times(wideA, C0, (vT[:, :], W["l3_sc_v"][:, :])).then_inc(done, 1)
                if pre is not None:
                    src = nrm if pre in (0, 2) else out
                    at(pe, "turn_p", g)
                    turn(src, 0, C0, psA)
                    turn(src, C0, CX, psA, 1024).then_inc(done, 1)
                    at(pe, "tables", g)
                    times(wideB, 0, (sT[0:W[f"l{pre}_tab_s"].shape[0], :], W[f"l{pre}_tab_s"][:, :]))
                    times(wideA, 0, (vT[:, :], W[f"l{pre}_tab_v"][:, :])).then_inc(done, 1)

        @block.scalar
        def _(act):
            def move(to, src, n, scale=1.0, bias=0.0):
                if isinstance(scale, float) and isinstance(bias, float):
                    return nc.scalar.activation(to[0:n, :], src[0:n, 0:G * P], ACT.Copy)
                return nc.scalar.activation(to[0:n, :], src[0:n, 0:G * P], ACT.Identity, scale=scale, bias=bias)

            second = psA[:, 1024:2048]

            def square(tag, src, g):
                at(act, tag + "square", g)
                nc.scalar.activation(sqr[:, :, 0:C0], cen[:, :, 0:C0], ACT.Square)
                nc.scalar.activation(sqr[:, :, C0:CX], src[:, :, C0:CX], ACT.Square).then_inc(done, 1)

            with act.Fori(0, NG) as g:
                if post in (0, 2):
                    at(act, "move_a", g)
                    move(sT, psA, 64)
                    move(vT, second, 96).then_inc(done, 1)
                if post == 0:
                    square("ln2_", res, g)
                    at(act, "move_n", g)
                    move(sT, psA, 64, W["l0_ln2_w0"][:, 0:1], W["l0_ln2_b0"][:, 0:1])
                    move(vT, second, 96, W["l0_ln2_w1"][:, 0:1]).then_inc(done, 1)
                    at(act, "scalars", g)
                    for t in range(G):
                        last = nc.scalar.activation(sc[:, t, :], wideB[:, t, 0:P], ACT.Silu, scale=attr[:, 0, t:t + 1])
                    last.then_inc(done, 1)
                    at(act, "gate_t", g)
                    for t in range(G):
                        last = nc.scalar.activation(th[:, t, :], wideB[:, t, P:192], ACT.Tanh, scale=attr[:, 1, t:t + 1])
                    last.then_inc(done, 1)
                    at(act, "gate_v", g)
                    for t in range(G):
                        last = nc.scalar.activation(fv[:, t, :], wideA[:, t, 0:192], ACT.Copy, scale=attr[:, 1, t:t + 1])
                    last.then_inc(done, 1)
                    at(act, "move_f", g)
                    move(scT, psA, P)
                    move(fvTa, second, P)
                    move(fvTb, psB, 64).then_inc(done, 1)
                if post in (1, 3):
                    per = 128 if post == 1 else 96
                    at(act, "move_s", g)
                    move(aT, psA, 96)
                    move(gT[0], second, per).then_inc(done, 1)
                    at(act, "move_v", g)
                    move(gT[1], psA, per)
                    move(gT[2], second, per).then_inc(done, 1)
                    at(act, "move_x", g)
                    move(sT, psA, 64)
                    move(vT, second, 96).then_inc(done, 1)
                if post == 1:
                    at(act, "silu", g)
                    nc.scalar.activation(out[:, :, 0:C0], wideB[:, :, 0:C0], ACT.Silu).then_inc(done, 1)
                    at(act, "gate_t", g)
                    nc.scalar.activation(th[:, :, :], wideB[:, :, C0:96], ACT.Tanh, scale=0.5).then_inc(done, 1)
                if post == 3:
                    at(act, "sine", g)
                    nc.scalar.activation(whole_t[:, :, :], ang[:, :, :], ACT.Sin).then_inc(done, 1)
                if post is not None:
                    at(act, "end_square", g)
                    nc.scalar.activation(sqr[:, :, :], cen[:, :, :], ACT.Square).then_inc(done, 1)
                if pre in (0, 2):
                    square("pre_", out, g)
                if pre is not None:
                    at(act, "move_p", g)
                    if pre == 0:
                        move(sT, psA, 64, W["l0_ln1_w0"][:, 0:1], W["l0_ln1_b0"][:, 0:1])
                        last = move(vT, second, 96, W["l0_ln1_w1"][:, 0:1])
                    elif pre == 2:
                        move(sT, psA, 64, W["l2_gamma_s"][:, 0:1], W["l2_beta_s"][:, 0:1])
                        last = move(vT, second, 96, W["l2_gamma_v"][:, 0:1])
                    else:
                        move(sT, psA, 64)
                        last = move(vT, second, 96)
                    last.then_inc(done, 1)
                    at(act, "move_t", g)
                    act.wait_ge(sem("stored"), g * 16 * n_tab)
                    for n in range(n_tab):
                        nc.scalar.activation(tab[:, n, :, 0:C0], wideB[:, :, C0 * n:C0 * n + C0], ACT.Copy)
                        last = nc.scalar.activation(tab[:, n, :, C0:CX], wideA[:, :, C1V * n:C1V * n + C1V], ACT.Copy)
                    last.then_inc(done, 1)

        @block.vector
        def _(dve):
            tt, ts, stt = nc.vector.tensor_tensor, nc.vector.tensor_scalar, nc.vector.scalar_tensor_tensor

            def reduce(to, src):
                return nc.vector.tensor_reduce(to, src, AX.X, ALU.add)

            def stats_eq(tag, src, g, dv, eps):
                s, v = src[:, :, 0:C0], src[:, :, C0:CX]
                at(dve, tag + "mean", g)
                reduce(st[:, 0, :], s).then_inc(done, 1)
                at(dve, tag + "scale_mean", g)
                ts(st[:, 0, :], st[:, 0, :], -1.0 / C0, None, ALU.mult).then_inc(done, 1)
                at(dve, tag + "centre", g)
                tt(cen[:, :, 0:C0], s, bcast(st[:, 0, :], 2, C0), ALU.add).then_inc(done, 1)
                at(dve, tag + "sum", g)
                reduce(st[:, 0, :], sqr[:, :, 0:C0])
                reduce(st[:, 1, :], sqr[:, :, C0:CX]).then_inc(done, 1)
                at(dve, tag + "var", g)
                ts(st[:, 0, :], st[:, 0, :], 1.0 / C0, eps, ALU.mult, ALU.add)
                ts(st[:, 1, :], st[:, 1, :], 1.0 / dv, eps, ALU.mult, ALU.add).then_inc(done, 1)
                at(dve, tag + "norm", g)
                tt(nrm[:, :, 0:C0], cen[:, :, 0:C0], bcast(st[:, 0, :], 2, C0), ALU.mult)
                tt(nrm[:, :, C0:CX], v, bcast(st[:, 1, :], 2, C1V), ALU.mult).then_inc(done, 1)

            nc.vector.memset(sT[64:65, :], 1.0).then_inc(sem("ones"), 1)
            with dve.Fori(0, NG) as g:
                if post is not None:
                    at(dve, "pair", g)
                    dve.wait_ge(sem("loaded"), (g + 1) * 16 * TM)
                    tt(ag[0][:, :, :], ag[0][:, :, :], ag[1][:, :, :], ALU.add)
                    tt(ag[2][:, :, :], ag[2][:, :, :], ag[3][:, :, :], ALU.add)
                    nc.vector.tensor_copy(res[:, :, :], X(g)).then_inc(done, 1)
                    at(dve, "sum", g)
                    tt(ag[0][:, :, :], ag[0][:, :, :], ag[2][:, :, :], ALU.add).then_inc(done, 1)
                if post in (0, 2):
                    total = ag[0][:, :, CX:CX + H]
                    at(dve, "denom", g)
                    ts(den[:, :, :], total, 1e-12 if post == 0 else 1e-16, None, ALU.add).then_inc(done, 1)
                    at(dve, "recip", g)
                    nc.vector.reciprocal(den[:, :, :], den[:, :, :]).then_inc(done, 1)
                    if post == 0:
                        at(dve, "ratio", g)
                        tt(ratio[:, :, :], total, den[:, :, :], ALU.mult).then_inc(done, 1)
                    at(dve, "share", g)
                    by_head = lambda t, a, c: t[:, :, a:a + c * H].rearrange("p t (h c) -> p t h c", h=H)
                    tt(by_head(nrm, 0, HS), by_head(ag[0], 0, HS), bcast(den[:, :, :], 3, HS), ALU.mult)
                    for d in range(3):
                        last = tt(by_head(nrm, C0 + C1 * d, HV), by_head(ag[0], C0 + C1 * d, HV), bcast(den[:, :, :], 3, HV), ALU.mult)
                    last.then_inc(done, 1)
                if post == 0:
                    at(dve, "bias", g)
                    tt(by_head(cen, 0, HS), bcast(W["l0_bias"][:, 64:128], 1, G).rearrange("p t (h c) -> p t h c", h=H),
                       bcast(ratio[:, :, :], 3, HS), ALU.mult).then_inc(done, 1)
                    at(dve, "merged", g)
                    tt(nrm[:, :, 0:C0], nrm[:, :, 0:C0], cen[:, :, 0:C0], ALU.add).then_inc(done, 1)
                if post == 0:
                    at(dve, "residual", g)
                    tt(res[:, :, :], X(g), wideB[:, :, 0:CX], ALU.add).then_inc(done, 1)
                    stats_eq("ln2_", res, g, C1V, 1e-5)
                    at(dve, "attr", g)
                    nc.vector.tensor_copy(attr[:, 0, :], NA(g))
                    ts(attr[:, 1, :], NA(g), 0.5, None, ALU.mult).then_inc(done, 1)
                    at(dve, "gated", g)
                    for d in range(3):
                        v = fv[:, :, 64 * d:64 * d + 64]
                        last = stt(out=v, in0=th[:, :, :], scalar=1.0, in1=v, op0=ALU.add, op1=ALU.mult)
                    last.then_inc(done, 1)
                    at(dve, "f2_bias", g)
                    tt(out[:, :, 0:C0], wideB[:, :, 0:C0], bcast(W["l0_f2_b"][:, :], 1, G), ALU.add)
                    nc.vector.tensor_copy(out[:, :, C0:CX], wideB[:, :, C0:CX]).then_inc(done, 1)
                    at(dve, "f2_attr", g)
                    tt(out[:, :, :], out[:, :, :], bcast(attr[:, 0, :], 2, CX), ALU.mult).then_inc(done, 1)
                    at(dve, "both", g)
                    tt(out[:, :, :], out[:, :, :], res[:, :, :], ALU.add).then_inc(done, 1)
                    at(dve, "whole", g)
                    tt(res[:, :, :], out[:, :, :], X(g), ALU.add).then_inc(done, 1)
                if post == 1:
                    at(dve, "gate_half", g)
                    ts(th[:, :, :], th[:, :, :], 0.5, 0.5, ALU.mult, ALU.add).then_inc(done, 1)
                    at(dve, "gated", g)
                    tt(comp(out[:, :, C0:CX]), comp(wideA[:, :, 0:C1V]), bcast(th[:, :, :], 2, 3), ALU.mult).then_inc(done, 1)
                    at(dve, "whole", g)
                    tt(res[:, :, :], res[:, :, :], out[:, :, :], ALU.add).then_inc(done, 1)
                if post == 2:
                    at(dve, "twice", g)
                    tt(out[:, :, :], res[:, :, :], wideB[:, :, 0:CX], ALU.add).then_inc(done, 1)
                    at(dve, "whole", g)
                    tt(res[:, :, :], res[:, :, :], out[:, :, :], ALU.add).then_inc(done, 1)
                if post == 3:
                    at(dve, "angle", g)
                    tt(ang[:, 0, :], wideB[:, :, 64:65].rearrange("p t c -> p (t c)"), NA(g), ALU.mult)
                    nc.vector.tensor_copy(attr[:, 0, :], NA(g)).then_inc(done, 1)
                    at(dve, "attr", g)
                    nc.vector.tensor_copy(attr[:, 1, :], attr[:, 0, :]).then_inc(done, 1)
                    at(dve, "turns", g)
                    ts(whole_t[:, 0, :], ang[:, 0, :], 1.0 / (2 * PI), None, ALU.mult).then_inc(done, 1)
                    at(dve, "turns_i", g)
                    nc.vector.tensor_copy(turns_i[:, 0, :], whole_t[:, 0, :]).then_inc(done, 1)
                    at(dve, "turns_f", g)
                    nc.vector.tensor_copy(whole_t[:, 0, :], turns_i[:, 0, :]).then_inc(done, 1)
                    at(dve, "reduce", g)
                    c1 = 6.28125
                    c2 = float(np.float32(2 * np.pi - c1) - np.float32(2 * np.pi - c1) % np.float32(2.0 ** -21))
                    c3 = 2 * np.pi - c1 - c2
                    for n, c in enumerate((c1, c2, c3)):
                        ins = stt(out=ang[:, 0, :], in0=whole_t[:, 0, :], scalar=-c, in1=ang[:, 0, :], op0=ALU.mult, op1=ALU.add)
                        if n < 2:
                            ins.then_inc(sem("part"), 1)
                            dve.wait_ge(sem("part"), g * 2 + n + 1)
                    ins.then_inc(done, 1)
                    at(dve, "shift", g)
                    ts(ang[:, 1, :], ang[:, 0, :], PI / 2, None, ALU.add).then_inc(done, 1)
                    at(dve, "shift_gt", g)
                    ts(whole_t[:, :, :], ang[:, :, :], PI, -2 * PI, ALU.is_gt, ALU.mult).then_inc(done, 1)
                    at(dve, "shift_in", g)
                    tt(ang[:, :, :], ang[:, :, :], whole_t[:, :, :], ALU.add).then_inc(sem("low"), 1)
                    dve.wait_ge(sem("low"), 4 * g + 1)
                    ts(whole_t[:, :, :], ang[:, :, :], -PI, 2 * PI, ALU.is_lt, ALU.mult).then_inc(sem("low"), 1)
                    dve.wait_ge(sem("low"), 4 * g + 2)
                    tt(ang[:, :, :], ang[:, :, :], whole_t[:, :, :], ALU.add).then_inc(sem("low"), 1)
                    dve.wait_ge(sem("low"), 4 * g + 3)
                    ts(ang[:, :, :], ang[:, :, :], float(np.nextafter(np.float32(PI), np.float32(0))), -float(np.nextafter(np.float32(PI), np.float32(0))),
                       ALU.min, ALU.max).then_inc(sem("low"), 1)
                    dve.wait_ge(sem("low"), 4 * g + 4)
                    dve.sem_inc(done, 1)
                    at(dve, "skip_attr", g)
                    tt(whole_t[:, :, :], whole_t[:, :, :], attr[:, :, :], ALU.mult).then_inc(done, 1)
                    at(dve, "conv_attr", g)
                    tt(out[:, :, 0:C0], wideB[:, :, 0:C0], bcast(whole_t[:, 0, :], 2, C0), ALU.mult)
                    tt(out[:, :, C0:CX], wideB[:, :, 65:161], bcast(whole_t[:, 0, :], 2, C1V), ALU.mult).then_inc(done, 1)
                    at(dve, "mix_a", g)
                    tt(skip[:, :, :], wideA[:, :, 0:CX], bcast(whole_t[:, 1, :], 2, CX), ALU.mult).then_inc(done, 1)
                    at(dve, "mix_b", g)
                    tt(out[:, :, :], out[:, :, :], skip[:, :, :], ALU.add).then_inc(done, 1)
                    at(dve, "mix_c", g)
                    tt(res[:, :, :], res[:, :, :], out[:, :, :], ALU.add).then_inc(done, 1)
                    at(dve, "whole", g)
                    dve.sem_inc(done, 1)
                if post is not None:
                    at(dve, "end_mean", g)
                    reduce(st[:, 0, :], res[:, :, :]).then_inc(done, 1)
                    at(dve, "end_scale_mean", g)
                    ts(st[:, 0, :], st[:, 0, :], -1.0 / CX, None, ALU.mult).then_inc(done, 1)
                    at(dve, "end_centre", g)
                    tt(cen[:, :, :], res[:, :, :], bcast(st[:, 0, :], 2, CX), ALU.add).then_inc(done, 1)
                    at(dve, "end_sum", g)
                    reduce(st[:, 0, :], sqr[:, :, :])
                    nc.vector.memset(st[:, 1, :], 1.0).then_inc(done, 1)
                    at(dve, "end_var", g)
                    ts(st[:, 0, :], st[:, 0, :], 1.0 / CX, 1e-5, ALU.mult, ALU.add).then_inc(done, 1)
                    at(dve, "end_norm", g)
                    if pre is None:
                        dve.wait_ge(sem("stored"), g * 16)
                        tt(final[:, :, :], cen[:, :, :], bcast(st[:, 0, :], 2, CX), ALU.mult).then_inc(done, 1)
                    else:
                        tt(out[:, :, :], cen[:, :, :], bcast(st[:, 0, :], 2, CX), ALU.mult)
                        tt(X(g), cen[:, :, :], bcast(st[:, 0, :], 2, CX), ALU.mult).then_inc(done, 1)
                if pre in (0, 2):
                    if post is None:
                        at(dve, "pre_mean", g)
                        nc.vector.tensor_copy(out[:, :, :], X(g)).then_inc(sem("copied"), 1)
                        dve.wait_ge(sem("copied"), g + 1)
                    stats_eq("pre_", out, g, C1V if pre == 0 else C1, 1e-5)
                if pre == 3:
                    at(dve, "tab_attr", g)
                    tt(tab[:, 0, :, :], tab[:, 0, :, :], bcast(NA(g), 2, CX), ALU.mult).then_inc(done, 1)



def graph_network(nc, D):
    with ExitStack() as ctx:
        W = setup(nc, ctx, D)
        node_phase(nc, W, D, None, 0)
        for layer, H, edges in ((0, 8, layer0_edges), (2, 4, layer2_edges)):
            with ExitStack() as inner:
                logits = inner.enter_context(nc.sbuf_tensor(f"logits{layer}", [P, ET, H], F32))
                edges(nc, W, D, logits)
                probs = inner.enter_context(nc.sbuf_tensor(f"probs{layer}", [P, ET, H], F32))
                softmax_weights(nc, W, D, logits, probs, H, f"m{layer}")
                attention_sums(nc, W, D, probs, layer, H, f"s{layer}", (1, 2, 3) if layer == 0 else ())
            node_phase(nc, W, D, layer, layer + 1)
            by = ("dst", "src") if layer == 0 else ("src", "dst")
            convolution_edges(nc, W, D, layer + 1, *by, f"e{layer + 1}")
            node_phase(nc, W, D, layer + 1, layer + 2 if layer == 0 else None)


_WEIGHTS = (
    [f"L0_gnn_{k}" for k in (
        "ln1_w0 ln1_b0 ln1_w1 ln2_w0 ln2_b0 ln2_w1 msrc_ws msrc_wv mdst_ws mdst_bs mdst_wv rw1 rb1 rg1 rbe1 rw2 rb2 rg2 rbe2 rw3 roff "
        "lin_ws lin_bs lin_wv alpha_dot proj_ws proj_bs proj_wv f1_ws f1_bs f1_wv f2_ws f2_bs f2_wv").split()]
    + [f"L1_gnn_{k}" for k in "W_skip0 W_skip1 W_nl0 W_nl1 W_fc1 W_fc2 W_out_s W_out_v".split()]
    + [f"L2_gnn_{k}" for k in (
        "gamma_s beta_s gamma_v Ws_src Wv_src Ws_dst Wv_dst W_rbf W_alpha alpha_dot Ws_val Wv_val Wg w2_ss w2_sv w2_vs w2_vv0 w2_vv1 "
        "Ws_vlin Wv_vlin Wps Wpv").split()]
    + [f"L3_gnn_{k}" for k in "W_sc_s W_sc_v W1_s W1_v W2_s W2_v W3 fcW1 fcW2".split()]
)


def _padded(a, rows, fill):
    a = np.asarray(a)
    return np.concatenate([a, np.full((rows - a.shape[0],) + a.shape[1:], fill, a.dtype)], axis=0)


def _turned(a):
    return np.ascontiguousarray(a.reshape(P, ET, -1).transpose(2, 1, 0).reshape(a.shape[1], EPAD))


def kernel(**inputs):
    import concourse.bacc as _bacc
    from concourse.bass_utils import run_bass_kernel_spmd as _run

    x = np.asarray(inputs["x"])
    by_component = x[:, C0:].reshape(-1, C1, 3).transpose(0, 2, 1).reshape(-1, C1V)
    arrays = {"x": _padded(np.concatenate([x[:, :C0], by_component], axis=1), NPAD, 0.0)}
    for k in ("src", "dst"):
        e = _padded(inputs[k], EPAD, NPAD - 1).reshape(P, ET)
        arrays[k], arrays[k + "_t"] = e, np.ascontiguousarray(e.T)
    for k in (3, 4):
        arrays[f"edge_attr_{k}"] = _padded(inputs[f"edge_attr_{k}"], EPAD, 1.0).reshape(P, ET * k)
    for k in (8, 16, 64):
        arrays[f"es{k}"] = _turned(_padded(inputs[f"edge_attr_{k}"], EPAD, 1.0))
    arrays["es64"] = np.concatenate([arrays["es64"], np.ones((1, EPAD), np.float32)], axis=0)
    arrays["node_vec1"] = _padded(inputs["node_vec1"], NPAD, 1.0).reshape(P, NT)
    for k in _WEIGHTS:
        arrays[k] = np.asarray(inputs[k])

    nc = _bacc.Bacc("TRN2", target_bir_lowering=False, num_devices=1)
    D = {}
    for k, a in arrays.items():
        D[k] = nc.dram_tensor("in_" + k, a.shape, mybir.dt.from_np(a.dtype), kind="ExternalInput").ap()
    for k in ("tab_src", "tab_dst"):
        D[k] = nc.dram_tensor(k, (NPAD, CX), F32, kind="Internal").ap()
    D["val"] = nc.dram_tensor("val", (P, ET, CX), F32, kind="Internal").ap()
    D["acc"] = [[nc.dram_tensor(f"acc{n}{k}", (ROWS, w), F32, kind="Internal").ap() for k in range(TM)] for n, w in enumerate(ACC_W)]
    D["out"] = nc.dram_tensor("out", (NPAD, CX), F32, kind="ExternalOutput").ap()
    graph_network(nc, D)
    r = _run(nc, [{"in_" + k: a for k, a in arrays.items()}], core_ids=[0])
    y = np.asarray(r.results[0]["out"])[:N_NODES]
    v = y[:, C0:].reshape(-1, 3, C1).transpose(0, 2, 1).reshape(-1, C1V)
    return np.ascontiguousarray(np.concatenate([y[:, :C0], v], axis=1))
```

```python
from contextlib import ExitStack

import numpy as np

import concourse.bass as bass
from concourse import mybir

F32 = mybir.dt.float32
I32 = mybir.dt.int32
ALU = mybir.AluOpType
ACT = mybir.ActivationFunctionType
AX = mybir.AxisListType

P = 128
N_NODES, N_EDGES = 6250, 100000
C0, C1 = 64, 32
C1V = 3 * C1
CX = C0 + C1V
G = 4
PAIRS = -(-N_NODES // (P * 2 * G))
NT = PAIRS * 2 * G
ET = 784
NPAD, EPAD = P * NT, P * ET
TM = 4
NM = ET // TM
ME = TM * P
ROWS = NPAD + P
ACC_W = (168, 480, 164, 384)
NBIG = -1.0e30
SQ3 = float(np.sqrt(np.float32(3.0)))


class Names:

    def __init__(self, nc, ctx, tag):
        self.nc, self.ctx, self.tag, self.sems = nc, ctx, tag, {}
        ctx.callback(self.release)

    def release(self):
        self.nc.clear_and_free_semaphores(list(self.sems.values()))
        self.nc.all_engine_barrier()

    def sb(self, name, shape, dt=F32):
        return self.ctx.enter_context(self.nc.sbuf_tensor(f"{self.tag}_{name}", shape, dt))

    def ps(self, name, shape):
        return self.ctx.enter_context(self.nc.psum_tensor(f"{self.tag}_{name}", shape, F32))

    def sem(self, name):
        if name not in self.sems:
            self.sems[name] = self.nc.alloc_semaphore(f"{self.tag}_{name}")
        return self.sems[name]


def wait(eng, sem, value):
    if not isinstance(value, int) or value > 0:
        eng.wait_ge(sem, value)


def wait_apart(eng, sem, value, passed):
    if not isinstance(value, int):
        eng.wait_ge(sem, value)
        eng.sem_inc(passed, 1)
    elif value > 0:
        eng.wait_ge(sem, value)


def steps(eng, n_macros, last_skew, body):
    total = n_macros + last_skew
    lead = last_skew + 3 + (last_skew + 3) % 2
    turns = (n_macros - lead) // 2

    def fixed(n):
        def i_of(skew, more=0):
            i = n - skew
            return (i, i % 2, i // 2) if 0 <= i < n_macros + more else None
        return i_of

    def looped(j, s):
        def i_of(skew, more=0):
            u = (s - skew) % 2
            half = (s - skew - u) // 2
            return (j + half) * 2 + u, u, j + half
        return i_of

    for n in range(lead):
        body(fixed(n))
    with eng.Fori(lead // 2, lead // 2 + turns) as j:
        for s in range(2):
            body(looped(j, s))
    for n in range(lead + 2 * turns, total):
        body(fixed(n))


def bcast(ap, axis, n):
    ap = ap.unsqueeze(axis)
    shape = list(ap.shape)
    shape[axis] = n
    return ap.to_broadcast(shape)


def col(ap):
    return ap.rearrange("(a b) -> a b", b=1)


def row(ap):
    return ap.rearrange("(a b) -> a b", a=1)



def setup(nc, ctx, D):
    N = Names(nc, ctx, "w")
    W = {}
    loads = []

    def tile(name, shape, *parts, dt=F32):
        W[name] = N.sb(name, shape, dt)
        loads.extend((W[name], region, src) for region, src in parts)

    def whole(name, shape, src):
        tile(name, shape, ((slice(0, shape[0]), slice(0, shape[1])), src))

    def blocks(name, shape, src, at):
        r, c = src.shape
        tile(name, shape, *[((slice(a, a + r), slice(b, b + c)), src) for a, b in at])

    W["x"] = N.sb("x", [P, NT, CX])
    W["na"] = N.sb("na", [P, NT])
    W["ident"] = N.sb("ident", [P, P])
    W["tri"] = N.sb("tri", [P, P])
    W["spare"] = N.sb("spare", [P, 1], I32)
    W["zeros"] = N.sb("zeros", [P, 512])
    W["half"] = N.sb("half", [P, ET // PAIRS])
    W["unsorted"] = N.sb("unsorted", [1, 1], I32)
    W["norm"] = [N.sb(f"norm{n}", [P, ET]) for n in range(2)]
    diag3 = [(C1 * d, C1 * d) for d in range(3)]

    tile("l0_rw1", [65, 64], ((slice(0, 64), slice(0, 64)), D["L0_gnn_rw1"]), ((slice(64, 65), slice(0, 64)), row(D["L0_gnn_rb1"])))
    tile("l0_rw2", [P, 64], ((slice(64, P), slice(0, 64)), D["L0_gnn_rw2"]))
    blocks("l0_rb2", [1, 64 * TM], row(D["L0_gnn_rb2"]), [(0, 64 * k) for k in range(TM)])
    tile("l0_rw3", [65, 224], ((slice(0, 64), slice(0, 224)), D["L0_gnn_rw3"]), ((slice(64, 65), slice(0, 224)), row(D["L0_gnn_roff"])))
    for k in ("rg1", "rbe1"):
        tile("l0_" + k, [P, 1], ((slice(64, P), slice(0, 1)), col(D["L0_gnn_" + k])))
    for k in ("rg2", "rbe2", "ln1_w0", "ln1_b0", "ln2_w0", "ln2_b0"):
        whole("l0_" + k, [64, 1], col(D["L0_gnn_" + k]))
    for k in ("ln1_w1", "ln2_w1"):
        tile("l0_" + k, [96, 1], *[((slice(C1 * d, C1 * d + C1), slice(0, 1)), col(D["L0_gnn_" + k])) for d in range(3)])
    tile("l0_tab_s", [65, 128], ((slice(0, 64), slice(0, 64)), D["L0_gnn_msrc_ws"]), ((slice(0, 64), slice(64, 128)), D["L0_gnn_mdst_ws"]),
         ((slice(64, 65), slice(64, 128)), row(D["L0_gnn_mdst_bs"])))
    tile("l0_tab_v", [96, 192], *[((slice(32 * d, 32 * d + 32), slice(o + 32 * d, o + 32 * d + 32)), D["L0_gnn_" + k])
                                  for d in range(3) for o, k in ((0, "msrc_wv"), (96, "mdst_wv"))])
    message_weights(tile, "l0", [(D["L0_gnn_lin_ws"], 0)], D["L0_gnn_lin_wv"])
    tile("l0_bias", [P, 128], ((slice(0, P), slice(0, 128)), D["L0_gnn_lin_bs"].partition_broadcast(P)))
    tile("l0_adot", [P, 64], ((slice(0, P), slice(0, 64)), D["L0_gnn_alpha_dot"].rearrange("h a -> (h a)").partition_broadcast(P)))
    tile("l0_proj_s", [65, 64], ((slice(0, 64), slice(0, 64)), D["L0_gnn_proj_ws"]), ((slice(64, 65), slice(0, 64)), row(D["L0_gnn_proj_bs"])))
    blocks("l0_proj_v", [96, 96], D["L0_gnn_proj_wv"], diag3)
    tile("l0_f1_s", [65, 192], ((slice(0, 64), slice(0, 192)), D["L0_gnn_f1_ws"]), ((slice(64, 65), slice(0, 192)), row(D["L0_gnn_f1_bs"])))
    blocks("l0_f1_v", [96, 192], D["L0_gnn_f1_wv"], [(C1 * d, 64 * d) for d in range(3)])
    whole("l0_f2_s", [128, 64], D["L0_gnn_f2_ws"])
    blocks("l0_f2_va", [128, 96], D["L0_gnn_f2_wv"], [(0, 0), (64, 32)])
    blocks("l0_f2_vb", [64, 96], D["L0_gnn_f2_wv"], [(0, 64)])
    tile("l0_f2_b", [P, 64], ((slice(0, P), slice(0, 64)), D["L0_gnn_f2_bs"].partition_broadcast(P)))
    whole("l1_fc1", [64, 64], D["L1_gnn_W_fc1"])
    whole("l1_fc2", [64, 224], D["L1_gnn_W_fc2"])
    whole("l1_tab_s", [64, 64], D["L1_gnn_W_nl0"])
    blocks("l1_tab_v", [96, 96], D["L1_gnn_W_nl1"], diag3)
    whole("l1_skip_s", [64, 96], D["L1_gnn_W_skip0"])
    blocks("l1_skip_v", [96, 96], D["L1_gnn_W_skip1"], diag3)
    whole("l1_out_s", [96, 96], D["L1_gnn_W_out_s"])
    whole("l1_out_v", [128, 32], D["L1_gnn_W_out_v"])
    whole("l2_rbf", [16, 224], D["L2_gnn_W_rbf"])
    for k in ("gamma_s", "beta_s"):
        whole("l2_" + k, [64, 1], col(D["L2_gnn_" + k]))
    tile("l2_gamma_v", [96, 1], *[((slice(C1 * d, C1 * d + C1), slice(0, 1)), col(D["L2_gnn_gamma_v"])) for d in range(3)])
    tile("l2_tab_s", [64, 128], ((slice(0, 64), slice(0, 64)), D["L2_gnn_Ws_src"]), ((slice(0, 64), slice(64, 128)), D["L2_gnn_Ws_dst"]))
    tile("l2_tab_v", [96, 192], *[((slice(32 * d, 32 * d + 32), slice(o + 32 * d, o + 32 * d + 32)), D["L2_gnn_" + k])
                                  for d in range(3) for o, k in ((0, "Wv_src"), (96, "Wv_dst"))])
    message_weights(tile, "l2", [(D["L2_gnn_W_alpha"], 0), (D["L2_gnn_Ws_val"], 64)], D["L2_gnn_Wv_val"])
    message_weights(tile, "l2b", [(D["L2_gnn_Ws_vlin"], 0)], D["L2_gnn_Wv_vlin"])
    whole("l2_wg", [64, 32], D["L2_gnn_Wg"])
    tile("l2_adot", [P, 64], ((slice(0, P), slice(0, 64)), D["L2_gnn_alpha_dot"].rearrange("o h a -> (o h a)").partition_broadcast(P)))
    tile("l2_w2", [P, 3], *[((slice(a, a + n), slice(c, c + 1)), col(D["L2_gnn_" + k])) for k, a, n, c in (
        ("w2_ss", 0, 64, 0), ("w2_vv0", 64, 32, 0), ("w2_vv1", 96, 32, 0),
        ("w2_vv1", 0, 32, 1), ("w2_vv1", 32, 32, 1), ("w2_sv", 64, 64, 1),
        ("w2_vs", 0, 32, 2), ("w2_vs", 32, 32, 2), ("w2_vs", 64, 32, 2))])
    whole("l2_proj_s", [64, 64], D["L2_gnn_Wps"])
    blocks("l2_proj_v", [96, 96], D["L2_gnn_Wpv"], diag3)
    whole("l3_fc1", [8, 64], D["L3_gnn_fcW1"])
    whole("l3_fc2", [64, 192], D["L3_gnn_fcW2"])
    whole("l3_tab_s", [64, 64], D["L3_gnn_W1_s"])
    blocks("l3_tab_v", [96, 96], D["L3_gnn_W1_v"], diag3)
    whole("l3_sc_s", [64, 64], D["L3_gnn_W_sc_s"])
    blocks("l3_sc_v", [96, 96], D["L3_gnn_W_sc_v"], diag3)
    tile("l3_w2_s", [96, 65], ((slice(0, 96), slice(0, 64)), D["L3_gnn_W2_s"]), ((slice(0, 96), slice(64, 65)), D["L3_gnn_W3"]))
    whole("l3_w2_v", [96, 32], D["L3_gnn_W2_v"])

    cleared = [k for k in W if k not in ("x", "na", "ident", "tri", "spare", "half", "norm", "unsorted")]
    with ExitStack() as inner:
        L = Names(nc, inner, "setup")
        filled, loaded, shaped, wiped = L.sem("filled"), L.sem("loaded"), L.sem("shaped"), L.sem("wiped")
        mean = L.sb("mean", [P, 3])
        block = inner.enter_context(nc.Block())
        dst, ends = L.sb("dst", [P, ET], I32), L.sb("ends", [1, 2, P], I32)
        falls, fall_sum, ends_fall = L.sb("falls", [P, ET]), L.sb("fall_sum", [P, 2]), L.sb("ends_fall", [1, P])
        psU = L.ps("psU", [1, 512])
        vec, vec_sq = L.sb("vec", [P, ET, 3]), L.sb("vec_sq", [P, ET, 3])

        @block.gpsimd
        def _(pool):
            nc.gpsimd.memset(W["ident"][:, :], 0.0).then_inc(filled, 1)
            nc.gpsimd.memset(W["tri"][:, :], 1.0).then_inc(filled, 1)
            nc.gpsimd.memset(W["half"][:, :], -0.5).then_inc(filled, 1)
            nc.gpsimd.iota(W["spare"][:, :], [[0, 1]], base=NPAD, channel_multiplier=1).then_inc(filled, 1)
            pool.wait_ge(filled, 4)
            nc.gpsimd.affine_select(out=W["ident"][:, :], in_=W["ident"][:, :], compare_op=ALU.not_equal, fill=1.0,
                                    base=0, pattern=[[-1, P]], channel_multiplier=1).then_inc(shaped, 1)
            nc.gpsimd.affine_select(out=W["tri"][:, :], in_=W["tri"][:, :], compare_op=ALU.is_gt, fill=0.0,
                                    base=0, pattern=[[-1, P]], channel_multiplier=1).then_inc(shaped, 1)

        @block.vector
        def _(dve):
            for k in cleared:
                t = W[k]
                last = nc.vector.memset(t[:, :], 0.0)
            last.then_inc(wiped, 1)
            dve.wait_ge(loaded, 16 * (len(loads) + 6))
            n = 0

            def link(ins):
                nonlocal n
                n += 1
                ins.then_inc(shaped_dve, 1)
                dve.wait_ge(shaped_dve, n)

            shaped_dve = L.sem("shaped_dve")
            link(nc.vector.tensor_tensor(falls[:, 0:ET - 1], dst[:, 1:ET], dst[:, 0:ET - 1], ALU.is_lt))
            link(nc.vector.tensor_reduce(fall_sum[:, 0:1], falls[:, 0:ET - 1], AX.X, ALU.add))
            link(nc.vector.memset(fall_sum[:, 1:2], 1.0))
            dve.sem_inc(L.sem("falls"), 1)
            link(nc.vector.tensor_tensor(ends_fall[:, 0:P - 1], ends[:, 0, 1:P], ends[:, 1, 0:P - 1], ALU.is_lt))
            link(nc.vector.tensor_reduce(ends_fall[:, P - 1:P], ends_fall[:, 0:P - 1], AX.X, ALU.add))
            dve.wait_ge(L.sem("fall_count"), 1)
            link(nc.vector.tensor_tensor(ends_fall[:, 0:1], ends_fall[:, P - 1:P], psU[:, 0:1], ALU.add))
            link(nc.vector.tensor_scalar(W["unsorted"][:, :], ends_fall[:, 0:1], 1.0, None, ALU.min))
            link(nc.vector.tensor_tensor(vec_sq[:, :, :], vec[:, :, :], vec[:, :, :], ALU.mult))
            link(nc.vector.tensor_reduce(W["norm"][1][:, :], vec_sq[:, :, :], AX.X, ALU.add))
            link(nc.vector.tensor_scalar(W["norm"][0][:, :], W["norm"][1][:, :], 1e-12, None, ALU.add))
            for c, (k, r) in enumerate((("l0_rw1", slice(0, 65)), ("l0_rw2", slice(64, P)), ("l0_rb2", slice(0, 1)))):
                m = mean[r, c:c + 1]
                link(nc.vector.tensor_reduce(m, W[k][r, :], AX.X, ALU.add))
                link(nc.vector.tensor_scalar(m, m, 1.0 / W[k].shape[1], None, ALU.mult))
                link(nc.vector.tensor_scalar(W[k][r, :], W[k][r, :], m, None, ALU.subtract))
            link(nc.vector.tensor_scalar(W["l0_adot"][:, :], W["l0_adot"][:, :], 0.4, None, ALU.mult))

            def scale(k, rows, cols, by):
                t = W[k][rows, cols]
                link(nc.vector.tensor_scalar(t, t, by, None, ALU.mult))

            A = slice(None)
            scale("l0_t1", slice(64, 128), A, SQ3)
            scale("l0_x0", slice(96, 128), A, float(np.sqrt(1.5)))
            scale("l0_t1", slice(0, 64), A, float(np.sqrt(1.5)))
            for k, w2 in (("l2", False), ("l2b", True)):
                scale(k + "_t0", slice(64, 96), A, 1.0 / SQ3)
                scale(k + "_x0", slice(96, 128), A, float(np.sqrt(0.5)))
                scale(k + "_t1", slice(0, 64), A, float(np.sqrt(0.5)))
                if w2:
                    scale(k + "_t0", slice(0, 96), A, W["l2_w2"][0:96, 0:1])
                    scale(k + "_x0", slice(96, 128), A, W["l2_w2"][96:128, 0:1])
                    scale(k + "_t1", A, A, W["l2_w2"][:, 1:2])
                    scale(k + "_t2", A, A, W["l2_w2"][0:96, 2:3])
            scale("l1_out_s", A, A, 1.0 / 32)
            scale("l1_out_v", slice(0, 64), A, SQ3 / 32)
            scale("l1_out_v", slice(64, 96), A, 1.0 / 32)
            scale("l1_out_v", slice(96, 128), A, SQ3 / 32 / float(np.sqrt(2.0)))
            f = 1.0 / 8 / float(np.sqrt(10.0)) / float(np.sqrt(96.0))
            scale("l3_tab_s", A, A, 1.0 / 8)
            scale("l3_tab_v", A, A, 1.0 / float(np.sqrt(32.0)))
            scale("l3_sc_s", A, A, 1.0 / 8)
            scale("l3_sc_v", A, A, 1.0 / float(np.sqrt(32.0)))
            scale("l3_w2_s", A, slice(0, 64), f)
            scale("l3_w2_s", A, slice(64, 65), 0.1 * f)
            scale("l3_w2_s", slice(64, 96), A, 1.0 / SQ3)
            scale("l3_w2_v", A, A, f)

        @block.sync
        def _(sp):
            sp.dma_start(W["x"][:, :, :], D["x"].rearrange("(p t) c -> p t c", p=P)).then_inc(loaded, 16)
            sp.dma_start(W["na"][:, :], D["node_vec1"]).then_inc(loaded, 16)
            sp.dma_start(dst[:, :], D["dst"]).then_inc(loaded, 16)
            for n, t in enumerate((0, ET - 1)):
                sp.dma_start(ends[:, n, :], D["dst_t"][t:t + 1, :]).then_inc(loaded, 16)
            sp.dma_start(vec[:, :, :], D["edge_attr_3"].rearrange("p (t c) -> p t c", c=3)).then_inc(loaded, 16)
            sp.wait_ge(wiped, 1)
            for t, region, src in loads[0::2]:
                sp.dma_start(t[region], src).then_inc(loaded, 16)

        @block.tensor
        def _(pe):
            pe.wait_ge(L.sem("falls"), 1)
            nc.tensor.matmul(psU[:, 0:1], fall_sum[:, 0:1], fall_sum[:, 1:2], start=True, stop=True).then_inc(L.sem("fall_count"), 1)

        @block.scalar
        def _(act):
            act.wait_ge(wiped, 1)
            for t, region, src in loads[1::2]:
                act.dma_start(t[region], src).then_inc(loaded, 16)
    return W


def message_weights(tile, tag, scalar, vector):
    width = max(o + s.shape[1] for s, o in scalar)
    wb, wc, wx = vector[0:64, :], vector[64:96, :], vector[96:128, :]
    tile(tag + "_t0", [96, width], *[((slice(0, 96), slice(o, o + s.shape[1])), s) for s, o in scalar])
    tile(tag + "_x0", [128, 96], ((slice(96, 128), slice(0, 32)), wx))
    tile(tag + "_t1", [128, 128], ((slice(0, 32), slice(32, 64)), wx), ((slice(32, 64), slice(64, 96)), wx),
         ((slice(64, 128), slice(96, 128)), wb))
    tile(tag + "_t2", [96, 96], *[((slice(32 * d, 32 * d + 32), slice(32 * d, 32 * d + 32)), wc) for d in range(3)])


def clear(sp, zeros, acc, share, shares, done):
    flat = acc.rearrange("(p t) c -> p (t c)", p=P)
    width = flat.shape[1] // shares
    sp.dma_start(flat[:, bass.ds(share * width, width)], zeros[:, 0:width]).then_inc(done, 16)
    rest = flat.shape[1] - shares * width
    if isinstance(share, int) and share == 0 and rest:
        sp.dma_start(flat[:, shares * width:], zeros[:, 0:rest]).then_inc(done, 16)



F_A, F_D, F_X, F_B, F_C, F_W = 0, 64, 96, 192, 256, 384


def load_directions(nc, S, D, norm):
    vec, dirs = S.sb("vec", [P, ET, 3]), S.sb("dirs", [P, ET, 5])
    loaded, scaled = S.sem("vec_loaded"), S.sem("dirs")

    def sp_part(sp):
        sp.dma_start(vec[:, :, :], D["edge_attr_3"].rearrange("p (t c) -> p t c", c=3)).then_inc(loaded, 16)

    def dve_part(dve):
        dve.wait_ge(loaded, 16)
        nc.vector.tensor_tensor(dirs[:, :, 0:3], vec[:, :, :], bcast(norm[:, :], 2, 3), ALU.mult).then_inc(scaled, 1)
        nc.vector.tensor_tensor(dirs[:, :, 3:5], vec[:, :, 0:2], bcast(norm[:, :], 2, 2), ALU.mult).then_inc(scaled, 1)
        dve.wait_ge(scaled, 2)

    return dirs, sp_part, dve_part


def comp(ap, n=3):
    return ap.rearrange("p t (d c) -> p t d c", d=n)


def dirs_of(dirs, i, a, b):
    return bcast(dirs[:, bass.ds(i * TM, TM), a:b], 3, C1)


def dve_cross(nc, dve, i, O, tmp, dirs, c0, x0, u0, S, tag):
    first, second, done = S.sem(tag + "_first"), S.sem(tag + "_second"), S.sem(tag + "_done")
    wait(dve, done, i)
    X = lambda a, b: O[:, :, x0 + C1 * a:x0 + C1 * b]
    T = lambda n, a, b: comp(tmp[:, n, :, C1 * a:C1 * b], b - a)
    tt = nc.vector.tensor_tensor
    tt(T(0, 0, 3), bcast(O[:, :, u0:u0 + C1], 2, 3), dirs_of(dirs, i, 0, 3), ALU.mult)
    tt(T(1, 0, 2), comp(X(1, 3), 2), dirs_of(dirs, i, 2, 4), ALU.mult)
    tt(T(1, 2, 3), comp(X(0, 1), 1), dirs_of(dirs, i, 4, 5), ALU.mult)
    tt(T(2, 0, 1), comp(X(2, 3), 1), dirs_of(dirs, i, 1, 2), ALU.mult)
    tt(T(2, 1, 3), comp(X(0, 2), 2), dirs_of(dirs, i, 2, 4), ALU.mult).then_inc(first, 1)
    C = O[:, :, c0:c0 + C1V]
    dve.wait_ge(first, i + 1)
    tt(C, C, tmp[:, 0, :, :], ALU.add)
    tt(tmp[:, 1, :, :], tmp[:, 1, :, :], tmp[:, 2, :, :], ALU.subtract).then_inc(second, 1)
    dve.wait_ge(second, i + 1)
    tt(C, C, tmp[:, 1, :, :], ALU.add).then_inc(done, 1)


def pe_linear(nc, pe, i, F, FT, psF, psO, W, w, scalars, ident, S, tag, free_f, free_o, between=None):
    turned, linear, moved = S.sem(tag + "_turned"), S.sem(tag + "_linear"), S.sem(tag + "_FT")
    passed = S.sem("pe_passed")
    c0, x0, u0 = scalars, scalars + C1V, scalars + 2 * C1V

    def turn(k):
        wait_apart(pe, *free_f(k), passed)
        for g in range(3):
            last = nc.tensor.transpose(psF[:, k % 2, P * g:P * g + P], F[:, k, P * g:P * g + P], ident[:, :])
        last.then_inc(turned, 1)

    def maps(k):
        wait_apart(pe, moved, i * TM + k + 1, passed)
        wait_apart(pe, *free_o(k), passed)
        o, f = psO[:, k % psO.shape[1], :], FT[:, k % 2, :]
        nc.tensor.matmul(o[:, 0:scalars], f[0:96, 0:P], W[w + "_t0"][:, :], start=True, stop=True, skip_group_check=True)
        nc.tensor.matmul(o[:, x0:x0 + C1V], f[:, 0:P], W[w + "_x0"][:, :], start=True, stop=False, skip_group_check=True)
        nc.tensor.matmul(o[:, x0:x0 + P], f[:, P:2 * P], W[w + "_t1"][:, :], start=False, stop=True, skip_group_check=True)
        nc.tensor.matmul(o[:, c0:c0 + C1V], f[0:96, 2 * P:3 * P], W[w + "_t2"][:, :], start=True, stop=True,
                         skip_group_check=True).then_inc(linear, 1)

    turn(0)
    turn(1)
    if between:
        between()
    maps(0)
    turn(2)
    maps(1)
    turn(3)
    maps(2)
    maps(3)


def act_linear(nc, act, i, FT, psF, O, psO, width, S, tag, between=None, beside=None):
    turned, linear, moved, out = S.sem(tag + "_turned"), S.sem(tag + "_linear"), S.sem(tag + "_FT"), S.sem(tag + "_O")

    def move(k):
        act.wait_ge(turned, i * TM + k + 1)
        wait(act, linear, i * TM + k - 1)
        nc.scalar.activation(FT[:, k % 2, :], psF[:, k % 2, 0:F_W], ACT.Copy).then_inc(moved, 1)

    def result(k):
        act.wait_ge(linear, i * TM + k + 1)
        nc.scalar.activation(O[:, k, :], psO[:, k % psO.shape[1], 0:width], ACT.Copy).then_inc(out, 1)

    move(0)
    move(1)
    if between:
        between()
    for k in range(TM):
        result(k)
        if k + 2 < TM:
            move(k + 2)
        if beside:
            beside(k)


def sp_indices(sp, i, u, j, ix, D, keys, S, used):
    wait_apart(sp, used[u], j * 16 * TM * len(keys), S.sem("sp_passed"))
    for n, k in enumerate(keys):
        sp.dma_start(ix[u][:, n, :], D[k][:, bass.ds(i * TM, TM)]).then_inc(S.sem(f"ix{u}"), 16)


def pool_gather(nc, pool, i, u, j, ix, tables, into, S, free):
    n = len(tables)
    wait_apart(pool, S.sem(f"ix{u}"), (j + 1) * 16 * n, S.sem("pool_passed"))
    wait_apart(pool, *free, S.sem("pool_passed"))
    for t in range(n):
        for k in range(TM):
            pool.indirect_dma_start(into[t][u][:, k, :], None, tables[t], bass.IndirectOffsetOnAxis(ix[u][:, t, k:k + 1], 0))\
                .then_inc(S.sem(f"gathered{u}"), 16)


def scatter_tensors(S, width):
    return dict(krow=[S.sb(f"krow{u}", [P, TM, P], I32) for u in range(2)],
                kcol=[S.sb(f"kcol{u}", [P, TM], I32) for u in range(2)],
                same=[S.sb(f"same{u}", [P, TM, P]) for u in range(2)], early=S.sb("early", [P, TM, P]), count=S.sb("count", [P, TM]),
                away=S.sb("away", [P, TM]), row=[S.sb(f"row{u}", [P, TM], I32) for u in range(2)],
                sums=[S.sb(f"sums{u}", [P, TM, width]) for u in range(2)])


def sp_keys(sp, i, u, j, T, D, key, S):
    wait_apart(sp, S.sem("rows"), i - 1, S.sem("sp_passed"))
    sp.dma_start(T["kcol"][u][:, :], D[key][:, bass.ds(i * TM, TM)]).then_inc(S.sem(f"keys{u}"), 16)
    sp.dma_start(T["krow"][u][:, :, :], D[key + "_t"][bass.ds(i * TM, TM), :].partition_broadcast(P))\
        .then_inc(S.sem(f"keys{u}"), 16)


def dve_rows(nc, dve, i, u, j, T, W, S):
    dve.wait_ge(S.sem(f"keys{u}"), (j + 1) * 32)
    wait(dve, S.sem("summed"), (i - 1) * TM)
    nc.vector.tensor_tensor(T["same"][u][:, :, :], T["krow"][u][:, :, :], bcast(T["kcol"][u][:, :], 2, P),
                            ALU.is_equal).then_inc(S.sem("same"), 1)
    dve.wait_ge(S.sem("same"), i + 1)
    wait(dve, S.sem("rows"), i)
    for k in range(TM):
        nc.vector.tensor_tensor_reduce(T["early"][:, k, :], T["same"][u][:, k, :], W["tri"][:, :], 1.0, 0.0, ALU.mult, ALU.add,
                                       T["count"][:, k:k + 1]).then_inc(S.sem("counted"), 1)
    nc.vector.tensor_tensor(T["away"][:, :], W["spare"][:, 0:1].to_broadcast([P, TM]), T["kcol"][u][:, :], ALU.subtract)\
        .then_inc(S.sem("away"), 1)
    dve.wait_ge(S.sem("counted"), (i + 1) * TM)
    dve.wait_ge(S.sem("away"), 2 * i + 1)
    nc.vector.scalar_tensor_tensor(out=T["away"][:, :], in0=T["count"][:, :], scalar=1.0, in1=T["away"][:, :], op0=ALU.min,
                                   op1=ALU.mult).then_inc(S.sem("away"), 1)
    dve.wait_ge(S.sem("away"), 2 * i + 2)
    for k in range(TM):
        wait(dve, S.sem(f"added{k}"), (i - 1) * 16)
    nc.vector.tensor_tensor(T["row"][u][:, :], T["away"][:, :], T["kcol"][u][:, :], ALU.add).then_inc(S.sem("rows"), 1)


def pe_sums(nc, pe, i, u, T, values, psS, S, ready):
    passed = S.sem("pe_passed")
    wait_apart(pe, S.sem("same"), i + 1, passed)
    wait_apart(pe, *ready, passed)
    for k in range(TM):
        wait_apart(pe, S.sem("sums"), i * TM + k - len(psS) + 1, passed)
        nc.tensor.matmul(psS[(k) % len(psS)], T["same"][u][:, k, :], values[:, k, :], start=True, stop=True)\
            .then_inc(S.sem("summed"), 1)


def act_sums(nc, act, i, u, j, T, psS, S):
    for k in range(TM):
        wait(act, S.sem(f"added{k}"), (i - 1) * 16)
        act.wait_ge(S.sem("summed"), i * TM + k + 1)
        nc.scalar.activation(T["sums"][u][:, k, :], psS[k % len(psS)], ACT.Copy).then_inc(S.sem("sums"), 1)


def pool_scatter(nc, pool, i, u, j, T, acc, S):
    passed = S.sem("pool_passed")
    wait_apart(pool, S.sem("rows"), i + 1, passed)
    for k in range(TM):
        wait_apart(pool, S.sem("sums"), i * TM + k + 1, passed)
        wait_apart(pool, S.sem(f"added{k}"), i * 16, passed)
        pool.indirect_dma_start(acc[k], bass.IndirectOffsetOnAxis(T["row"][u][:, k:k + 1], 0), T["sums"][u][:, k, :], None,
                                compute_op=ALU.add).then_inc(S.sem(f"added{k}"), 16)



def layer0_edges(nc, W, D, logits):
    LAG = 3
    WEIGHTS, PRODUCT, LINEAR, CROSS, LAST = 2 * LAG, 2 * LAG + 1, 2 * LAG + 2, 2 * LAG + 3, 2 * LAG + 4
    with ExitStack() as ctx:
        S = Names(nc, ctx, "e0")
        sem = S.sem
        dirs, sp_dirs, dve_dirs = load_directions(nc, S, D, W["norm"][0])
        pair = lambda name, shape: [S.sb(f"{name}{u}", shape) for u in range(2)]
        es = pair("es", [65, ME])
        ix = [S.sb(f"ix{u}", [P, 2, TM], I32) for u in range(2)]
        gs, gd = pair("gs", [P, TM, CX]), pair("gd", [P, TM, CX])
        raw, sq = pair("raw", [P, 2 * TM, 64]), pair("sq", [P, 2 * TM, 64])
        var, rstd = pair("var", [P, 2 * TM]), pair("rstd", [P, 2 * TM])
        hn = pair("hn", [P, TM, 2, 64])
        h1, h2 = pair("h1", [P, ME]), pair("h2", [65, ME])
        one = S.sb("one", [1, P])
        msg, prod, dot = S.sb("msg", [P, TM, CX]), S.sb("prod", [P, TM, C1V]), S.sb("dot", [P, TM, C1])
        F = pair("F", [P, TM, F_W])
        FT, tmp = S.sb("FT", [P, 2, F_W]), S.sb("tmp", [P, 3, TM, C1V])
        O_W = 352
        O = pair("O", [P, TM, O_W])
        xb, th = S.sb("xb", [P, TM, 64]), S.sb("th", [P, TM, 64])
        psH, psT = S.ps("psH", [P, 2 * TM, 64]), S.ps("psT", [P, 512])
        psW, psF, psO = S.ps("psW", [P, TM, 256]), S.ps("psF", [P, 2, 512]), S.ps("psO", [P, 2, 512])
        block = ctx.enter_context(nc.Block())

        @block.sync
        def _(sp):
            sp_dirs(sp)

            def body(i_of):
                if m := i_of(0):
                    i, u, j = m
                    wait_apart(sp, sem("pre"), i - 1, sem("sp_passed"))
                    sp.dma_start(es[u][:, :], D["es64"][:, bass.ds(i * ME, ME)]).then_inc(sem(f"es{u}"), 16)
                if m := i_of(WEIGHTS - 1):
                    sp_indices(sp, *m, ix, D, ("src", "dst"), S, [sem("gathered0"), sem("gathered1")])
                if m := i_of(0):
                    i, u, j = m
                    for layer in (2 * u, 2 * u + 1):
                        for acc in D["acc"][layer]:
                            clear(sp, W["zeros"], acc, j, NM // 2, sem(f"clear{layer}"))
                if m := i_of(LAST):
                    i, u, j = m
                    wait_apart(sp, sem("cross_done"), i + 1, sem("sp_passed"))
                    sp.dma_start(D["val"][:, bass.ds(i * TM, TM), :], O[u][:, :, 64:224]).then_inc(sem(f"stored{u}"), 16)

            steps(sp, NM, LAST, body)
            for u in range(2):
                sp.wait_ge(sem(f"stored{u}"), 16 * (NM // 2))
            for layer, width in enumerate(ACC_W):
                rest = ROWS // P * width % (NM // 2) > 0
                sp.wait_ge(sem(f"clear{layer}"), 16 * TM * (NM // 2 + rest))

        @block.gpsimd
        def _(pool):
            def body(i_of):
                if m := i_of(WEIGHTS):
                    pool_gather(nc, pool, *m, ix, (D["tab_src"], D["tab_dst"]), (gs, gd), S, (sem("msg"), m[0] - 1))
                if c := i_of(1, LAG):
                    j, u, _ = c
                    pool.wait_ge(sem("var"), 2 * j + 2)
                    wait(pool, sem("hn"), j - 1)
                    nc.gpsimd.tensor_tensor(rstd[u][:, :], var[u][:, :], W["half"][:, 0:2 * TM], ALU.pow).then_inc(sem("rstd"), 1)

            steps(pool, NM, LAST, body)

        @block.scalar
        def _(act):
            def body(i_of):
                if c := i_of(LAG, LAG):
                    j, u, _ = c
                    act.wait_ge(sem("turned_h"), j + 1)
                    wait(act, sem("pre"), min(j + LAG - 1, NM + LAG) if isinstance(j, int) else j + LAG - 1)
                    nc.scalar.activation(h1[u][64:P, :], psT[64:P, :], ACT.Silu, scale=W["l0_rg1"][64:P, 0:1], bias=W["l0_rbe1"][64:P, 0:1])
                    wait(act, sem("weights"), j - LAG - 1)
                    nc.scalar.activation(h2[u][0:64, :], psT[0:64, :], ACT.Silu, scale=W["l0_rg2"][:, 0:1], bias=W["l0_rbe2"][:, 0:1])\
                        .then_inc(sem("h"), 1)
                if m := i_of(LAST):
                    act.wait_ge(sem("xb"), m[0] + 1)
                    wait(act, sem("leaky"), m[0])
                    nc.scalar.activation(th[:, :, :], xb[:, :, :], ACT.Tanh, scale=0.5).then_inc(sem("th"), 1)

                def hidden():
                    if c := i_of(0, LAG):
                        j, u, _ = c
                        act.wait_ge(sem("pre"), j + 1)
                        wait(act, sem("var"), 2 * j - 2)
                        nc.scalar.activation(sq[u][:, :, :], psH[:, :, :], ACT.Square)
                        wait(act, sem("hn"), j - 1)
                        nc.scalar.activation(raw[u][:, :, :], psH[:, :, :], ACT.Copy).then_inc(sem("raw"), 1)

                if m := i_of(LINEAR):
                    i, u, j = m
                    wait(act, sem(f"stored{u}"), j * 16)
                    act_linear(nc, act, i, FT, psF, O[u], psO, O_W, S, "lin", hidden)
                else:
                    hidden()

            steps(act, NM, LAST, body)

        @block.tensor
        def _(pe):
            passed = sem("pe_passed")

            def body(i_of):
                def hidden():
                    if not (c := i_of(0, LAG)):
                        return
                    j, u, half = c
                    first, second = not isinstance(j, int) or j < NM, not isinstance(j, int) or j >= LAG
                    if first:
                        wait_apart(pe, sem(f"es{u}"), (half + 1) * 16, passed)
                    wait_apart(pe, sem("raw"), j, passed)
                    v = (u + LAG) % 2
                    for k in range(TM):
                        nc.tensor.matmul(psH[:, k, :], es[u][:, P * k:P * k + P], W["l0_rw1"][:, :], start=True, stop=True)
                    if second:
                        wait_apart(pe, sem("h"), j - LAG + 1, passed)
                        nc.tensor.matmul(psH[:, TM:2 * TM, :].rearrange("p t c -> p (t c)"), one[:, :], W["l0_rb2"][:, :], start=True,
                                         stop=False, skip_group_check=True)
                    for k in range(TM):
                        if second:
                            last = nc.tensor.matmul(psH[:, TM + k, :], h1[v][64:P, P * k:P * k + P], W["l0_rw2"][64:P, :], start=False,
                                                    stop=True, skip_group_check=True)
                        else:
                            last = nc.tensor.matmul(psH[:, TM + k, :], es[u][:, P * k:P * k + P], W["l0_rw1"][:, :], start=True, stop=True)
                    last.then_inc(sem("pre"), 1)

                if m := i_of(LINEAR):
                    i, u, j = m
                    wait_apart(pe, sem("products"), i + 1, passed)
                    pe_linear(nc, pe, i, F[u], FT, psF, psO, W, "l0", 128, W["ident"], S, "lin",
                              lambda k: (sem("lin_FT"), i * TM + k - 1), lambda k: (sem("lin_O"), i * TM + k - 1), hidden)
                else:
                    hidden()
                if c := i_of(LAG - 1, LAG):
                    j, u, _ = c
                    wait_apart(pe, sem("hn"), j + 1, passed)
                    wait_apart(pe, sem("h"), j, passed)
                    for k in range(TM):
                        last = nc.tensor.transpose(psT[:, P * k:P * k + P], hn[u][:, k, :, :].rearrange("p n c -> p (n c)"), W["ident"][:, :])
                    last.then_inc(sem("turned_h"), 1)
                if m := i_of(WEIGHTS):
                    i, u, j = m
                    v = (u + LAG) % 2
                    wait_apart(pe, sem("h"), i + LAG + 1, passed)
                    wait_apart(pe, sem("products"), i, passed)
                    for k in range(TM):
                        last = nc.tensor.matmul(psW[:, k, 0:224], h2[v][:, P * k:P * k + P], W["l0_rw3"][:, :], start=True, stop=True)
                    last.then_inc(sem("weights"), 1)

            pe.wait_ge(sem("ones"), 5)
            steps(pe, NM, LAST, body)

        @block.vector
        def _(dve):
            for n in range(2):
                nc.vector.memset(h2[n][64:65, :], 1.0).then_inc(sem("ones"), 1)
                nc.vector.memset(F[n][:, :, 352:F_W], 0.0).then_inc(sem("ones"), 1)
            nc.vector.memset(one[:, :], 1.0).then_inc(sem("ones"), 1)
            dve_dirs(dve)
            tt = nc.vector.tensor_tensor

            def body(i_of):
                if c := i_of(1, LAG):
                    j, u, _ = c
                    dve.wait_ge(sem("raw"), j + 1)
                    wait(dve, sem("rstd"), j - 1)
                    nc.vector.tensor_reduce(var[u][:, :], sq[u][:, :, :], AX.X, ALU.add).then_inc(sem("var"), 1)
                if c := i_of(LAG - 1, LAG):
                    j, u, _ = c
                    dve.wait_ge(sem("rstd"), j + 1)
                    wait(dve, sem("turned_h"), j - 1)
                    for n in range(2):
                        last = tt(hn[u][:, :, 1 - n, :], raw[u][:, TM * n:TM * n + TM, :], bcast(rstd[u][:, TM * n:TM * n + TM], 2, 64), ALU.mult)
                    last.then_inc(sem("hn"), 1)
                if c := i_of(1, LAG):
                    j, u, _ = c
                    dve.wait_ge(sem("var"), 2 * j + 1)
                    nc.vector.tensor_scalar(var[u][:, :], var[u][:, :], 1.0 / 64, 1e-5, ALU.mult, ALU.add).then_inc(sem("var"), 1)
                if m := i_of(PRODUCT):
                    i, u, j = m
                    dve.wait_ge(sem(f"gathered{u}"), (j + 1) * 16 * 2 * TM)
                    wait(dve, sem("products"), i)
                    tt(msg[:, :, :], gs[u][:, :, :], gd[u][:, :, :], ALU.add).then_inc(sem("msg"), 1)
                if m := i_of(LAST):
                    i, u, j = m
                    dve.wait_ge(sem("th"), i + 1)
                    nc.vector.scalar_tensor_tensor(out=xb[:, :, :], in0=th[:, :, :], scalar=1.5, in1=xb[:, :, :], op0=ALU.add,
                                                   op1=ALU.mult).then_inc(sem("leaky_a"), 1)
                if m := i_of(PRODUCT):
                    i, u, j = m
                    dve_products(nc, dve, i, psW, msg, msg, prod, dot, F[u], dirs_of(dirs, i, 0, 3), S,
                                 (sem("msg"), i + 1), (sem("lin_turned"), (i - 1) * TM))
                if m := i_of(LAST):
                    i, u, j = m
                    dve.wait_ge(sem("leaky_a"), 2 * i + 1)
                    tt(xb[:, :, :], xb[:, :, :], bcast(W["l0_adot"][:, :], 1, TM), ALU.mult).then_inc(sem("leaky_a"), 1)
                if m := i_of(CROSS):
                    i, u, j = m
                    dve.wait_ge(sem("lin_O"), (i + 1) * TM)
                    dve_cross(nc, dve, i, O[u], tmp, dirs, 128, 224, 320, S, "cross")
                if m := i_of(LAST):
                    i, u, j = m
                    dve.wait_ge(sem("leaky_a"), 2 * i + 2)
                    dve.sem_inc(sem("dve_passed"), 1)
                    nc.vector.tensor_reduce(logits[:, bass.ds(i * TM, TM), :], xb[:, :, :].rearrange("p t (h a) -> p t h a", a=8),
                                            AX.X, ALU.add).then_inc(sem("leaky"), 1)
                if m := i_of(CROSS):
                    i, u, j = m
                    wait(dve, sem("leaky"), i)
                    tt(xb[:, :, :], O[u][:, :, 0:64], bcast(W["l0_bias"][:, 0:64], 1, TM), ALU.add).then_inc(sem("xb"), 1)

            steps(dve, NM, LAST, body)


def dve_products(nc, dve, i, psW, msg, msg0, prod, dot, F, r, S, ready, free, ready0=None):
    tt = nc.vector.tensor_tensor
    v, v0 = comp(msg[:, :, C0:CX]), comp(msg0[:, :, C0:CX])
    dve.wait_ge(*ready)
    tt(comp(prod[:, :, :]), v, r, ALU.mult).then_inc(S.sem("prod"), 1)
    dve.wait_ge(S.sem("prod"), i + 1)
    nc.vector.tensor_reduce(dot[:, :, :], prod[:, :, :].rearrange("p t (d c) -> p t c d", d=3), AX.X, ALU.add)\
        .then_inc(S.sem("dot"), 1)
    dve.wait_ge(S.sem("weights"), i + 1)
    wait(dve, *free)
    tt(F[:, :, F_B:F_B + C0], psW[:, :, 64:128], msg[:, :, 0:C0], ALU.mult)
    tt(comp(F[:, :, F_X:F_X + C1V]), bcast(psW[:, :, 192:224], 2, 3), v, ALU.mult)
    if ready0:
        dve.wait_ge(*ready0)
    tt(F[:, :, F_A:F_A + C0], psW[:, :, 0:64], msg0[:, :, 0:C0], ALU.mult)
    tt(comp(F[:, :, F_C:F_C + C1V]), bcast(psW[:, :, 128:160], 2, 3), v0, ALU.mult)
    dve.wait_ge(S.sem("dot"), i + 1)
    tt(F[:, :, F_D:F_D + C1], psW[:, :, 160:192], dot[:, :, :], ALU.mult).then_inc(S.sem("products"), 1)



def sorted_maxima(nc, W, D, logits, probs, H, tag):
    with ExitStack() as ctx:
        S = Names(nc, ctx, tag)
        dst, gap = S.sb("dst", [P, ET], I32), S.sb("gap", [P, ET + 1])
        ends = S.sb("ends", [H, 2, P], I32)
        link = S.sb("link", [H, P + 1])
        thru = S.sb("thru", [H, P + 1])
        one = S.sb("one", [H, P])
        edge, edgeT = S.sb("edge", [P, H]), S.sb("edgeT", [H, P])
        run, carryT = S.sb("run", [H, P]), S.sb("carryT", [H, P])
        carry = S.sb("carry", [P, H])
        best = S.sb("best", [P, ET, H])
        psC, psR = S.ps("psC", [P, 512]), S.ps("psR", [P, 512])
        sem = S.sem
        block = ctx.enter_context(nc.Block())

        @block.sync
        def _(sp):
            sp.dma_start(dst[:, :], D["dst"]).then_inc(sem("dst"), 16)
            sp.dma_start(ends[:, 0, :], D["dst_t"][0, :].partition_broadcast(H)).then_inc(sem("ends"), 16)
            sp.dma_start(ends[:, 1, :], D["dst_t"][ET - 1, :].partition_broadcast(H)).then_inc(sem("ends"), 16)

        @block.tensor
        def _(pe):
            for n in range(2):
                pe.wait_ge(sem("edge"), n + 1)
                nc.tensor.transpose(psR[0:H, 0:P], edge[:, :], W["ident"][:, :]).then_inc(sem("edge_T"), 1)
                pe.wait_ge(sem("carry_T"), n + 1)
                nc.tensor.transpose(psC[:, 0:H], carryT[:, :], W["ident"][0:H, 0:H]).then_inc(sem("carry_ps"), 1)

        @block.vector
        def _(dve):
            count = 0

            def then(ins):
                nonlocal count
                count += 1
                ins.then_inc(sem("order"), 1)
                dve.wait_ge(sem("order"), count)

            tt, ts = nc.vector.tensor_tensor, nc.vector.tensor_scalar
            scan = nc.vector.tensor_tensor_scan
            dve.wait_ge(sem("dst"), 16)
            dve.wait_ge(sem("ends"), 32)
            nc.vector.memset(link[:, :], NBIG)
            nc.vector.memset(thru[:, :], NBIG)
            then(nc.vector.memset(gap[:, :], NBIG))
            then(tt(gap[:, 1:ET], dst[:, 1:ET], dst[:, 0:ET - 1], ALU.not_equal))
            ts(gap[:, 1:ET], gap[:, 1:ET], NBIG, None, ALU.mult)
            then(tt(link[:, 1:P], ends[:, 0, 1:P], ends[:, 1, 0:P - 1], ALU.not_equal))
            then(tt(one[:, :], ends[:, 0, :], ends[:, 1, :], ALU.not_equal))

            def across(backward):
                a = slice(0, P) if not backward else slice(1, P + 1)
                then(tt(thru[:, 0:P], one[:, :], link[:, a], ALU.add))
                then(ts(thru[:, 0:P], thru[:, 0:P], 1.0, NBIG, ALU.min, ALU.mult))
                r = slice(None, None, -1) if backward else slice(None)
                then(scan(run[:, r], thru[:, 0:P][:, r], edgeT[:, r], NBIG, ALU.add, ALU.max))
                then(nc.vector.memset(carryT[:, :], NBIG))
                if backward:
                    then(ts(carryT[:, 0:P - 1], link[:, 1:P], NBIG, None, ALU.mult))
                    tt(carryT[:, 0:P - 1], carryT[:, 0:P - 1], run[:, 1:P], ALU.add).then_inc(sem("carry_T"), 1)
                else:
                    then(ts(carryT[:, 1:P], link[:, 1:P], NBIG, None, ALU.mult))
                    tt(carryT[:, 1:P], carryT[:, 1:P], run[:, 0:P - 1], ALU.add).then_inc(sem("carry_T"), 1)

            nc.vector.memset(link[:, 0:1], 1.0)
            then(nc.vector.memset(link[:, P:P + 1], 1.0))
            for backward in (False, True):
                src = best if backward else logits
                r = slice(None, None, -1) if backward else slice(None)
                g = gap[:, 1:ET + 1][:, r] if backward else gap[:, 0:ET]
                for h in range(H):
                    last = scan(probs[:, r, h], g, src[:, r, h], NBIG, ALU.add, ALU.max)
                then(last)
                end = 0 if backward else ET - 1
                then(nc.vector.tensor_copy(edge[:, :], probs[:, end, :]))
                dve.sem_inc(sem("edge"), 1)
                dve.wait_ge(sem("edge_T"), 1 + backward)
                then(nc.vector.tensor_copy(edgeT[:, :], psR[0:H, 0:P]))
                across(backward)
                dve.wait_ge(sem("carry_ps"), 1 + backward)
                then(nc.vector.tensor_copy(carry[:, :], psC[:, 0:H]))
                then(nc.vector.memset(gap[:, ET:ET + 1] if backward else gap[:, 0:1], 0.0))
                out = probs if backward else best
                for h in range(H):
                    last = scan(out[:, r, h], g, src[:, r, h], carry[:, h:h + 1], ALU.add, ALU.max)
                then(last)


def unsorted_maxima(nc, W, D, logits, probs, H, tag):
    with ExitStack() as ctx:
        S = Names(nc, ctx, tag)
        sem = S.sem
        T = scatter_tensors(S, H)
        kcol, krow, row = T["kcol"][0], T["krow"][0], T["row"][0]
        same, early, count, away = T["same"][0], T["early"], T["count"], T["away"]
        lt, aT = S.sb("lt", [P, TM, H]), S.sb("aT", [H, TM * P])
        pick = S.sb("pick", [H, H, P])
        low, spread = S.sb("low", [P, ROWS // P * H]), S.sb("spread", [P, H, P])
        best, old = S.sb("best", [P, TM, H]), S.sb("old", [P, TM, H])
        found = S.sb("found", [P, TM, TM, H])
        psT, psB = S.ps("psT", [H, TM * P]), S.ps("psB", [P, H * P])
        step, key, put, got = sem("step"), sem("keys"), sem("put"), sem("got")
        stages = ["tile", "turn", "move", "same"] + [f"{n}{k}" for k in range(TM) for n in ("spread", "best")] + ["merge", "put"]
        L = len(stages)
        block = ctx.enter_context(nc.Block())

        def at(eng, name, i):
            eng.wait_ge(step, 1 + i * L + stages.index(name))

        def unsorted(eng):
            return eng.If(eng.value_load(W["unsorted"][0:1, 0:1], min_val=0, max_val=1) == 1)

        def again(eng, i):
            eng.wait_ge(step, 1 + NM * L + i)

        @block.sync
        def _(sp):
            with unsorted(sp):
                sp.wait_ge(sem("low"), 1)
                for k in range(TM):
                    sp.dma_start(D["max"][H][k].rearrange("(p t) c -> p (t c)", p=P), low[:, :]).then_inc(sem("filled"), 16)
                sp.wait_ge(sem("filled"), 16 * TM)
                sp.sem_inc(step, 1)
                with sp.Fori(0, NM) as i:
                    wait_apart(sp, step, 1 + i * L, sem("sp_passed"))
                    sp.dma_start(kcol[:, :], D["dst"][:, bass.ds(i * TM, TM)]).then_inc(key, 16)
                    sp.dma_start(krow[:, :, :], D["dst_t"][bass.ds(i * TM, TM), :].partition_broadcast(P)).then_inc(key, 16)
                with sp.Fori(0, NM) as i:
                    wait_apart(sp, step, 1 + NM * L + i, sem("sp_passed"))
                    sp.dma_start(kcol[:, :], D["dst"][:, bass.ds(i * TM, TM)]).then_inc(sem("again"), 16)

        @block.tensor
        def _(pe):
            passed = sem("pe_passed")
            with unsorted(pe):
                with pe.Fori(0, NM) as i:
                    wait_apart(pe, step, 1 + i * L + stages.index("turn"), passed)
                    for k in range(TM):
                        last = nc.tensor.transpose(psT[:, P * k:P * k + P], lt[:, k, :], W["ident"][:, :])
                    last.then_inc(step, 1)
                    for k in range(TM):
                        wait_apart(pe, step, 1 + i * L + stages.index(f"spread{k}"), passed)
                        for h in range(H):
                            last = nc.tensor.matmul(psB[:, P * h:P * h + P], pick[:, h, :], aT[:, P * k:P * k + P], start=True, stop=True)
                        last.then_inc(step, 1)

        @block.scalar
        def _(act):
            with unsorted(act):
                with act.Fori(0, NM) as i:
                    at(act, "move", i)
                    nc.scalar.activation(aT[:, :], psT[:, :], ACT.Copy).then_inc(step, 1)

        @block.gpsimd
        def _(pool):
            passed = sem("pool_passed")
            with unsorted(pool):
                with pool.Fori(0, NM) as i:
                    wait_apart(pool, key, (i + 1) * 32, passed)
                    wait_apart(pool, step, 1 + i * L + stages.index("same"), passed)
                    for k in range(TM):
                        pool.indirect_dma_start(old[:, k, :], None, D["max"][H][k], bass.IndirectOffsetOnAxis(kcol[:, k:k + 1], 0)).then_inc(got, 16)
                    wait_apart(pool, step, 1 + i * L + stages.index("put"), passed)
                    for k in range(TM):
                        pool.indirect_dma_start(D["max"][H][k], bass.IndirectOffsetOnAxis(row[:, k:k + 1], 0), old[:, k, :], None).then_inc(put, 16)
                    wait_apart(pool, put, (i + 1) * 16 * TM, passed)
                    pool.sem_inc(step, 1)
                with pool.Fori(0, NM) as i:
                    wait_apart(pool, sem("again"), (i + 1) * 16, passed)
                    for n in range(TM):
                        for k in range(TM):
                            pool.indirect_dma_start(found[:, n, k, :], None, D["max"][H][n], bass.IndirectOffsetOnAxis(kcol[:, k:k + 1], 0))\
                                .then_inc(sem("found"), 16)

        @block.vector
        def _(dve):
            tt, ts = nc.vector.tensor_tensor, nc.vector.tensor_scalar
            inner = sem("inner")
            with unsorted(dve):
                nc.vector.tensor_copy(pick[:, :, :], bcast(W["ident"][0:H, 0:H], 2, P)).then_inc(inner, 1)
                nc.vector.memset(low[:, :], NBIG).then_inc(sem("low"), 1)
                with dve.Fori(0, NM) as i:
                    links = 0

                    def then(ins):
                        nonlocal links
                        links += 1
                        ins.then_inc(inner, 1)
                        dve.wait_ge(inner, 1 + i * 6 + links)

                    at(dve, "tile", i)
                    nc.vector.tensor_copy(lt[:, :, :], logits[:, bass.ds(i * TM, TM), :]).then_inc(step, 1)
                    at(dve, "same", i)
                    dve.wait_ge(key, (i + 1) * 32)
                    then(tt(same[:, :, :], krow[:, :, :], bcast(kcol[:, :], 2, P), ALU.is_equal))
                    dve.sem_inc(sem("dve_passed"), 1)
                    for k in range(TM):
                        last = nc.vector.tensor_tensor_reduce(early[:, k, :], same[:, k, :], W["tri"][:, :], 1.0, 0.0, ALU.mult, ALU.add,
                                                              count[:, k:k + 1])
                    then(last)
                    then(tt(away[:, :], W["spare"][:, 0:1].to_broadcast([P, TM]), kcol[:, :], ALU.subtract))
                    then(nc.vector.scalar_tensor_tensor(out=away[:, :], in0=count[:, :], scalar=1.0, in1=away[:, :], op0=ALU.min, op1=ALU.mult))
                    then(tt(row[:, :], away[:, :], kcol[:, :], ALU.add))
                    then(ts(same[:, :, :], same[:, :, :], -1.0, -NBIG, ALU.add, ALU.mult))
                    dve.sem_inc(step, 1)
                    for k in range(TM):
                        at(dve, f"best{k}", i)
                        tt(spread[:, :, :], bcast(same[:, k, :], 1, H), psB[:, :].rearrange("p (h q) -> p h q", h=H), ALU.add)\
                            .then_inc(sem("masked"), 1)
                        dve.wait_ge(sem("masked"), i * TM + k + 1)
                        nc.vector.tensor_reduce(best[:, k, :], spread[:, :, :], AX.X, ALU.max).then_inc(step, 1)
                    at(dve, "merge", i)
                    dve.wait_ge(got, (i + 1) * 16 * TM)
                    tt(old[:, :, :], old[:, :, :], best[:, :, :], ALU.max).then_inc(step, 1)
                with dve.Fori(0, NM) as i:
                    dve.wait_ge(sem("found"), (i + 1) * 16 * TM * TM)
                    tt(found[:, 0:2, :, :], found[:, 0:2, :, :], found[:, 2:4, :, :], ALU.max).then_inc(sem("half"), 1)
                    dve.wait_ge(sem("half"), i + 1)
                    tt(probs[:, bass.ds(i * TM, TM), :], found[:, 0, :, :], found[:, 1, :, :], ALU.max).then_inc(step, 1)


def softmax_weights(nc, W, logits, probs, H, tag):
    with ExitStack() as ctx:
        S = Names(nc, ctx, tag)
        sem = S.sem
        best, power = S.sb("best", [P, ET, H]), S.sb("power", [P, ET, H], I32)
        block = ctx.enter_context(nc.Block())
        chunks = [slice(a, a + ET // 4) for a in range(0, ET, ET // 4)]

        @block.scalar
        def _(act):
            for n, c in enumerate(chunks):
                act.wait_ge(sem("rest"), 2 * n + 2)
                nc.scalar.activation(best[:, c, :], probs[:, c, :], ACT.Tanh, scale=0.5).then_inc(sem("tanh"), 1)

        @block.vector
        def _(dve):
            count = 0

            def then(ins):
                nonlocal count
                count += 1
                ins.then_inc(sem("order"), 1)
                dve.wait_ge(sem("order"), count)

            tt, ts = nc.vector.tensor_tensor, nc.vector.tensor_scalar
            ln2_high = 0.693359375
            ln2_low = float(np.log(2.0) - ln2_high)
            for n_chunk, c in enumerate(chunks):
                x, n, whole = probs[:, c, :], logits[:, c, :], power[:, c, :]
                then(tt(x, n, x, ALU.subtract))
                then(ts(whole, x, -87.0, float(np.log2(np.e)), ALU.max, ALU.mult))
                then(nc.vector.tensor_copy(n, whole))
                nc.vector.scalar_tensor_tensor(out=x, in0=n, scalar=-ln2_high, in1=x, op0=ALU.mult, op1=ALU.add).then_inc(sem("rest"), 1)
                dve.wait_ge(sem("rest"), 2 * n_chunk + 1)
                nc.vector.scalar_tensor_tensor(out=x, in0=n, scalar=-ln2_low, in1=x, op0=ALU.mult, op1=ALU.add).then_inc(sem("rest"), 1)
                then(ts(whole, n, 127.0, 2.0 ** 23, ALU.add, ALU.mult))
            for n_chunk, c in enumerate(chunks):
                x, t = probs[:, c, :], best[:, c, :]
                dve.wait_ge(sem("tanh"), n_chunk + 1)
                then(ts(x, t, -1.0, 1.0, ALU.mult, ALU.add))
                then(nc.vector.reciprocal(x, x))
                then(nc.vector.scalar_tensor_tensor(out=x, in0=t, scalar=1.0, in1=x, op0=ALU.add, op1=ALU.mult))
                then(tt(x, x, power[:, c, :].bitcast(F32), ALU.mult))



def attention_sums(nc, W, D, probs, layer, H, tag):
    HS, HV = C0 // H, C1 // H
    width = CX + H
    acc = D["acc"][layer]
    with ExitStack() as ctx:
        S = Names(nc, ctx, tag)
        T = scatter_tensors(S, width)
        val = [S.sb(f"val{u}", [P, TM, CX]) for u in range(2)]
        wv = [S.sb(f"wv{u}", [P, TM, width]) for u in range(2)]
        pb = [S.sb(f"pb{u}", [P, TM, H]) for u in range(2)]
        psS = S.ps("psS", [P, 4, 512])
        banks = [psS[:, k, 0:width] for k in range(4)]
        sem = S.sem
        LAST = 2
        block = ctx.enter_context(nc.Block())

        @block.sync
        def _(sp):
            def body(i_of):
                if m := i_of(0):
                    i, u, j = m
                    wait_apart(sp, sem("weighted"), i - 1, S.sem("sp_passed"))
                    sp.dma_start(val[u][:, :, :], D["val"][:, bass.ds(i * TM, TM), :]).then_inc(sem(f"val{u}"), 16)
                    sp_keys(sp, i, u, j, T, D, "dst", S)

            steps(sp, NM, LAST, body)

        @block.vector
        def _(dve):
            tt = nc.vector.tensor_tensor

            def body(i_of):
                if m := i_of(1):
                    i, u, j = m
                    wait(dve, sem("weighted"), i - 1)
                    nc.vector.tensor_copy(pb[u][:, :, :], probs[:, bass.ds(i * TM, TM), :]).then_inc(sem("pb"), 1)
                    dve_rows(nc, dve, i, u, j, T, W, S)
                    dve.wait_ge(sem(f"val{u}"), (j + 1) * 16)
                    dve.wait_ge(sem("pb"), i + 1)
                    wait(dve, sem("summed"), (i - 1) * TM)
                    tt(wv[u][:, :, 0:C0].rearrange("p t (h c) -> p t h c", h=H), val[u][:, :, 0:C0].rearrange("p t (h c) -> p t h c", h=H),
                       bcast(pb[u][:, :, :], 3, HS), ALU.mult)
                    for d in range(3):
                        a = C0 + C1 * d
                        tt(wv[u][:, :, a:a + C1].rearrange("p t (h c) -> p t h c", h=H),
                           val[u][:, :, a:a + C1].rearrange("p t (h c) -> p t h c", h=H), bcast(pb[u][:, :, :], 3, HV), ALU.mult)
                    nc.vector.tensor_copy(wv[u][:, :, CX:width], pb[u][:, :, :]).then_inc(sem("weighted"), 1)

            steps(dve, NM, LAST, body)

        @block.tensor
        def _(pe):
            def body(i_of):
                if m := i_of(1):
                    i, u, j = m
                    pe_sums(nc, pe, i, u, T, wv[u], banks, S, (sem("weighted"), i + 1))

            steps(pe, NM, LAST, body)

        @block.scalar
        def _(act):
            def body(i_of):
                if m := i_of(1):
                    act_sums(nc, act, *m, T, banks, S)

            steps(act, NM, LAST, body)

        @block.gpsimd
        def _(pool):
            def body(i_of):
                if m := i_of(2):
                    pool_scatter(nc, pool, *m, T, acc, S)

            steps(pool, NM, LAST, body)
            for k in range(TM):
                pool.wait_ge(sem(f"added{k}"), 16 * NM)



def convolution_edges(nc, W, D, layer, gather_by, sum_by, tag):
    cross = layer == 1
    kin, wn = (64, 224) if cross else (8, 192)
    per = 128 if cross else 96
    width = 96 + 3 * per
    acc = D["acc"][layer]
    with ExitStack() as ctx:
        S = Names(nc, ctx, tag)
        if cross:
            dirs, sp_dirs, dve_dirs = load_directions(nc, S, D, W["norm"][1])
            Y = lambda i, a, b: dirs_of(dirs, i, a, b)
        else:
            y = S.sb("y", [P, ET, 4])
            Y = lambda i, a, b: bcast(y[:, bass.ds(i * TM, TM), 1 + a:1 + b], 3, C1)
        T = scatter_tensors(S, width)
        es = [S.sb(f"es{u}", [kin, ME]) for u in range(2)]
        ix = [S.sb(f"ix{u}", [P, 1, TM], I32) for u in range(2)]
        g = [S.sb(f"g{u}", [P, TM, CX]) for u in range(2)]
        g0 = S.sb("feat_y0", [P, TM, CX])
        h = [S.sb(f"h{u}", [64, ME]) for u in range(2)]
        prod, dot, bs = S.sb("prod", [P, TM, C1V]), S.sb("dot", [P, TM, C1]), S.sb("bs", [P, TM, C0])
        xw, tmp = S.sb("xw", [P, TM, C1V]), S.sb("tmp", [P, TM, C1V])
        rows = [S.sb(f"rows{u}", [P, TM, width]) for u in range(2)]
        psH, psS = S.ps("psH", [64, 512]), S.ps("psS", [P, 2, 512])
        psWs = [S.ps(f"psW{u}", [P, TM, 256]) for u in range(2)]
        banks = [psS[:, k, 0:width] for k in range(2)]
        sem = S.sem
        LAST = 3
        source = D["es64"] if cross else D["es8"]
        block = ctx.enter_context(nc.Block())

        @block.sync
        def _(sp):
            if cross:
                sp_dirs(sp)
            else:
                sp.dma_start(y[:, :, :], D["edge_attr_4"].rearrange("p (t c) -> p t c", c=4)).then_inc(sem("y"), 16)

            def body(i_of):
                if m := i_of(0):
                    i, u, j = m
                    wait_apart(sp, sem("pre"), i - 1, S.sem("sp_passed"))
                    sp.dma_start(es[u][:, :], source[0:kin, bass.ds(i * ME, ME)]).then_inc(sem(f"es{u}"), 16)
                    sp_indices(sp, i, u, j, ix, D, (gather_by,), S, [sem("gathered0"), sem("gathered1")])
                    sp_keys(sp, *m, T, D, sum_by, S)

            steps(sp, NM, LAST, body)

        @block.gpsimd
        def _(pool):
            def body(i_of):
                if m := i_of(LAST):
                    pool_scatter(nc, pool, *m, T, acc, S)
                if m := i_of(0):
                    pool_gather(nc, pool, *m, ix, (D["tab_src"],), (g,), S, (sem("products"), m[0] - 1))

            steps(pool, NM, LAST, body)
            for k in range(TM):
                pool.wait_ge(sem(f"added{k}"), 16 * NM)

        @block.tensor
        def _(pe):
            passed = sem("pe_passed")

            def body(i_of):
                if m := i_of(0):
                    i, u, j = m
                    wait_apart(pe, sem(f"es{u}"), (j + 1) * 16, passed)
                    wait_apart(pe, sem("h"), i, passed)
                    nc.tensor.matmul(psH[:, :], W[f"l{layer}_fc1"][:, :], es[u][:, :], start=True, stop=True).then_inc(sem("pre"), 1)
                if m := i_of(2):
                    i, u, j = m
                    pe_sums(nc, pe, i, u, T, rows[u], banks, S, (sem("products"), i + 1))
                if m := i_of(0):
                    i, u, j = m
                    wait_apart(pe, sem("h"), i + 1, passed)
                    wait_apart(pe, sem("products"), i - 1, passed)
                    for k in range(TM):
                        last = nc.tensor.matmul(psWs[u][:, k, 0:wn], h[u][:, P * k:P * k + P], W[f"l{layer}_fc2"][:, :], start=True, stop=True)
                    last.then_inc(sem("weights"), 1)

            steps(pe, NM, LAST, body)

        @block.scalar
        def _(act):
            if not cross:
                act.wait_ge(sem("y"), 16)

            def body(i_of):
                if m := i_of(0):
                    i, u, j = m
                    act.wait_ge(sem("pre"), i + 1)
                    wait(act, sem("weights"), i - 1)
                    nc.scalar.activation(h[u][:, :], psH[:, :], ACT.Relu if cross else ACT.Silu,
                                         scale=1.0 if cross else 1.0 / float(np.sqrt(8.0))).then_inc(sem("h"), 1)
                if m := i_of(2):
                    act_sums(nc, act, *m, T, banks, S)

            steps(act, NM, LAST, body)

        @block.vector
        def _(dve):
            if cross:
                dve_dirs(dve)
            else:
                dve.wait_ge(sem("y"), 16)
            tt = nc.vector.tensor_tensor

            def body(i_of):
                if m := i_of(1):
                    i, u, j = m
                    psW = psWs[u]
                    dve.wait_ge(sem(f"gathered{u}"), (j + 1) * 16 * TM)
                    wait(dve, sem("products"), i)
                    R = rows[u]
                    s, v = g[u][:, :, 0:C0], comp(g[u][:, :, C0:CX])
                    D3 = R[:, :, 96:width].rearrange("p t (d c) -> p t d c", d=3)
                    if cross:
                        s0, v0 = s, v
                    else:
                        y0 = y[:, bass.ds(i * TM, TM), 0:1].rearrange("p t c -> p (t c)")
                        tt(g0[:, :, :], g[u][:, :, :], bcast(y0, 2, CX), ALU.mult).then_inc(sem("g0"), 1)
                        s0, v0 = g0[:, :, 0:C0], comp(g0[:, :, C0:CX])
                    tt(comp(prod[:, :, :]), v, Y(i, 0, 3), ALU.mult).then_inc(sem("prod"), 1)
                    dve.wait_ge(sem("weights"), i + 1)
                    tt(bs[:, :, :], psW[:, :, 64:128], s, ALU.mult)
                    if cross:
                        tt(comp(xw[:, :, :]), bcast(psW[:, :, 192:224], 2, 3), v, ALU.mult)
                    dve.wait_ge(sem("prod"), i + 1)
                    nc.vector.tensor_reduce(dot[:, :, :], prod[:, :, :].rearrange("p t (d c) -> p t c d", d=3), AX.X, ALU.add)\
                        .then_inc(sem("dot"), 1)
                    wait(dve, sem("summed"), (i - 1) * TM)
                    if not cross:
                        dve.wait_ge(sem("g0"), i + 1)
                    tt(R[:, :, 0:C0], psW[:, :, 0:64], s0, ALU.mult)
                    tt(D3[:, :, :, 64:96], bcast(psW[:, :, 128:160], 2, 3), v0, ALU.mult)
                    dve.wait_ge(sem("dot"), i + 1)
                    tt(R[:, :, C0:96], psW[:, :, 160:192], dot[:, :, :], ALU.mult)
                    for half in range(2):
                        c = slice(C1 * half, C1 * half + C1)
                        last = tt(D3[:, :, :, c], bcast(bs[:, :, c], 2, 3), Y(i, 0, 3), ALU.mult)
                    if cross:
                        X = lambda a, b: comp(xw[:, :, C1 * a:C1 * b], b - a)
                        Z = lambda a, b: comp(tmp[:, :, C1 * a:C1 * b], b - a)
                        tt(D3[:, :, 0:2, 96:128], X(1, 3), Y(i, 2, 4), ALU.mult)
                        tt(D3[:, :, 2:3, 96:128], X(0, 1), Y(i, 4, 5), ALU.mult)
                        tt(Z(0, 1), X(2, 3), Y(i, 1, 2), ALU.mult)
                        tt(Z(1, 3), X(0, 2), Y(i, 2, 4), ALU.mult).then_inc(sem("crossed"), 1)
                        dve.wait_ge(sem("crossed"), i + 1)
                        last = tt(D3[:, :, :, 96:128], D3[:, :, :, 96:128], comp(tmp[:, :, :]), ALU.subtract)
                    last.then_inc(sem("products"), 1)
                    dve_rows(nc, dve, i, u, j, T, W, S)

            steps(dve, NM, LAST, body)



def layer2_edges(nc, W, D, logits):
    JOIN, PRODUCT, FIRST, CROSS, SECOND_IN, SECOND, CROSS2, LAST = 1, 2, 3, 4, 5, 6, 7, 8
    with ExitStack() as ctx:
        S = Names(nc, ctx, "e2")
        sem = S.sem
        pair = lambda name, shape: [S.sb(f"{name}{u}", shape) for u in range(2)]
        y, dirs = S.sb("y", [P, ET, 4]), S.sb("dirs", [P, ET, 5])
        es = pair("es", [16, ME])
        ix = [S.sb(f"ix{u}", [P, 2, TM], I32) for u in range(2)]
        gs, gd, msg = pair("gs", [P, TM, CX]), pair("gd", [P, TM, CX]), S.sb("msg", [P, TM, CX])
        msg0 = S.sb("msg_y0", [P, TM, CX])
        prod, dot, prod2 = S.sb("prod", [P, TM, C1V]), S.sb("dot", [P, TM, C1]), S.sb("prod2", [P, TM, C1V])
        F, F2 = pair("F", [P, TM, F_W]), pair("F2", [P, TM, F_W])
        FT, FT2 = S.sb("FT", [P, 2, F_W]), S.sb("FT2", [P, 2, F_W])
        tmp, tmp2 = S.sb("tmp", [P, 3, TM, C1V]), S.sb("tmp2", [P, 3, TM, C1V])
        O_W, O2_W = 352, 288
        O, O2 = pair("O", [P, TM, O_W]), pair("O2", [P, TM, O2_W])
        lk, valT, gate = S.sb("lk", [P, TM, 64]), S.sb("valT", [64, ME]), S.sb("gate", [P, TM, C1])
        psW, psF, psO = S.ps("psW", [P, TM, 256]), S.ps("psF", [P, 2, 512]), S.ps("psO", [P, 2, 512])
        psV, psG = S.ps("psV", [64, 512]), S.ps("psG", [P, 512])
        block = ctx.enter_context(nc.Block())

        @block.sync
        def _(sp):
            sp.dma_start(y[:, :, :], D["edge_attr_4"].rearrange("p (t c) -> p t c", c=4)).then_inc(sem("y"), 16)

            def body(i_of):
                if m := i_of(0):
                    i, u, j = m
                    sp_indices(sp, i, u, j, ix, D, ("src", "dst"), S, [sem("gathered0"), sem("gathered1")])
                    wait_apart(sp, sem("weights"), i - 1, sem("sp_passed"))
                    sp.dma_start(es[u][:, :], D["es16"][:, bass.ds(i * ME, ME)]).then_inc(sem(f"es{u}"), 16)
                if m := i_of(LAST):
                    i, u, j = m
                    wait_apart(sp, sem("cross2_done"), i + 1, sem("sp_passed"))
                    sp.dma_start(D["val"][:, bass.ds(i * TM, TM), :], O2[u][:, :, 0:CX]).then_inc(sem(f"stored{u}"), 16)

            steps(sp, NM, LAST, body)
            for u in range(2):
                sp.wait_ge(sem(f"stored{u}"), 16 * (NM // 2))

        @block.gpsimd
        def _(pool):
            def body(i_of):
                if m := i_of(0):
                    pool_gather(nc, pool, *m, ix, (D["tab_src"], D["tab_dst"]), (gs, gd), S, (sem("msg"), m[0] - 1))

            steps(pool, NM, LAST, body)

        @block.scalar
        def _(act):
            act.wait_ge(sem("y"), 16)

            def times_y0(to, src, i, k):
                return nc.scalar.activation(to[:, k, :], src[:, k, :], ACT.Copy, scale=y[:, bass.ds(i * TM + k, 1), 0:1].rearrange("p t c -> p (t c)"))

            def body(i_of):
                def passed_on():
                    if m := i_of(SECOND_IN):
                        i, u, j = m
                        wait(act, sem("lin2_turned"), (i - 1) * TM)
                        nc.scalar.activation(F2[u][:, :, F_B:F_B + C0], O[u][:, :, 64:128], ACT.Sigmoid).then_inc(sem("sig"), 1)
                        act.wait_ge(sem("sig"), i + 1)

                def times_y0_beside(k):
                    if m := i_of(SECOND_IN):
                        i, u, j = m
                        done = times_y0(F2[u][:, :, F_A:F_A + C0], F2[u][:, :, F_B:F_B + C0], i, k)
                        if k == TM - 1:
                            done.then_inc(sem("second_in"), 1)

                def raw_values():
                    if m := i_of(CROSS):
                        act.wait_ge(sem("val_T"), m[0] + 1)
                        wait(act, sem("gate_in"), m[0])
                        nc.scalar.activation(valT[:, :], psV[:, :], ACT.Copy).then_inc(sem("valT"), 1)

                def gates():
                    if m := i_of(CROSS):
                        act.wait_ge(sem("gate_in"), m[0] + 1)
                        wait(act, sem("gated"), m[0])
                        nc.scalar.activation(gate[:, :, :], psG[:, 0:P].rearrange("p (t c) -> p t c", t=TM), ACT.Sigmoid).then_inc(sem("gate"), 1)

                if m := i_of(FIRST):
                    i, u, j = m

                    def free_O():
                        raw_values()
                        passed_on()
                        wait(act, sem("gated"), i - 1)
                        wait(act, sem("leaky"), 2 * i - 2)
                        wait(act, sem("val_T"), i - 1)

                    act_linear(nc, act, i, FT, psF, O[u], psO, O_W, S, "lin", free_O, times_y0_beside)
                else:
                    raw_values()
                    passed_on()
                    for k in range(TM):
                        times_y0_beside(k)
                if m := i_of(JOIN):
                    i, u, j = m
                    act.wait_ge(sem("msg"), i + 1)
                    wait(act, sem("products"), i)
                    for k in range(TM):
                        last = times_y0(msg0, msg, i, k)
                    last.then_inc(sem("msg_y0"), 1)
                if m := i_of(SECOND):
                    i, u, j = m
                    wait(act, sem(f"stored{u}"), j * 16)
                    act_linear(nc, act, i, FT2, psF, O2[u], psO, O2_W, S, "lin2", gates)
                else:
                    gates()
            steps(act, NM, LAST, body)

        @block.tensor
        def _(pe):
            passed = sem("pe_passed")
            GAP = SECOND - FIRST

            def body(i_of):
                def turn_values():
                    if m := i_of(CROSS):
                        i, u, j = m
                        wait_apart(pe, sem("lin_O"), (i + 1) * TM, passed)
                        wait_apart(pe, sem("valT"), i, passed)
                        for k in range(TM):
                            last = nc.tensor.transpose(psV[:, P * k:P * k + P], O[u][:, k, 64:128], W["ident"][:, :])
                        last.then_inc(sem("val_T"), 1)

                def gates():
                    if m := i_of(CROSS):
                        i, u, j = m
                        wait_apart(pe, sem("valT"), i + 1, passed)
                        wait_apart(pe, sem("gate"), i, passed)
                        for k in range(TM):
                            last = nc.tensor.matmul(psG[:, C1 * k:C1 * k + C1], valT[:, P * k:P * k + P], W["l2_wg"][:, :], start=True, stop=True)
                        last.then_inc(sem("gate_in"), 1)

                if m := i_of(FIRST):
                    i, u, j = m
                    wait_apart(pe, sem("products"), i + 1, passed)
                    before = lambda own, other: (lambda k: (sem(own), i * TM + k - 1) if k > 1 else (sem(other), (i - GAP) * TM))
                    pe_linear(nc, pe, i, F[u], FT, psF, psO, W, "l2", 128, W["ident"], S, "lin",
                              before("lin_FT", "lin2_FT"), before("lin_O", "lin2_O"), turn_values)
                else:
                    turn_values()
                if m := i_of(JOIN):
                    i, u, j = m
                    wait_apart(pe, sem(f"es{u}"), (j + 1) * 16, passed)
                    wait_apart(pe, sem("products"), i, passed)
                    for k in range(TM):
                        last = nc.tensor.matmul(psW[:, k, 0:224], es[u][:, P * k:P * k + P], W["l2_rbf"][:, :], start=True, stop=True)
                    last.then_inc(sem("weights"), 1)
                if m := i_of(SECOND):
                    i, u, j = m
                    wait_apart(pe, sem("products2"), i + 1, passed)
                    wait_apart(pe, sem("second_in"), i + 1, passed)
                    ahead = (min(i + GAP + 1, NM) if isinstance(i, int) else i + GAP + 1) * TM
                    after = lambda own, other: (lambda k: (sem(own), i * TM + k - 1) if k > 1 else (sem(other), ahead))
                    pe_linear(nc, pe, i, F2[u], FT2, psF, psO, W, "l2b", 64, W["ident"], S, "lin2",
                              after("lin2_FT", "lin_FT"), after("lin2_O", "lin_O"), gates)
                else:
                    gates()

            pe.wait_ge(sem("padded"), 4)
            steps(pe, NM, LAST, body)

        @block.vector
        def _(dve):
            tt = nc.vector.tensor_tensor
            for f in F + F2:
                nc.vector.memset(f[:, :, 352:F_W], 0.0).then_inc(sem("padded"), 1)
            dve.wait_ge(sem("y"), 16)
            nc.vector.tensor_copy(dirs[:, :, 0:3], y[:, :, 1:4]).then_inc(sem("dirs"), 1)
            nc.vector.tensor_copy(dirs[:, :, 3:5], y[:, :, 1:3]).then_inc(sem("dirs"), 1)
            dve.wait_ge(sem("dirs"), 2)

            def body(i_of):
                if m := i_of(PRODUCT):
                    i, u, j = m
                    wait(dve, sem("dot"), i)
                    wait(dve, sem("products"), i)
                    dve_products(nc, dve, i, psW, msg, msg0, prod, dot, F[u], dirs_of(dirs, i, 0, 3), S,
                                 (sem("msg"), i + 1), (sem("lin_turned"), (i - 1) * TM), (sem("msg_y0"), i + 1))
                if m := i_of(SECOND_IN):
                    i, u, j = m
                    dve.wait_ge(sem("gate"), i + 1)
                    dve.wait_ge(sem("cross_done"), i + 1)
                    wait(dve, sem("lin2_turned"), (i - 1) * TM)
                    V2 = comp(F2[u][:, :, F_X:F_X + C1V])
                    tt(V2, comp(O[u][:, :, 128:224]), bcast(gate[:, :, :], 2, 3), ALU.mult).then_inc(sem("gated"), 1)
                if m := i_of(JOIN):
                    i, u, j = m
                    dve.wait_ge(sem(f"gathered{u}"), (j + 1) * 16 * 2 * TM)
                    wait(dve, sem("products"), i)
                    wait(dve, sem("msg_y0"), i)
                    tt(msg[:, :, :], gs[u][:, :, :], gd[u][:, :, :], ALU.add).then_inc(sem("msg"), 1)
                if m := i_of(CROSS):
                    i, u, j = m
                    dve.wait_ge(sem("lin_O"), (i + 1) * TM)
                    wait(dve, sem("logit"), i)
                    a = O[u][:, :, 0:64]
                    nc.vector.scalar_tensor_tensor(out=lk[:, :, :], in0=a, scalar=0.2, in1=a, op0=ALU.mult, op1=ALU.max)\
                        .then_inc(sem("leaky"), 1)
                if m := i_of(SECOND_IN):
                    i, u, j = m
                    dve.wait_ge(sem("gated"), i + 1)
                    wait(dve, sem("products2"), i)
                    tt(comp(prod2[:, :, :]), comp(F2[u][:, :, F_X:F_X + C1V]), dirs_of(dirs, i, 0, 3), ALU.mult).then_inc(sem("prod2"), 1)
                    y0 = y[:, bass.ds(i * TM, TM), 0:1].rearrange("p t c -> p (t c)")
                    tt(F2[u][:, :, F_C:F_C + C1V], F2[u][:, :, F_X:F_X + C1V], bcast(y0, 2, C1V), ALU.mult)
                if m := i_of(CROSS):
                    i, u, j = m
                    dve_cross(nc, dve, i, O[u], tmp, dirs, 128, 224, 320, S, "cross")
                    dve.wait_ge(sem("leaky"), 2 * i + 1)
                    tt(lk[:, :, :], lk[:, :, :], bcast(W["l2_adot"][:, :], 1, TM), ALU.mult).then_inc(sem("leaky"), 1)
                if m := i_of(SECOND_IN):
                    i, u, j = m
                    dve.wait_ge(sem("prod2"), i + 1)
                    nc.vector.tensor_reduce(F2[u][:, :, F_D:F_D + C1], prod2[:, :, :].rearrange("p t (d c) -> p t c d", d=3), AX.X,
                                            ALU.add).then_inc(sem("products2"), 1)
                if m := i_of(CROSS2):
                    i, u, j = m
                    dve.wait_ge(sem("lin2_O"), (i + 1) * TM)
                    dve_cross(nc, dve, i, O2[u], tmp2, dirs, 64, 160, 256, S, "cross2")
                if m := i_of(CROSS):
                    i, u, j = m
                    dve.wait_ge(sem("leaky"), 2 * i + 2)
                    dve.sem_inc(sem("dve_passed"), 1)
                    nc.vector.tensor_reduce(logits[:, bass.ds(i * TM, TM), :], lk[:, :, :].rearrange("p t (h a) -> p t h a", a=16),
                                            AX.X, ALU.add).then_inc(sem("logit"), 1)

            steps(dve, NM, LAST, body)



class Group:

    def __init__(self, S, n, post, pre, n_tab, H):
        self.n = n
        sb = lambda name, shape, dt=F32: S.sb(f"{name}_{n}", shape, dt)
        self.done, self.loaded, self.stored = (S.sem(f"{name}_{n}") for name in ("done", "loaded", "stored"))
        self.part, self.low, self.copied = (S.sem(f"{name}_{n}") for name in ("part", "low", "copied"))
        self.cen, self.sqr, self.nrm, self.res, self.out = (sb(name, [P, G, CX]) for name in ("cen", "sqr", "nrm", "res", "out"))
        self.st, self.attr = sb("st", [P, 2, G]), sb("attr", [P, 2, G])
        self.sT, self.vT = sb("sT", [65, G * P]), sb("vT", [96, G * P])
        self.psA, self.psB = S.ps(f"psA_{n}", [P, G * 256]), S.ps(f"psB_{n}", [P, G * 256])
        self.second = self.psA[:, G * P:2 * G * P]
        self.wideA, self.wideB = (t[:, :].rearrange("p (t c) -> p t c", t=G) for t in (self.psA, self.psB))
        if post is not None:
            self.ag = [sb(f"ag{k}", [P, G, ACC_W[post]]) for k in range(TM)]
        if post in (0, 2):
            self.den, self.ratio = sb("den", [P, G, H]), sb("ratio", [P, G, H])
        if post == 0:
            self.th, self.fv = sb("th", [P, G, 64]), sb("fv", [P, G, 192])
            self.sc, self.scT = sb("sc", [P, G, P]), sb("scT", [P, G * P])
            self.fvTa, self.fvTb = sb("fvTa", [P, G * P]), sb("fvTb", [64, G * P])
        if post == 1:
            self.th = sb("th", [P, G, C1])
        if post in (1, 3):
            self.gT = [sb(f"gT{d}", [P if post == 1 else 96, G * P]) for d in range(3)]
            self.aT = sb("aT", [96, G * P])
        if post == 3:
            self.ang, self.whole_t = sb("ang", [P, 2, G]), sb("whole_t", [P, 2, G])
            self.turns_i = sb("turns_i", [P, 2, G], I32)
            self.skip = sb("skip", [P, G, CX])
        if pre is not None:
            self.tab = sb("tab", [P, n_tab, G, CX])
        else:
            self.final = sb("final", [P, G, CX])


def node_phase(nc, W, D, post, pre):
    PI = float(np.pi)
    norms = W["norm"][(pre or 0)] if pre in (0, 1) else None
    stages = []

    def stats(tag):
        stages.extend(tag + n for n in ("mean", "scale_mean", "centre", "square", "sum", "var", "root", "norm"))

    if post is not None:
        stages += ["pair", "sum"]
        if post in (0, 2):
            stages += ["denom", "recip", "ratio", "share"] if post == 0 else ["denom", "recip", "share"]
        if post == 0:
            stages += ["bias", "merged"]
        if post in (1, 3):
            stages += ["turn_s", "move_s", "turn_v", "move_v", "turn_x", "move_x", "product", "product_v"]
        else:
            stages += ["turn_a", "move_a", "product"]
        if post == 0:
            stages += ["residual"]
            stats("ln2_")
            stages += ["turn_n", "move_n", "f1", "attr", "scalars", "gate_t", "gate_v", "gated", "turn_f", "move_f", "f2", "f2_bias",
                       "f2_attr", "both", "whole"]
        if post == 1:
            stages += ["silu", "gate_t", "gate_half", "gated", "whole"]
        if post == 2:
            stages += ["twice", "whole"]
        if post == 3:
            stages += ["angle", "attr", "turns", "turns_i", "turns_f", "reduce", "shift", "shift_gt", "shift_in", "sine", "skip_attr",
                       "conv_attr", "mix_a", "mix_b", "mix_c", "whole"]
        stats("end_")
    if pre is not None:
        if pre in (0, 2):
            stats("pre_")
        stages += ["turn_p", "move_p", "tables", "move_t"]
        if pre == 3:
            stages += ["tab_attr"]
    L = len(stages)
    index = {n: k for k, n in enumerate(stages)}

    SECOND = G * P
    n_tab = {0: 2, 2: 2, 1: 1, 3: 1}[pre] if pre is not None else 1
    used = None if post is None else "turn_a" if post in (0, 2) else "move_v"
    H = ACC_W[post] - CX if post in (0, 2) else 1
    HS, HV = C0 // H, C1 // H

    with ExitStack() as ctx:
        S = Names(nc, ctx, f"n{post}{pre}".replace("None", "x"))
        sem = S.sem
        both = [Group(S, n, post, pre, n_tab, H) for n in range(2)]
        X = lambda B, j: W["x"][:, bass.ds((j * 2 + B.n) * G, G), :]
        NA = lambda B, j: W["na"][:, bass.ds((j * 2 + B.n) * G, G)]
        rows = lambda t, g: t.rearrange("(p t) c -> p t c", p=P)[:, bass.ds(g * G, G), :]
        block = ctx.enter_context(nc.Block())

        def at(eng, name, B, j):
            eng.wait_ge(B.done, 1 + j * L + index[name])

        @block.sync
        def _(sp):
            def load(B, j):
                for k in range(TM):
                    sp.dma_start(B.ag[k][:, :, :], rows(D["acc"][post][k][0:NPAD, :], j * 2 + B.n)).then_inc(B.loaded, 16)

            def store(B, j):
                if pre is not None:
                    for n, name in enumerate(("tab_src", "tab_dst")[0:n_tab]):
                        sp.dma_start(rows(D[name], j * 2 + B.n), B.tab[:, n, :, :]).then_inc(B.stored, 16)
                else:
                    sp.dma_start(rows(D["out"], j * 2 + B.n), B.final[:, :, :]).then_inc(B.stored, 16)

            for B in both:
                sp.sem_inc(B.done, 1)
                sp.sem_inc(B.stored, 16)
            if post is not None:
                for B in both:
                    load(B, 0)
            with sp.Fori(1, PAIRS) as j:
                if post is not None:
                    for B in both:
                        wait_apart(sp, B.done, 1 + (j - 1) * L + index[used], sem("sp_passed"))
                        load(B, j)
                for B in both:
                    wait_apart(sp, B.done, 1 + j * L, sem("sp_passed"))
                    store(B, j - 1)
            for B in both:
                sp.wait_ge(B.done, 1 + PAIRS * L)
                store(B, PAIRS - 1)
            for B in both:
                sp.wait_ge(B.stored, 16 * (1 + PAIRS * n_tab))

        @block.gpsimd
        def _(pool):
            with pool.Fori(0, PAIRS) as j:
                for tag in ("ln2_", "end_", "pre_"):
                    if tag + "root" in index:
                        for B in both:
                            at(pool, tag + "root", B, j)
                            nc.gpsimd.tensor_tensor(B.st[:, :, :], B.st[:, :, :], W["half"][:, 0:2 * G].rearrange("p (a t) -> p a t", a=2), ALU.pow)\
                                .then_inc(B.done, 1)
                if norms is not None:
                    share = norms[:, bass.ds(j * (ET // PAIRS), ET // PAIRS)]
                    nc.gpsimd.tensor_tensor(share, share, W["half"][:, 0:ET // PAIRS], ALU.pow).then_inc(sem("norms"), 1)

        @block.tensor
        def _(pe):
            ident = W["ident"]

            def turn(src, a, b, to, base=0):
                for t in range(G):
                    last = nc.tensor.transpose(to[0:b - a, base + P * t:base + P * t + P], src[:, t, a:b], ident[:, :])
                return last

            def times(to, a, *pairs):
                for t in range(G):
                    for n, (f, w) in enumerate(pairs):
                        last = nc.tensor.matmul(to[:, t, a:a + w.shape[1]], f[:, P * t:P * t + P], w, start=(n == 0), stop=(n == len(pairs) - 1),
                                                skip_group_check=True)
                return last

            def at(eng, name, B, j):
                wait_apart(eng, B.done, 1 + j * L + index[name], sem("pe_passed"))

            pe.wait_ge(sem("ones"), 2)
            with pe.Fori(0, PAIRS) as j:
                if post in (0, 2):
                    for B in both:
                        at(pe, "turn_a", B, j)
                        turn(B.nrm, 0, C0, B.psA)
                        turn(B.nrm, C0, CX, B.psA, SECOND).then_inc(B.done, 1)
                    for B in both:
                        at(pe, "product", B, j)
                        if post == 0:
                            times(B.wideB, 0, (B.sT[:, :], W["l0_proj_s"][:, :]))
                        else:
                            times(B.wideB, 0, (B.sT[0:64, :], W["l2_proj_s"][:, :]))
                        times(B.wideB, C0, (B.vT[:, :], W[f"l{post}_proj_v"][:, :])).then_inc(B.done, 1)
                if post == 0:
                    for B in both:
                        at(pe, "turn_n", B, j)
                        turn(B.nrm, 0, C0, B.psA)
                        turn(B.nrm, C0, CX, B.psA, SECOND).then_inc(B.done, 1)
                    for B in both:
                        at(pe, "f1", B, j)
                        times(B.wideB, 0, (B.sT[:, :], W["l0_f1_s"][:, :]))
                        times(B.wideA, 0, (B.vT[:, :], W["l0_f1_v"][:, :])).then_inc(B.done, 1)
                    for B in both:
                        at(pe, "turn_f", B, j)
                        turn(B.sc, 0, P, B.psA)
                        turn(B.fv, 0, P, B.psA, SECOND)
                        turn(B.fv, P, 192, B.psB).then_inc(B.done, 1)
                    for B in both:
                        at(pe, "f2", B, j)
                        times(B.wideB, 0, (B.scT[:, :], W["l0_f2_s"][:, :]))
                        times(B.wideB, C0, (B.fvTa[:, :], W["l0_f2_va"][:, :]), (B.fvTb[:, :], W["l0_f2_vb"][:, :])).then_inc(B.done, 1)
                if post in (1, 3):
                    per = 128 if post == 1 else 96
                    for B in both:
                        at(pe, "turn_s", B, j)
                        turn(B.ag[0], 0, 96, B.psA)
                        turn(B.ag[0], 96, 96 + per, B.psA, SECOND).then_inc(B.done, 1)
                    for B in both:
                        at(pe, "turn_v", B, j)
                        turn(B.ag[0], 96 + per, 96 + 2 * per, B.psA)
                        turn(B.ag[0], 96 + 2 * per, 96 + 3 * per, B.psA, SECOND).then_inc(B.done, 1)
                    for B in both:
                        at(pe, "turn_x", B, j)
                        for t in range(G):
                            nc.tensor.transpose(B.psA[0:64, P * t:P * t + P], B.res[:, t, 0:C0], ident[:, :])
                            last = nc.tensor.transpose(B.psA[0:96, SECOND + P * t:SECOND + P * t + P], B.res[:, t, C0:CX], ident[:, :])
                        last.then_inc(B.done, 1)
                    if post == 1:
                        for B in both:
                            at(pe, "product", B, j)
                            times(B.wideB, 0, (B.aT[:, :], W["l1_out_s"][:, :]), (B.sT[0:64, :], W["l1_skip_s"][:, :])).then_inc(B.done, 1)
                        for B in both:
                            at(pe, "product_v", B, j)
                            for t in range(G):
                                c = slice(P * t, P * t + P)
                                nc.tensor.matmul(B.wideA[:, t, 0:C1V], B.vT[:, c], W["l1_skip_v"][:, :], start=True, stop=False, skip_group_check=True)
                                for d in range(3):
                                    last = nc.tensor.matmul(B.wideA[:, t, C1 * d:C1 * d + C1], B.gT[d][:, c], W["l1_out_v"][:, :], start=False,
                                                            stop=True, skip_group_check=True)
                            last.then_inc(B.done, 1)
                    else:
                        for B in both:
                            at(pe, "product", B, j)
                            times(B.wideB, 0, (B.aT[:, :], W["l3_w2_s"][:, :]))
                            for d in range(3):
                                last = times(B.wideB, 65 + C1 * d, (B.gT[d][:, :], W["l3_w2_v"][:, :]))
                            last.then_inc(B.done, 1)
                        for B in both:
                            at(pe, "product_v", B, j)
                            times(B.wideA, 0, (B.sT[0:64, :], W["l3_sc_s"][:, :]))
                            times(B.wideA, C0, (B.vT[:, :], W["l3_sc_v"][:, :])).then_inc(B.done, 1)
                if pre is not None:
                    for B in both:
                        src = B.nrm if pre in (0, 2) else B.out
                        at(pe, "turn_p", B, j)
                        turn(src, 0, C0, B.psA)
                        turn(src, C0, CX, B.psA, SECOND).then_inc(B.done, 1)
                    for B in both:
                        at(pe, "tables", B, j)
                        times(B.wideB, 0, (B.sT[0:W[f"l{pre}_tab_s"].shape[0], :], W[f"l{pre}_tab_s"][:, :]))
                        times(B.wideA, 0, (B.vT[:, :], W[f"l{pre}_tab_v"][:, :])).then_inc(B.done, 1)

        @block.scalar
        def _(act):
            def move(to, src, n, scale=1.0, bias=0.0):
                if isinstance(scale, float) and isinstance(bias, float):
                    return nc.scalar.activation(to[0:n, :], src[0:n, 0:G * P], ACT.Copy)
                return nc.scalar.activation(to[0:n, :], src[0:n, 0:G * P], ACT.Identity, scale=scale, bias=bias)

            def square(tag, source, j):
                for B in both:
                    src = source(B)
                    at(act, tag + "square", B, j)
                    nc.scalar.activation(B.sqr[:, :, 0:C0], B.cen[:, :, 0:C0], ACT.Square)
                    nc.scalar.activation(B.sqr[:, :, C0:CX], src[:, :, C0:CX], ACT.Square).then_inc(B.done, 1)

            with act.Fori(0, PAIRS) as j:
                if post in (0, 2):
                    for B in both:
                        at(act, "move_a", B, j)
                        move(B.sT, B.psA, 64)
                        move(B.vT, B.second, 96).then_inc(B.done, 1)
                if post == 0:
                    square("ln2_", lambda B: B.res, j)
                    for B in both:
                        at(act, "move_n", B, j)
                        move(B.sT, B.psA, 64, W["l0_ln2_w0"][:, 0:1], W["l0_ln2_b0"][:, 0:1])
                        move(B.vT, B.second, 96, W["l0_ln2_w1"][:, 0:1]).then_inc(B.done, 1)
                    for B in both:
                        at(act, "scalars", B, j)
                        for t in range(G):
                            last = nc.scalar.activation(B.sc[:, t, :], B.wideB[:, t, 0:P], ACT.Silu, scale=B.attr[:, 0, t:t + 1])
                        last.then_inc(B.done, 1)
                    for B in both:
                        at(act, "gate_t", B, j)
                        for t in range(G):
                            last = nc.scalar.activation(B.th[:, t, :], B.wideB[:, t, P:192], ACT.Tanh, scale=B.attr[:, 1, t:t + 1])
                        last.then_inc(B.done, 1)
                    for B in both:
                        at(act, "gate_v", B, j)
                        for t in range(G):
                            last = nc.scalar.activation(B.fv[:, t, :], B.wideA[:, t, 0:192], ACT.Copy, scale=B.attr[:, 1, t:t + 1])
                        last.then_inc(B.done, 1)
                    for B in both:
                        at(act, "move_f", B, j)
                        move(B.scT, B.psA, P)
                        move(B.fvTa, B.second, P)
                        move(B.fvTb, B.psB, 64).then_inc(B.done, 1)
                if post in (1, 3):
                    per = 128 if post == 1 else 96
                    for B in both:
                        at(act, "move_s", B, j)
                        move(B.aT, B.psA, 96)
                        move(B.gT[0], B.second, per).then_inc(B.done, 1)
                    for B in both:
                        at(act, "move_v", B, j)
                        move(B.gT[1], B.psA, per)
                        move(B.gT[2], B.second, per).then_inc(B.done, 1)
                    for B in both:
                        at(act, "move_x", B, j)
                        move(B.sT, B.psA, 64)
                        move(B.vT, B.second, 96).then_inc(B.done, 1)
                if post == 1:
                    for B in both:
                        at(act, "silu", B, j)
                        nc.scalar.activation(B.out[:, :, 0:C0], B.wideB[:, :, 0:C0], ACT.Silu).then_inc(B.done, 1)
                    for B in both:
                        at(act, "gate_t", B, j)
                        nc.scalar.activation(B.th[:, :, :], B.wideB[:, :, C0:96], ACT.Tanh, scale=0.5).then_inc(B.done, 1)
                if post == 3:
                    for B in both:
                        at(act, "sine", B, j)
                        nc.scalar.activation(B.whole_t[:, :, :], B.ang[:, :, :], ACT.Sin).then_inc(B.done, 1)
                if post is not None:
                    for B in both:
                        at(act, "end_square", B, j)
                        nc.scalar.activation(B.sqr[:, :, :], B.cen[:, :, :], ACT.Square).then_inc(B.done, 1)
                if pre in (0, 2):
                    square("pre_", lambda B: B.out, j)
                if pre is not None:
                    for B in both:
                        at(act, "move_p", B, j)
                        if pre == 0:
                            move(B.sT, B.psA, 64, W["l0_ln1_w0"][:, 0:1], W["l0_ln1_b0"][:, 0:1])
                            last = move(B.vT, B.second, 96, W["l0_ln1_w1"][:, 0:1])
                        elif pre == 2:
                            move(B.sT, B.psA, 64, W["l2_gamma_s"][:, 0:1], W["l2_beta_s"][:, 0:1])
                            last = move(B.vT, B.second, 96, W["l2_gamma_v"][:, 0:1])
                        else:
                            move(B.sT, B.psA, 64)
                            last = move(B.vT, B.second, 96)
                        last.then_inc(B.done, 1)
                    for B in both:
                        at(act, "move_t", B, j)
                        act.wait_ge(B.stored, 16 + j * 16 * n_tab)
                        for n in range(n_tab):
                            nc.scalar.activation(B.tab[:, n, :, 0:C0], B.wideB[:, :, C0 * n:C0 * n + C0], ACT.Copy)
                            last = nc.scalar.activation(B.tab[:, n, :, C0:CX], B.wideA[:, :, C1V * n:C1V * n + C1V], ACT.Copy)
                        last.then_inc(B.done, 1)

        @block.vector
        def _(dve):
            tt, ts, stt = nc.vector.tensor_tensor, nc.vector.tensor_scalar, nc.vector.scalar_tensor_tensor

            def by_head(t, a, c):
                return t[:, :, a:a + c * H].rearrange("p t (h c) -> p t h c", h=H)

            def reduce(to, src):
                return nc.vector.tensor_reduce(to, src, AX.X, ALU.add)

            def stats_eq(tag, source, j, dv, eps):
                scalars, vectors = lambda B: source(B)[:, :, 0:C0], lambda B: source(B)[:, :, C0:CX]
                for B in both:
                    at(dve, tag + "mean", B, j)
                    reduce(B.st[:, 0, :], scalars(B)).then_inc(B.done, 1)
                for B in both:
                    at(dve, tag + "scale_mean", B, j)
                    ts(B.st[:, 0, :], B.st[:, 0, :], -1.0 / C0, None, ALU.mult).then_inc(B.done, 1)
                for B in both:
                    at(dve, tag + "centre", B, j)
                    tt(B.cen[:, :, 0:C0], scalars(B), bcast(B.st[:, 0, :], 2, C0), ALU.add).then_inc(B.done, 1)
                for B in both:
                    at(dve, tag + "sum", B, j)
                    reduce(B.st[:, 0, :], B.sqr[:, :, 0:C0])
                    reduce(B.st[:, 1, :], B.sqr[:, :, C0:CX]).then_inc(B.done, 1)
                for B in both:
                    at(dve, tag + "var", B, j)
                    ts(B.st[:, 0, :], B.st[:, 0, :], 1.0 / C0, eps, ALU.mult, ALU.add)
                    ts(B.st[:, 1, :], B.st[:, 1, :], 1.0 / dv, eps, ALU.mult, ALU.add).then_inc(B.done, 1)
                for B in both:
                    at(dve, tag + "norm", B, j)
                    tt(B.nrm[:, :, 0:C0], B.cen[:, :, 0:C0], bcast(B.st[:, 0, :], 2, C0), ALU.mult)
                    tt(B.nrm[:, :, C0:CX], vectors(B), bcast(B.st[:, 1, :], 2, C1V), ALU.mult).then_inc(B.done, 1)

            for B in both:
                nc.vector.memset(B.sT[64:65, :], 1.0).then_inc(sem("ones"), 1)
            with dve.Fori(0, PAIRS) as j:
                if post is not None:
                    for B in both:
                        at(dve, "pair", B, j)
                        dve.wait_ge(B.loaded, (j + 1) * 16 * TM)
                        tt(B.ag[0][:, :, :], B.ag[0][:, :, :], B.ag[1][:, :, :], ALU.add)
                        tt(B.ag[2][:, :, :], B.ag[2][:, :, :], B.ag[3][:, :, :], ALU.add)
                        nc.vector.tensor_copy(B.res[:, :, :], X(B, j)).then_inc(B.done, 1)
                    for B in both:
                        at(dve, "sum", B, j)
                        tt(B.ag[0][:, :, :], B.ag[0][:, :, :], B.ag[2][:, :, :], ALU.add).then_inc(B.done, 1)
                if post in (0, 2):
                    total = lambda B: B.ag[0][:, :, CX:CX + H]
                    for B in both:
                        at(dve, "denom", B, j)
                        ts(B.den[:, :, :], total(B), 1e-12 if post == 0 else 1e-16, None, ALU.add).then_inc(B.done, 1)
                    for B in both:
                        at(dve, "recip", B, j)
                        nc.vector.reciprocal(B.den[:, :, :], B.den[:, :, :]).then_inc(B.done, 1)
                    if post == 0:
                        for B in both:
                            at(dve, "ratio", B, j)
                            tt(B.ratio[:, :, :], total(B), B.den[:, :, :], ALU.mult).then_inc(B.done, 1)
                    for B in both:
                        at(dve, "share", B, j)
                        tt(by_head(B.nrm, 0, HS), by_head(B.ag[0], 0, HS), bcast(B.den[:, :, :], 3, HS), ALU.mult)
                        for d in range(3):
                            last = tt(by_head(B.nrm, C0 + C1 * d, HV), by_head(B.ag[0], C0 + C1 * d, HV), bcast(B.den[:, :, :], 3, HV), ALU.mult)
                        last.then_inc(B.done, 1)
                if post == 0:
                    for B in both:
                        at(dve, "bias", B, j)
                        tt(by_head(B.cen, 0, HS), bcast(W["l0_bias"][:, 64:128], 1, G).rearrange("p t (h c) -> p t h c", h=H),
                           bcast(B.ratio[:, :, :], 3, HS), ALU.mult).then_inc(B.done, 1)
                    for B in both:
                        at(dve, "merged", B, j)
                        tt(B.nrm[:, :, 0:C0], B.nrm[:, :, 0:C0], B.cen[:, :, 0:C0], ALU.add).then_inc(B.done, 1)
                if post == 0:
                    for B in both:
                        at(dve, "residual", B, j)
                        tt(B.res[:, :, :], X(B, j), B.wideB[:, :, 0:CX], ALU.add).then_inc(B.done, 1)
                    stats_eq("ln2_", lambda B: B.res, j, C1V, 1e-5)
                    for B in both:
                        at(dve, "attr", B, j)
                        nc.vector.tensor_copy(B.attr[:, 0, :], NA(B, j))
                        ts(B.attr[:, 1, :], NA(B, j), 0.5, None, ALU.mult).then_inc(B.done, 1)
                    for B in both:
                        at(dve, "gated", B, j)
                        for d in range(3):
                            v = B.fv[:, :, 64 * d:64 * d + 64]
                            last = stt(out=v, in0=B.th[:, :, :], scalar=1.0, in1=v, op0=ALU.add, op1=ALU.mult)
                        last.then_inc(B.done, 1)
                    for B in both:
                        at(dve, "f2_bias", B, j)
                        tt(B.out[:, :, 0:C0], B.wideB[:, :, 0:C0], bcast(W["l0_f2_b"][:, :], 1, G), ALU.add)
                        nc.vector.tensor_copy(B.out[:, :, C0:CX], B.wideB[:, :, C0:CX]).then_inc(B.done, 1)
                    for B in both:
                        at(dve, "f2_attr", B, j)
                        tt(B.out[:, :, :], B.out[:, :, :], bcast(B.attr[:, 0, :], 2, CX), ALU.mult).then_inc(B.done, 1)
                    for B in both:
                        at(dve, "both", B, j)
                        tt(B.out[:, :, :], B.out[:, :, :], B.res[:, :, :], ALU.add).then_inc(B.done, 1)
                    for B in both:
                        at(dve, "whole", B, j)
                        tt(B.res[:, :, :], B.out[:, :, :], X(B, j), ALU.add).then_inc(B.done, 1)
                if post == 1:
                    for B in both:
                        at(dve, "gate_half", B, j)
                        ts(B.th[:, :, :], B.th[:, :, :], 0.5, 0.5, ALU.mult, ALU.add).then_inc(B.done, 1)
                    for B in both:
                        at(dve, "gated", B, j)
                        tt(comp(B.out[:, :, C0:CX]), comp(B.wideA[:, :, 0:C1V]), bcast(B.th[:, :, :], 2, 3), ALU.mult).then_inc(B.done, 1)
                    for B in both:
                        at(dve, "whole", B, j)
                        tt(B.res[:, :, :], B.res[:, :, :], B.out[:, :, :], ALU.add).then_inc(B.done, 1)
                if post == 2:
                    for B in both:
                        at(dve, "twice", B, j)
                        tt(B.out[:, :, :], B.res[:, :, :], B.wideB[:, :, 0:CX], ALU.add).then_inc(B.done, 1)
                    for B in both:
                        at(dve, "whole", B, j)
                        tt(B.res[:, :, :], B.res[:, :, :], B.out[:, :, :], ALU.add).then_inc(B.done, 1)
                if post == 3:
                    for B in both:
                        at(dve, "angle", B, j)
                        tt(B.ang[:, 0, :], B.wideB[:, :, 64:65].rearrange("p t c -> p (t c)"), NA(B, j), ALU.mult)
                        nc.vector.tensor_copy(B.attr[:, 0, :], NA(B, j)).then_inc(B.done, 1)
                    for B in both:
                        at(dve, "attr", B, j)
                        nc.vector.tensor_copy(B.attr[:, 1, :], B.attr[:, 0, :]).then_inc(B.done, 1)
                    for B in both:
                        at(dve, "turns", B, j)
                        ts(B.whole_t[:, 0, :], B.ang[:, 0, :], 1.0 / (2 * PI), None, ALU.mult).then_inc(B.done, 1)
                    for B in both:
                        at(dve, "turns_i", B, j)
                        nc.vector.tensor_copy(B.turns_i[:, 0, :], B.whole_t[:, 0, :]).then_inc(B.done, 1)
                    for B in both:
                        at(dve, "turns_f", B, j)
                        nc.vector.tensor_copy(B.whole_t[:, 0, :], B.turns_i[:, 0, :]).then_inc(B.done, 1)
                    for B in both:
                        at(dve, "reduce", B, j)
                        c1 = 6.28125
                        c2 = float(np.float32(2 * np.pi - c1) - np.float32(2 * np.pi - c1) % np.float32(2.0 ** -21))
                        c3 = 2 * np.pi - c1 - c2
                        for n, c in enumerate((c1, c2, c3)):
                            ins = stt(out=B.ang[:, 0, :], in0=B.whole_t[:, 0, :], scalar=-c, in1=B.ang[:, 0, :], op0=ALU.mult, op1=ALU.add)
                            if n < 2:
                                ins.then_inc(B.part, 1)
                                dve.wait_ge(B.part, j * 2 + n + 1)
                        ins.then_inc(B.done, 1)
                    for B in both:
                        at(dve, "shift", B, j)
                        ts(B.ang[:, 1, :], B.ang[:, 0, :], PI / 2, None, ALU.add).then_inc(B.done, 1)
                    for B in both:
                        at(dve, "shift_gt", B, j)
                        ts(B.whole_t[:, :, :], B.ang[:, :, :], PI, -2 * PI, ALU.is_gt, ALU.mult).then_inc(B.done, 1)
                    for B in both:
                        at(dve, "shift_in", B, j)
                        tt(B.ang[:, :, :], B.ang[:, :, :], B.whole_t[:, :, :], ALU.add).then_inc(B.low, 1)
                        dve.wait_ge(B.low, 4 * j + 1)
                        ts(B.whole_t[:, :, :], B.ang[:, :, :], -PI, 2 * PI, ALU.is_lt, ALU.mult).then_inc(B.low, 1)
                        dve.wait_ge(B.low, 4 * j + 2)
                        tt(B.ang[:, :, :], B.ang[:, :, :], B.whole_t[:, :, :], ALU.add).then_inc(B.low, 1)
                        dve.wait_ge(B.low, 4 * j + 3)
                        ts(B.ang[:, :, :], B.ang[:, :, :], float(np.nextafter(np.float32(PI), np.float32(0))), -float(np.nextafter(np.float32(PI), np.float32(0))),
                           ALU.min, ALU.max).then_inc(B.low, 1)
                        dve.wait_ge(B.low, 4 * j + 4)
                        dve.sem_inc(B.done, 1)
                    for B in both:
                        at(dve, "skip_attr", B, j)
                        tt(B.whole_t[:, :, :], B.whole_t[:, :, :], B.attr[:, :, :], ALU.mult).then_inc(B.done, 1)
                    for B in both:
                        at(dve, "conv_attr", B, j)
                        tt(B.out[:, :, 0:C0], B.wideB[:, :, 0:C0], bcast(B.whole_t[:, 0, :], 2, C0), ALU.mult)
                        tt(B.out[:, :, C0:CX], B.wideB[:, :, 65:161], bcast(B.whole_t[:, 0, :], 2, C1V), ALU.mult).then_inc(B.done, 1)
                    for B in both:
                        at(dve, "mix_a", B, j)
                        tt(B.skip[:, :, :], B.wideA[:, :, 0:CX], bcast(B.whole_t[:, 1, :], 2, CX), ALU.mult).then_inc(B.done, 1)
                    for B in both:
                        at(dve, "mix_b", B, j)
                        tt(B.out[:, :, :], B.out[:, :, :], B.skip[:, :, :], ALU.add).then_inc(B.done, 1)
                    for B in both:
                        at(dve, "mix_c", B, j)
                        tt(B.res[:, :, :], B.res[:, :, :], B.out[:, :, :], ALU.add).then_inc(B.done, 1)
                    for B in both:
                        at(dve, "whole", B, j)
                        dve.sem_inc(B.done, 1)
                if post is not None:
                    for B in both:
                        at(dve, "end_mean", B, j)
                        reduce(B.st[:, 0, :], B.res[:, :, :]).then_inc(B.done, 1)
                    for B in both:
                        at(dve, "end_scale_mean", B, j)
                        ts(B.st[:, 0, :], B.st[:, 0, :], -1.0 / CX, None, ALU.mult).then_inc(B.done, 1)
                    for B in both:
                        at(dve, "end_centre", B, j)
                        tt(B.cen[:, :, :], B.res[:, :, :], bcast(B.st[:, 0, :], 2, CX), ALU.add).then_inc(B.done, 1)
                    for B in both:
                        at(dve, "end_sum", B, j)
                        reduce(B.st[:, 0, :], B.sqr[:, :, :])
                        nc.vector.memset(B.st[:, 1, :], 1.0).then_inc(B.done, 1)
                    for B in both:
                        at(dve, "end_var", B, j)
                        ts(B.st[:, 0, :], B.st[:, 0, :], 1.0 / CX, 1e-5, ALU.mult, ALU.add).then_inc(B.done, 1)
                    for B in both:
                        at(dve, "end_norm", B, j)
                        if pre is None:
                            dve.wait_ge(B.stored, 16 + j * 16)
                            tt(B.final[:, :, :], B.cen[:, :, :], bcast(B.st[:, 0, :], 2, CX), ALU.mult).then_inc(B.done, 1)
                        else:
                            tt(B.out[:, :, :], B.cen[:, :, :], bcast(B.st[:, 0, :], 2, CX), ALU.mult)
                            tt(X(B, j), B.cen[:, :, :], bcast(B.st[:, 0, :], 2, CX), ALU.mult).then_inc(B.done, 1)
                if pre in (0, 2):
                    if post is None:
                        for B in both:
                            at(dve, "pre_mean", B, j)
                            nc.vector.tensor_copy(B.out[:, :, :], X(B, j)).then_inc(B.copied, 1)
                            dve.wait_ge(B.copied, j + 1)
                    stats_eq("pre_", lambda B: B.out, j, C1V if pre == 0 else C1, 1e-5)
                if pre == 3:
                    for B in both:
                        at(dve, "tab_attr", B, j)
                        tt(B.tab[:, 0, :, :], B.tab[:, 0, :, :], bcast(NA(B, j), 2, CX), ALU.mult).then_inc(B.done, 1)



def graph_network(nc, D):
    with ExitStack() as ctx:
        W = setup(nc, ctx, D)
        node_phase(nc, W, D, None, 0)
        for layer, H, edges in ((0, 8, layer0_edges), (2, 4, layer2_edges)):
            with ExitStack() as inner:
                logits = inner.enter_context(nc.sbuf_tensor(f"logits{layer}", [P, ET, H], F32))
                edges(nc, W, D, logits)
                probs = inner.enter_context(nc.sbuf_tensor(f"probs{layer}", [P, ET, H], F32))
                sorted_maxima(nc, W, D, logits, probs, H, f"m{layer}")
                unsorted_maxima(nc, W, D, logits, probs, H, f"u{layer}")
                softmax_weights(nc, W, logits, probs, H, f"p{layer}")
                attention_sums(nc, W, D, probs, layer, H, f"s{layer}")
            node_phase(nc, W, D, layer, layer + 1)
            by = ("dst", "src") if layer == 0 else ("src", "dst")
            convolution_edges(nc, W, D, layer + 1, *by, f"e{layer + 1}")
            node_phase(nc, W, D, layer + 1, layer + 2 if layer == 0 else None)


_WEIGHTS = (
    [f"L0_gnn_{k}" for k in (
        "ln1_w0 ln1_b0 ln1_w1 ln2_w0 ln2_b0 ln2_w1 msrc_ws msrc_wv mdst_ws mdst_bs mdst_wv rw1 rb1 rg1 rbe1 rw2 rb2 rg2 rbe2 rw3 roff "
        "lin_ws lin_bs lin_wv alpha_dot proj_ws proj_bs proj_wv f1_ws f1_bs f1_wv f2_ws f2_bs f2_wv").split()]
    + [f"L1_gnn_{k}" for k in "W_skip0 W_skip1 W_nl0 W_nl1 W_fc1 W_fc2 W_out_s W_out_v".split()]
    + [f"L2_gnn_{k}" for k in (
        "gamma_s beta_s gamma_v Ws_src Wv_src Ws_dst Wv_dst W_rbf W_alpha alpha_dot Ws_val Wv_val Wg w2_ss w2_sv w2_vs w2_vv0 w2_vv1 "
        "Ws_vlin Wv_vlin Wps Wpv").split()]
    + [f"L3_gnn_{k}" for k in "W_sc_s W_sc_v W1_s W1_v W2_s W2_v W3 fcW1 fcW2".split()]
)


def _padded(a, rows, fill):
    a = np.asarray(a)
    return np.concatenate([a, np.full((rows - a.shape[0],) + a.shape[1:], fill, a.dtype)], axis=0)


def _turned(a):
    return np.ascontiguousarray(a.reshape(P, ET, -1).transpose(2, 1, 0).reshape(a.shape[1], EPAD))


def kernel(**inputs):
    import concourse.bacc as _bacc
    from concourse.bass_utils import run_bass_kernel_spmd as _run

    x = np.asarray(inputs["x"])
    by_component = x[:, C0:].reshape(-1, C1, 3).transpose(0, 2, 1).reshape(-1, C1V)
    arrays = {"x": _padded(np.concatenate([x[:, :C0], by_component], axis=1), NPAD, 0.0)}
    for k in ("src", "dst"):
        e = _padded(inputs[k], EPAD, NPAD - 1).reshape(P, ET)
        arrays[k], arrays[k + "_t"] = e, np.ascontiguousarray(e.T)
    for k in (3, 4):
        arrays[f"edge_attr_{k}"] = _padded(inputs[f"edge_attr_{k}"], EPAD, 1.0).reshape(P, ET * k)
    for k in (8, 16, 64):
        arrays[f"es{k}"] = _turned(_padded(inputs[f"edge_attr_{k}"], EPAD, 1.0))
    arrays["es64"] = np.concatenate([arrays["es64"], np.ones((1, EPAD), np.float32)], axis=0)
    arrays["node_vec1"] = _padded(inputs["node_vec1"], NPAD, 1.0).reshape(P, NT)
    for k in _WEIGHTS:
        arrays[k] = np.asarray(inputs[k])

    nc = _bacc.Bacc("TRN2", target_bir_lowering=False, num_devices=1)
    D = {}
    for k, a in arrays.items():
        D[k] = nc.dram_tensor("in_" + k, a.shape, mybir.dt.from_np(a.dtype), kind="ExternalInput").ap()
    for k in ("tab_src", "tab_dst"):
        D[k] = nc.dram_tensor(k, (NPAD, CX), F32, kind="Internal").ap()
    D["val"] = nc.dram_tensor("val", (P, ET, CX), F32, kind="Internal").ap()
    D["acc"] = [[nc.dram_tensor(f"acc{n}{k}", (ROWS, w), F32, kind="Internal").ap() for k in range(TM)] for n, w in enumerate(ACC_W)]
    D["max"] = {H: [nc.dram_tensor(f"max{H}_{k}", (ROWS, H), F32, kind="Internal").ap() for k in range(TM)] for H in (8, 4)}
    D["out"] = nc.dram_tensor("out", (NPAD, CX), F32, kind="ExternalOutput").ap()
    graph_network(nc, D)
    r = _run(nc, [{"in_" + k: a for k, a in arrays.items()}], core_ids=[0])
    y = np.asarray(r.results[0]["out"])[:N_NODES]
    v = y[:, C0:].reshape(-1, 3, C1).transpose(0, 2, 1).reshape(-1, C1V)
    return np.ascontiguousarray(np.concatenate([y[:, :C0], v], axis=1))
```
